# Optimizing a Trainium2 kernel written in Bass

```python
import numpy as np
import jax
import jax.numpy as jnp

def _softmax(x, axis=-1):
    return jax.nn.softmax(x, axis=axis)

def _gelu(x):
    return jax.nn.gelu(x, approximate=True)

def _silu(x):
    return jax.nn.silu(x)

def _sigmoid(x):
    return jax.nn.sigmoid(x)

def _layernorm(x, axis=-1, eps=1e-05):
    m = jnp.mean(x, axis=axis, keepdims=True)
    v = jnp.var(x, axis=axis, keepdims=True)
    return (x - m) / jnp.sqrt(v + eps)

def _scatter_add(tgt, idx, src, axis=0):
    return tgt.at[idx].add(src)

def _segment_sum(src, seg, n):
    return jax.ops.segment_sum(src, seg, n)
kernel_name = 'mk_gnn_resnorm_d2_gnn_r32_a782fe'

def setup_inputs(seed: int=0):
    np.random.seed(seed)
    _w = jnp.asarray

    def _rec_inputs():
        import jax
        import jax.numpy as jnp
        _gk = jax.random.key(seed)
        x = -0.0008691 + 1 * jax.random.normal(jax.random.fold_in(_gk, 1), (50000, 128), jnp.float32)
        src = jax.random.randint(jax.random.fold_in(_gk, 2), (25000,), 0, 50000, jnp.int32)
        dst = jax.random.randint(jax.random.fold_in(_gk, 3), (25000,), 0, 50000, jnp.int32)
        _o = jnp.argsort(dst, stable=True)
        src = src[_o]
        dst = dst[_o]
        edge_attr_96 = 5.93493e-05 + 1.00006 * jax.random.normal(jax.random.fold_in(_gk, 12), (25000, 96), jnp.float32)
        return (x, src, dst, edge_attr_96)
    x, src, dst, edge_attr_96 = _rec_inputs()

    def _L0_gnn_setup():
        import jax, jax.numpy as jnp
        import numpy as np
        N, D, H = (10000, 128, 128)
        E = 20000
        EPS = 1e-05

        def _layer_norm(x, g, b):
            mu = jnp.mean(x, axis=-1, keepdims=True)
            var = jnp.mean((x - mu) ** 2, axis=-1, keepdims=True)
            return (x - mu) * jax.lax.rsqrt(var + EPS) * g + b

        def _scatter_mean(x_t, src, dst, n):
            msgs = x_t[src]
            agg = jax.ops.segment_sum(msgs, dst, num_segments=n)
            deg = jax.ops.segment_sum(jnp.ones_like(dst, dtype=x_t.dtype), dst, num_segments=n)
            return agg / jnp.clip(deg, 1.0)[:, None]
        key = jax.random.key(seed)
        ks = jax.random.split(key, 8)
        x = jax.random.normal(ks[0], (N, D), dtype=jnp.float32)
        edge_index = jax.random.randint(ks[1], (2, E), 0, N, dtype=jnp.int64)
        s = 1.0 / np.sqrt(H)
        W1 = jax.random.uniform(ks[2], (D, H), jnp.float32, -s, s)
        b1 = jnp.zeros((H,), jnp.float32)
        g1 = jnp.ones((H,), jnp.float32)
        be1 = jnp.zeros((H,), jnp.float32)
        W2 = jax.random.uniform(ks[3], (H, H), jnp.float32, -s, s)
        b2 = jnp.zeros((H,), jnp.float32)
        g2 = jnp.ones((H,), jnp.float32)
        be2 = jnp.zeros((H,), jnp.float32)
        Wo = jax.random.uniform(ks[4], (H, D), jnp.float32, -s, s)
        bo = jnp.zeros((D,), jnp.float32)
        return dict(subgraph_embeddings=x, edge_index=edge_index, W1=W1, b1=b1, g1=g1, be1=be1, W2=W2, b2=b2, g2=g2, be2=be2, Wo=Wo, bo=bo)
    _L0_gnn_all = _L0_gnn_setup()
    _L0_gnn_in = {k: v for k, v in _L0_gnn_all.items() if k in ('W1', 'b1', 'g1', 'be1', 'W2', 'b2', 'g2', 'be2', 'Wo', 'bo')}
    del _L0_gnn_all

    def _L1_gnn_setup():
        import jax, jax.numpy as jnp
        import numpy as np
        N_NODES = 50000
        N_EDGES = 25000
        D_NODE_IN, D_EDGE, D_GRAPH = (128, 96, 64)
        HIDDEN, D_NODE_OUT = (256, 128)
        NUM_GRAPHS = 64
        BN_EPS = 1e-05
        key = jax.random.key(seed)
        ks = jax.random.split(key, 10)
        d_in = D_NODE_IN + D_EDGE + D_GRAPH
        return {'x': jax.random.normal(ks[0], (N_NODES, D_NODE_IN), jnp.float32), 'edge_index': jax.random.randint(ks[1], (2, N_EDGES), 0, N_NODES, jnp.int64), 'edge_attr': jax.random.normal(ks[2], (N_EDGES, D_EDGE), jnp.float32), 'u': jax.random.normal(ks[3], (NUM_GRAPHS, D_GRAPH), jnp.float32), 'batch': jnp.sort(jax.random.randint(ks[4], (N_NODES,), 0, NUM_GRAPHS, jnp.int64)), 'W1': jax.random.normal(ks[5], (d_in, HIDDEN), jnp.float32) / np.sqrt(d_in), 'b1': jnp.zeros((HIDDEN,), jnp.float32), 'gamma': jnp.ones((HIDDEN,), jnp.float32), 'beta': jnp.zeros((HIDDEN,), jnp.float32), 'W2': jax.random.normal(ks[6], (HIDDEN, D_NODE_OUT), jnp.float32) / np.sqrt(HIDDEN), 'b2': jnp.zeros((D_NODE_OUT,), jnp.float32)}
    _L1_gnn_all = _L1_gnn_setup()
    _L1_gnn_in = {k: v for k, v in _L1_gnn_all.items() if k in ('u', 'W1', 'b1', 'gamma', 'beta', 'W2', 'b2')}
    del _L1_gnn_all
    return {'x': x, 'src': src, 'dst': dst, 'edge_attr_96': edge_attr_96, 'L0_gnn_W1': _L0_gnn_in['W1'], 'L0_gnn_b1': _L0_gnn_in['b1'], 'L0_gnn_g1': _L0_gnn_in['g1'], 'L0_gnn_be1': _L0_gnn_in['be1'], 'L0_gnn_W2': _L0_gnn_in['W2'], 'L0_gnn_b2': _L0_gnn_in['b2'], 'L0_gnn_g2': _L0_gnn_in['g2'], 'L0_gnn_be2': _L0_gnn_in['be2'], 'L0_gnn_Wo': _L0_gnn_in['Wo'], 'L0_gnn_bo': _L0_gnn_in['bo'], 'L1_gnn_u': _L1_gnn_in['u'], 'L1_gnn_W1': _L1_gnn_in['W1'], 'L1_gnn_b1': _L1_gnn_in['b1'], 'L1_gnn_gamma': _L1_gnn_in['gamma'], 'L1_gnn_beta': _L1_gnn_in['beta'], 'L1_gnn_W2': _L1_gnn_in['W2'], 'L1_gnn_b2': _L1_gnn_in['b2']}

def reference(x, src, dst, edge_attr_96, L0_gnn_W1, L0_gnn_b1, L0_gnn_g1, L0_gnn_be1, L0_gnn_W2, L0_gnn_b2, L0_gnn_g2, L0_gnn_be2, L0_gnn_Wo, L0_gnn_bo, L1_gnn_u, L1_gnn_W1, L1_gnn_b1, L1_gnn_gamma, L1_gnn_beta, L1_gnn_W2, L1_gnn_b2):
    import jax
    import jax.numpy as jnp

    def _L0_gnn_ref(subgraph_embeddings, edge_index, W1, b1, g1, be1, W2, b2, g2, be2, Wo, bo):
        import jax, jax.numpy as jnp
        import numpy as np
        N, D, H = (10000, 128, 128)
        E = 20000
        EPS = 1e-05

        def _layer_norm(x, g, b):
            mu = jnp.mean(x, axis=-1, keepdims=True)
            var = jnp.mean((x - mu) ** 2, axis=-1, keepdims=True)
            return (x - mu) * jax.lax.rsqrt(var + EPS) * g + b

        def _scatter_mean(x_t, src, dst, n):
            msgs = x_t[src]
            agg = jax.ops.segment_sum(msgs, dst, num_segments=n)
            deg = jax.ops.segment_sum(jnp.ones_like(dst, dtype=x_t.dtype), dst, num_segments=n)
            return agg / jnp.clip(deg, 1.0)[:, None]
        x0 = subgraph_embeddings
        n = x0.shape[0]
        src, dst = (edge_index[0], edge_index[1])
        x_t = x0 @ W1 + b1
        x_t = _scatter_mean(x_t, src, dst, n)
        x = jax.nn.relu(_layer_norm(x_t, g1, be1))
        x_t = x @ W2 + b2
        x_t = _scatter_mean(x_t, src, dst, n)
        x = jax.nn.relu(_layer_norm(x + x_t, g2, be2))
        return x @ Wo + bo + x0

    def _L1_gnn_ref(x, edge_index, edge_attr, u, batch, W1, b1, gamma, beta, W2, b2):
        import jax, jax.numpy as jnp
        import numpy as np
        N_NODES = 50000
        N_EDGES = 25000
        D_NODE_IN, D_EDGE, D_GRAPH = (128, 96, 64)
        HIDDEN, D_NODE_OUT = (256, 128)
        NUM_GRAPHS = 64
        BN_EPS = 1e-05
        col = edge_index[1]
        n = x.shape[0]
        sums = jax.ops.segment_sum(edge_attr, col, num_segments=n)
        cnt = jax.ops.segment_sum(jnp.ones((edge_attr.shape[0], 1), edge_attr.dtype), col, num_segments=n)
        e_aggr = sums / jnp.maximum(cnt, 1.0)
        h = jnp.concatenate([x, e_aggr, u[batch]], axis=1)
        h = h @ W1 + b1
        mu = jnp.mean(h, axis=0)
        var = jnp.mean((h - mu) ** 2, axis=0)
        h = (h - mu) * jax.lax.rsqrt(var + BN_EPS) * gamma + beta
        h = jax.nn.relu(h)
        return h @ W2 + b2
    edge_index = jnp.stack([src, dst])
    batch0 = jnp.zeros((50000,), jnp.int32)
    x = _layernorm(x + _L0_gnn_ref(x, edge_index, L0_gnn_W1, L0_gnn_b1, L0_gnn_g1, L0_gnn_be1, L0_gnn_W2, L0_gnn_b2, L0_gnn_g2, L0_gnn_be2, L0_gnn_Wo, L0_gnn_bo), axis=-1)
    x = _layernorm(x + _L1_gnn_ref(x, edge_index, edge_attr_96, L1_gnn_u, batch0, L1_gnn_W1, L1_gnn_b1, L1_gnn_gamma, L1_gnn_beta, L1_gnn_W2, L1_gnn_b2), axis=-1)
    return x

_drawn_inputs = setup_inputs


def setup_inputs(seed=0):
    import zlib

    import numpy as np

    out = dict(_drawn_inputs(seed))
    spreads = {'L0_gnn_b1': (0.0, 0.277),
     'L0_gnn_g1': (1.0, 0.574),
     'L0_gnn_be1': (0.0, 0.1),
     'L0_gnn_b2': (0.0, 0.581),
     'L0_gnn_g2': (1.0, 0.2),
     'L0_gnn_be2': (0.0, 0.559),
     'L0_gnn_bo': (0.0, 0.1),
     'L1_gnn_b1': (0.0, 2.0),
     'L1_gnn_gamma': (1.0, 0.2),
     'L1_gnn_beta': (0.0, 0.1),
     'L1_gnn_b2': (0.0, 0.1)}
    factors = {'L1_gnn_u': 64.0}
    for name, (base, spread) in spreads.items():
        noise = np.random.default_rng([zlib.crc32(name.encode()), seed]).standard_normal(out[name].shape)
        drawn = base * np.exp(spread * noise) if base else spread * noise
        out[name] = jnp.asarray(drawn.astype(out[name].dtype))
    for name, factor in factors.items():
        out[name] = (out[name] * factor).astype(out[name].dtype)
    return out
```

```python
import concourse.bass as bass
from concourse import mybir
from contextlib import ExitStack


def wait(eng, sem, value):
    if isinstance(value, int) and value <= 0:
        return
    eng.wait_ge(sem, value)


def build_gnn(nc, x, src, dst, ea, W1, b1, g1, be1, W2, b2, g2, be2, Wo, bo,
              u, V1, c1, gamma, beta, V2, c2, out):
    f32, i32 = mybir.dt.float32, mybir.dt.int32
    ALU = mybir.AluOpType
    ACT = mybir.ActivationFunctionType

    P = 128
    N, D = x.shape
    E, DE = ea.shape
    H = V1.shape[1]
    DU = u.shape[1]
    EPS = 1e-5

    TH = 4
    TS = 2 * TH
    STEPS = -(-E // (P * TS))
    TILES = STEPS * TS
    EP = TILES * P
    HALF = TH * P
    STEP = TS * P
    TQ = TILES // 2
    SKIP = 60000
    FILL_R = 23
    FILL_A = 17
    NT = P * FILL_R * FILL_A
    assert NT >= N and N + SKIP > N - 1 and EP >= E
    YW = D + DE

    BR = 5
    BLK = P * BR
    BLOCKS = N // BLK
    REST = N - BLOCKS * BLK
    assert BLOCKS % 2 == 0 and 0 < REST <= P

    src_s = nc.dram_tensor("src_sorted", [EP], i32).ap()
    dst_s = nc.dram_tensor("dst_sorted", [EP + 2], i32).ap()
    ea_s = nc.dram_tensor("edge_attr_sorted", [EP, DE], f32).ap()
    x1_tab = nc.dram_tensor("x1_by_node", [NT, D], f32).ap()
    x1_slot = nc.dram_tensor("x1_by_slot", [STEPS * 2, P, TH * D], f32).ap()
    ye_tab = nc.dram_tensor("y_e_by_node", [NT, YW], f32).ap()

    ctx = ExitStack()
    with ctx:
        def sb(name, shape, dt=f32):
            return ctx.enter_context(nc.sbuf_tensor(name, shape, dt))

        def sem(name):
            return ctx.enter_context(nc.semaphore(name))

        ident = sb("ident", [P, P])
        ones = sb("ones", [P, 1])
        w1 = sb("w1", [P, D])
        w2 = sb("w2", [P, D])
        wo = sb("wo", [P, D])
        b1_row = sb("b1_row", [1, D])
        g1_bc = sb("g1_bc", [P, D])
        be1_bc = sb("be1_bc", [P, D])
        b2_bc = sb("b2_bc", [P, D])
        bo_bc = sb("bo_bc", [P, D])
        c2_bc = sb("c2_bc", [P, D])
        g2_col = sb("g2_col", [P, 1])
        be2_col = sb("be2_col", [P, 1])
        vx = sb("vx", [P, H])
        ve = sb("ve", [DE, H])
        vu = sb("vu", [DU, H])
        v2 = sb("v2", [P, 2, D])
        u_col = sb("u_col", [DU, 1])
        c1_col = sb("c1_col", [P, 2])
        gamma_col = sb("gamma_col", [P, 2])
        beta_col = sb("beta_col", [P, 2])
        src_idx = sb("src_idx", [P, TILES], i32)
        put_idx = sb("put_idx", [P, TILES], i32)
        dst_col = sb("dst_col", [P, TILES], i32)
        rdeg = sb("rdeg", [P, TILES])

        loaded = sem("weights_loaded")
        edges_ready = sem("edge_indices_ready")
        turns = sem("turns")

        def hold(eng):
            eng.sem_inc(turns, 1)

        x1_filled = sem("x1_table_filled")
        ye_filled = sem("ye_table_filled")

        fills = ExitStack()
        fill_x1 = fills.enter_context(nc.sbuf_tensor("fill_x1", [P, FILL_R, D], f32))
        fill_ye = fills.enter_context(nc.sbuf_tensor("fill_ye", [P, FILL_R, YW], f32))

        with ExitStack() as st:
            def tb(name, shape, dt=f32):
                return st.enter_context(nc.sbuf_tensor(name, shape, dt))
            pad_src = tb("pad_src", [1, EP - E], i32)
            pad_dst = tb("pad_dst", [1, EP - E + 1], i32)
            pad_front = tb("pad_front", [1, 1], i32)
            pad_ea = tb("pad_ea", [P, (EP - E) * DE // P])
            src_t = tb("src_t", [TQ, 2 * P], i32)
            dst_t = tb("dst_t", [TQ, 2 * P], i32)
            nxt_t = tb("nxt_t", [TQ, 2 * P], i32)
            src_f = tb("src_f", [TQ, 2 * P])
            dst_f = tb("dst_f", [TQ, 2 * P])
            put_f = tb("put_f", [TQ, 2 * P])
            same = tb("same", [TQ, 2 * P])
            x1c = tb("x1c", [P, D])
            x2n = tb("x2n", [P, D])
            x2t = tb("x2t", [P, D])
            st6 = tb("st6", [P, 6])
            mv = tb("mv", [P, 2])
            rs = tb("rs", [P, 1])
            ps_i = [st.enter_context(nc.psum_tensor(f"ps_i{k}", [P, 512], f32)) for k in range(6)]
            ps_t = st.enter_context(nc.psum_tensor("ps_t", [P, 512], f32))
            ps_y = st.enter_context(nc.psum_tensor("ps_y", [P, 512], f32))

            zeroed = sem("ident_zeroed")
            ident_ok = sem("ident_ready")
            pads_ok = sem("pads_ready")
            copied = sem("edges_copied")
            idx_loaded = sem("indices_loaded")
            idx_f = sem("indices_float")
            idx_t = sem("indices_transposed")
            v_step = sem("prologue_vector_steps")
            c_var = sem("const_row_variance")
            c_std = sem("const_row_std")
            c_norm = sem("const_row_normed")
            c_tr = sem("const_row_transposed")
            c_act = sem("const_row_relu")
            c_y = sem("const_row_y")
            c_x1 = sem("const_fill_x1")
            c_ye = sem("const_fill_ye")

            with nc.Block() as block:
                @block.sync
                def _(sp):
                    col = lambda a: a.rearrange("(p o) -> p o", o=1)
                    bc = lambda a: a.rearrange("(o d) -> o d", o=1).to_broadcast([P, D])
                    weights = [
                        (w1[:, :], W1), (w2[:, :], W2), (wo[:, :], Wo),
                        (b1_row[:, :], b1.rearrange("(o d) -> o d", o=1)),
                        (g1_bc[:, :], bc(g1)), (be1_bc[:, :], bc(be1)), (b2_bc[:, :], bc(b2)),
                        (bo_bc[:, :], bc(bo)), (c2_bc[:, :], bc(c2)),
                        (g2_col[:, :], col(g2)), (be2_col[:, :], col(be2)),
                        (vx[:, :], V1[0:D, :]), (ve[:, :], V1[D:D + DE, :]), (vu[:, :], V1[D + DE:, :]),
                        (v2[:, :, :], V2.rearrange("(k p) d -> p k d", p=P)),
                        (u_col[:, :], u[0:1, :].rearrange("o d -> d o")),
                        (c1_col[:, :], c1.rearrange("(k p) -> p k", p=P)),
                        (gamma_col[:, :], gamma.rearrange("(k p) -> p k", p=P)),
                        (beta_col[:, :], beta.rearrange("(k p) -> p k", p=P)),
                    ]
                    with nc.allow_non_contiguous_dma(reason="small columns"):
                        for to, frm in weights:
                            sp.dma_start(to, frm).then_inc(loaded, 16)
                    sp.wait_ge(loaded, 16 * len(weights))
                    sp.wait_ge(c_x1, 1)
                    sp.dma_start(x1_tab.rearrange("(p a r) d -> p a (r d)", a=FILL_A, r=FILL_R),
                                 fill_x1[:, :, :].rearrange("p (o r) d -> p o (r d)", o=1)
                                 .to_broadcast([P, FILL_A, FILL_R * D])).then_inc(x1_filled, 16)
                    sp.wait_ge(c_ye, 1)
                    sp.dma_start(ye_tab.rearrange("(p a r) d -> p a (r d)", a=FILL_A, r=FILL_R),
                                 fill_ye[:, :, :].rearrange("p (o r) d -> p o (r d)", o=1)
                                 .to_broadcast([P, FILL_A, FILL_R * YW])).then_inc(ye_filled, 16)

                @block.gpsimd
                def _(pool):
                    pool.memset(ident[:, :], 0.0).then_inc(zeroed, 1)
                    pool.memset(pad_src[:, :], 0)
                    pool.memset(pad_dst[:, :], N)
                    pool.memset(pad_front[:, :], -1)
                    pool.memset(pad_ea[:, :], 0.0)
                    pool.memset(ones[:, :], 1.0).then_inc(pads_ok, 1)
                    pool.wait_ge(zeroed, 1)
                    pool.affine_select(out=ident[:, :], in_=ident[:, :], compare_op=ALU.not_equal, fill=1.0,
                                       base=0, pattern=[[-1, P]], channel_multiplier=1).then_inc(ident_ok, 1)

                @block.scalar
                def _(act):
                    act.dma_start(src_s[0:E], src).then_inc(copied, 16)
                    act.dma_start(dst_s[1:E + 1], dst).then_inc(copied, 16)
                    act.dma_start(ea_s[0:E, :], ea).then_inc(copied, 16)
                    act.wait_ge(pads_ok, 1)
                    act.dma_start(src_s[E:EP].rearrange("(o n) -> o n", o=1), pad_src[:, :]).then_inc(copied, 16)
                    act.dma_start(dst_s[E + 1:EP + 2].rearrange("(o n) -> o n", o=1),
                                  pad_dst[:, :]).then_inc(copied, 16)
                    act.dma_start(dst_s[0:1].rearrange("(o n) -> o n", o=1), pad_front[:, :]).then_inc(copied, 16)
                    act.dma_start(ea_s[E:EP, :].rearrange("r d -> (r d)").rearrange("(p n) -> p n", p=P),
                                  pad_ea[:, :]).then_inc(copied, 16)
                    act.wait_ge(copied, 16 * 7)
                    rows = lambda a: a.rearrange("(q n) -> q n", n=2 * P)
                    act.dma_start(src_t[:, :], rows(src_s)).then_inc(idx_loaded, 16)
                    act.dma_start(dst_t[:, :], rows(dst_s[1:EP + 1])).then_inc(idx_loaded, 16)
                    act.dma_start(nxt_t[:, :], rows(dst_s[2:EP + 2])).then_inc(idx_loaded, 16)
                    act.wait_ge(c_var, 1)
                    act.activation(rs[:, :], rs[:, :], ACT.Sqrt).then_inc(c_std, 1)
                    act.wait_ge(c_tr, 1)
                    act.activation(x2t[:, :], ps_t[:, 0:D], ACT.Relu, bias=be2_col[:, :],
                                   scale=g2_col[:, :]).then_inc(c_act, 1)

                @block.tensor
                def _(pe):
                    pe.wait_ge(ident_ok, 1)
                    pe.wait_ge(c_norm, 1)
                    pe.transpose(ps_t[:, 0:D], x2n[:, :], ident[:, :]).then_inc(c_tr, 1)
                    pe.wait_ge(c_act, 1)
                    pe.matmul(ps_y[:, 0:D], x2t[:, :], wo[:, :], start=True, stop=True).then_inc(c_y, 1)
                    pe.wait_ge(idx_f, 1)
                    for k, t in enumerate((src_f, dst_f, put_f)):
                        for j in range(2):
                            last = pe.transpose(ps_i[2 * k + j][:, 0:TQ], t[:, j * P:(j + 1) * P],
                                                ident[0:TQ, 0:TQ])
                    last.then_inc(idx_t, 1)

                @block.vector
                def _(dve):
                    done = [0]

                    def step(ins):
                        done[0] += 1
                        ins.then_inc(v_step, 1)
                        dve.wait_ge(v_step, done[0])

                    dve.wait_ge(loaded, 16 * 19)
                    step(dve.tensor_scalar(x1c[:, :], be1_bc[:, :], 0.0, None, ALU.max))
                    dve.tensor_copy(fill_x1[:, :, :], x1c[:, :].rearrange("p (o d) -> p o d", o=1)
                                    .to_broadcast([P, FILL_R, D])).then_inc(c_x1, 1)
                    step(dve.bn_stats(st6[:, :], x1c[:, :]))
                    step(dve.bn_aggr(mv[:, :], st6[:, :]))
                    dve.tensor_scalar(rs[:, :], mv[:, 1:2], EPS, None, ALU.add).then_inc(c_var, 1)
                    dve.wait_ge(c_std, 1)
                    step(dve.reciprocal(rs[:, :], rs[:, :]))
                    dve.tensor_scalar(x2n[:, :], x1c[:, :], mv[:, 0:1], rs[:, :], ALU.subtract,
                                      ALU.mult).then_inc(c_norm, 1)
                    dve.memset(fill_ye[:, :, D:YW], 0.0)
                    dve.wait_ge(c_y, 1)
                    step(dve.tensor_tensor(x1c[:, :], ps_y[:, 0:D], bo_bc[:, :], ALU.add))
                    dve.tensor_copy(fill_ye[:, :, 0:D], x1c[:, :].rearrange("p (o d) -> p o d", o=1)
                                    .to_broadcast([P, FILL_R, D])).then_inc(c_ye, 1)
                    dve.wait_ge(idx_loaded, 16 * 3)
                    dve.tensor_copy(src_f[:, :], src_t[:, :])
                    dve.tensor_copy(dst_f[:, :], dst_t[:, :])
                    step(dve.tensor_tensor(same[:, :], dst_t[:, :], nxt_t[:, :], ALU.is_equal))
                    dve.scalar_tensor_tensor(put_f[:, :], same[:, :], float(SKIP), dst_f[:, :], ALU.mult,
                                             ALU.add).then_inc(idx_f, 1)
                    dve.wait_ge(idx_t, 1)
                    for k, t in enumerate((src_idx, dst_col, put_idx)):
                        for j in range(2):
                            last = dve.tensor_copy(t[:, j:TILES:2], ps_i[2 * k + j][:, 0:TQ])
                    last.then_inc(edges_ready, 1)

        gat = [sem(f"rows_gathered{k}") for k in range(TS)]
        with ExitStack() as st:
            def tb(name, shape, dt=f32):
                return st.enter_context(nc.sbuf_tensor(name, shape, dt))

            def ps(name):
                return st.enter_context(nc.psum_tensor(name, [P, 512], f32))
            idx = tb("idx_a", [P, TS], i32)
            pidx = tb("put_a", [P, TS], i32)
            xg = [tb(f"xg{k}", [P, D]) for k in range(TS)]
            drow = [tb(f"drow{j}", [P, STEP + 1], i32) for j in range(2)]
            S = [tb(f"S{h}", [P, TH, P]) for h in range(2)]
            Q = [tb(f"Q{h}", [P, TH, P]) for h in range(2)]
            aT = tb("aT", [P, TS, P])
            degr = tb("degr", [1, TS, P])
            degc = tb("degc", [P, 2, TH])
            de2 = tb("de2", [P, 2, TH])
            st6 = tb("st6a", [P, 2, TH, 6])
            mv = tb("mva", [P, 2, TH, 2])
            var = tb("vara", [P, 2, TH])
            r = tb("ra", [P, 2, TH])
            nmr = tb("nmra", [P, 2, TH])
            z = tb("za", [P, 2, TH, D])
            x1 = [tb(f"x1_{k}", [P, D]) for k in range(TS)]
            x1b = tb("x1b", [P, 2, TH, D])
            psA = [ps("psA0"), ps("psA1")]
            psR = [ps("psR0"), ps("psR1")]
            psZ = [ps("psZ0"), ps("psZ1")]
            psC = [ps("psC0"), ps("psC1")]

            row_in = [sem(f"a_dst_row_loaded{j}") for j in range(2)]
            idx_copied = sem("a_idx_copied")
            pidx_copied = sem("a_put_idx_copied")
            match = sem("a_match_ready")
            summed = sem("a_tile_sums_ready")
            aT_done = sem("a_sums_with_carry")
            dg_done = sem("a_degrees_with_carry")
            z_done = sem("a_product_ready")
            deg_out = sem("a_degree_column")
            small = sem("a_small_steps")
            std_done = sem("a_std_ready")
            r1_done = sem("a_rstd_ready")
            r_done = sem("a_rstd_and_shift_ready")
            n_done = sem("a_normed")
            zg = sem("a_scaled")
            zb = sem("a_shifted")
            x1_done = sem("a_x1_ready")
            x1b_done = sem("a_x1_plus_b2_ready")
            put = [sem(f"a_x1_scattered{k}") for k in range(TS)]
            kept = [sem(f"a_x1_slot_stored{h}") for h in range(2)]
            primed = sem("a_carry_zeroed")

            with nc.Block() as block:
                @block.sync
                def _(sp):
                    def load(s, j):
                        wait(sp, match, 2 * s - 2)
                        sp.dma_start(drow[j][:, :], dst_s[bass.ds(s * STEP, STEP + 1)]
                                     .rearrange("(o n) -> o n", o=1).to_broadcast([P, STEP + 1])
                                     ).then_inc(row_in[j], 16)

                    def store(s, j):
                        for h in range(2):
                            sp.wait_ge(x1b_done, 2 * s + h + 1)
                            sp.dma_start(x1_slot[bass.ds(2 * s + h, 1), :, :].rearrange("o p n -> (o p) n"),
                                         x1b[:, h, :, :].rearrange("p t d -> p (t d)")).then_inc(kept[h], 16)

                    load(0, 0)
                    load(1, 1)

                    def pair(i, last=False):
                        for j in range(2):
                            s = 2 * i + j
                            store(s, j)
                            if not last or j == 0:
                                load(s + 2, j)
                    PAIRS = STEPS // 2
                    with sp.Fori(0, PAIRS - 1) as i:
                        pair(i)
                    pair(PAIRS - 1, last=True)
                    store(STEPS - 1, 0)
                    for h in range(2):
                        sp.wait_ge(kept[h], 16 * STEPS)

                @block.gpsimd
                def _(pool):
                    def gather(s, h):
                        for k in range(h * TH, h * TH + TH):
                            wait(pool, gat[k], 16 * s)
                        pool.tensor_copy(idx[:, h * TH:h * TH + TH],
                                         src_idx[:, bass.ds(s * TS + h * TH, TH)]).then_inc(idx_copied, 1)
                        pool.wait_ge(idx_copied, 2 * s + h + 1)
                        wait(pool, summed, 2 * s + h - 1)
                        hold(pool)
                        for k in range(h * TH, h * TH + TH):
                            pool.indirect_dma_start(
                                xg[k][:, :], None, x[:, :],
                                bass.IndirectOffsetOnAxis(ap=idx[:, k:k + 1], axis=0),
                                bounds_check=N - 1, oob_is_err=False).then_inc(gat[k], 16)

                    def scatter(s, h):
                        for k in range(h * TH, h * TH + TH):
                            wait(pool, put[k], 16 * s)
                        pool.tensor_copy(pidx[:, h * TH:h * TH + TH],
                                         put_idx[:, bass.ds(s * TS + h * TH, TH)]).then_inc(pidx_copied, 1)
                        pool.wait_ge(pidx_copied, 2 * s + h + 1)
                        pool.wait_ge(x1_done, 2 * s + h + 1)
                        pool.wait_ge(x1_filled, 16)
                        hold(pool)
                        for k in range(h * TH, h * TH + TH):
                            pool.indirect_dma_start(
                                x1_tab[:, :], bass.IndirectOffsetOnAxis(ap=pidx[:, k:k + 1], axis=0),
                                x1[k][:, :], None, bounds_check=N - 1,
                                oob_is_err=False).then_inc(put[k], 16)

                    for h in range(2):
                        gather(0, h)

                    def step(s, last=False):
                        for h in range(2):
                            if not last:
                                gather(s + 1, h)
                            scatter(s, h)
                    step(0)
                    with pool.Fori(1, STEPS - 1) as s:
                        step(s)
                    step(STEPS - 1, last=True)
                    for k in range(TS):
                        pool.wait_ge(put[k], 16 * STEPS)

                @block.tensor
                def _(pe):
                    def step(s):
                        def sums(h):
                            pe.wait_ge(match, 2 * s + h + 1)
                            wait(pe, aT_done, TS * s - TH + h * TH)
                            wait(pe, dg_done, TS * s - TH + h * TH)
                            for j in range(TH):
                                k = h * TH + j
                                pe.wait_ge(gat[k], 16 * (s + 1))
                                pe.matmul(psA[h][:, j * P:(j + 1) * P], xg[k][:, :], S[h][:, j, :],
                                          start=True, stop=True)
                            pe.matmul(psR[h][0:1, :], ones[:, :], S[h][:, :, :].rearrange("p t n -> p (t n)"),
                                      start=True, stop=True).then_inc(summed, 1)

                        def product(h):
                            pe.wait_ge(aT_done, TS * s + h * TH + TH)
                            pe.wait_ge(dg_done, TS * s + h * TH + TH)
                            wait(pe, n_done, 2 * s + h - 1)
                            wait(pe, deg_out, 2 * s + h - 1)
                            for j in range(TH):
                                k = h * TH + j
                                o = psZ[h][:, j * D:(j + 1) * D]
                                pe.matmul(o, aT[:, k, :], w1[:, :], start=True, stop=False)
                                pe.matmul(o, degr[:, k, :], b1_row[:, :], start=False, stop=True)
                                last = pe.matmul(psC[h][:, j:j + 1], degr[:, k, :], ones[0:1, :],
                                                 start=True, stop=True)
                            last.then_inc(z_done, 1)
                        for h in range(2):
                            sums(h)
                            product(h)
                    step(0)
                    with pe.Fori(1, STEPS) as s:
                        step(s)

                @block.scalar
                def _(act):
                    def step(s):
                        for h in range(2):
                            act.wait_ge(small, 4 * (2 * s + h) + 4)
                            act.activation(var[:, h, :], var[:, h, :], ACT.Sqrt).then_inc(std_done, 1)
                            act.wait_ge(r_done, 2 * s + h + 1)
                            wait(act, zg, 2 * s + h - 1)
                            for j in range(TH):
                                last = act.activation(z[:, h, j, :], psZ[h][:, j * D:(j + 1) * D], ACT.Identity,
                                                      bias=nmr[:, h, j:j + 1], scale=r[:, h, j:j + 1])
                            last.then_inc(n_done, 1)
                            act.wait_ge(zb, 2 * s + h + 1)
                            for j in range(TH):
                                k = h * TH + j
                                wait(act, put[k], 16 * s)
                            wait(act, x1b_done, 2 * s + h - 1)
                            for j in range(TH):
                                last = act.activation(x1[h * TH + j][:, :], z[:, h, j, :], ACT.Relu)
                            last.then_inc(x1_done, 1)
                    step(0)
                    with act.Fori(1, STEPS) as s:
                        step(s)

                @block.vector
                def _(dve):
                    dve.memset(aT[:, TS - 1, :], 0.0)
                    dve.memset(degr[:, TS - 1, :], 0.0).then_inc(primed, 1)
                    dve.wait_ge(primed, 1)

                    def matches(s, h, b, n):
                        g = 2 * s + h
                        if h == 0:
                            dve.wait_ge(row_in[b], 16 * n)
                        wait(dve, summed, g - 1)
                        wait(dve, aT_done, TS * s - TH + h * TH)
                        wait(dve, dg_done, TS * s - TH + h * TH)
                        cur = drow[b][:, 1 + h * HALF:1 + (h + 1) * HALF].rearrange("p (t n) -> p t n", n=P)
                        own = dst_col[:, bass.ds(s * TS + h * TH, TH)].rearrange("p (t o) -> p t o", o=1)
                        before = drow[b][:, h * HALF:(h + 1) * HALF:P].rearrange("p (t o) -> p t o", o=1)
                        dve.tensor_tensor(S[h][:, :, :], cur, own.to_broadcast([P, TH, P]), ALU.is_equal)
                        dve.tensor_tensor(Q[h][:, :, :], cur, before.to_broadcast([P, TH, P]),
                                          ALU.is_equal).then_inc(match, 1)

                    def half(s, h, after):
                        g = 2 * s + h
                        dve.wait_ge(match, g + 1)
                        dve.wait_ge(summed, g + 1)
                        wait(dve, z_done, g - 1)
                        for j in range(TH):
                            k = h * TH + j
                            b4 = (k - 1) % TS
                            wait(dve, aT_done, TS * s + k)
                            dve.scalar_tensor_tensor(aT[:, k, :], Q[h][:, j, :], aT[:, b4, P - 1:P],
                                                     psA[h][:, j * P:(j + 1) * P], ALU.mult,
                                                     ALU.add).then_inc(aT_done, 1)
                            wait(dve, dg_done, TS * s + k)
                            dve.scalar_tensor_tensor(degr[:, k, :], Q[h][0:1, j, :], degr[:, b4, P - 1:P],
                                                     psR[h][0:1, j * P:(j + 1) * P], ALU.mult,
                                                     ALU.add).then_inc(dg_done, 1)
                        if after:
                            matches(*after)
                        dve.wait_ge(z_done, g + 1)
                        dve.tensor_copy(degc[:, h, :], psC[h][:, 0:TH]).then_inc(deg_out, 1)
                        for j in range(TH):
                            last = dve.bn_stats(st6[:, h, j, :], psZ[h][:, j * D:(j + 1) * D])
                        last.then_inc(small, 1)
                        S7 = 4
                        dve.wait_ge(small, S7 * g + 1)
                        dve.wait_ge(deg_out, g + 1)
                        dve.reciprocal(rdeg[:, bass.ds(s * TS + h * TH, TH)], degc[:, h, :])
                        dve.scalar_tensor_tensor(de2[:, h, :], degc[:, h, :], EPS, degc[:, h, :], ALU.mult,
                                                 ALU.mult).then_inc(small, 1)
                        for j in range(TH):
                            last = dve.bn_aggr(mv[:, h, j, :], st6[:, h, j, :])
                        last.then_inc(small, 1)
                        dve.wait_ge(small, S7 * g + 3)
                        dve.tensor_tensor(var[:, h, :], mv[:, h, :, 1], de2[:, h, :], ALU.add).then_inc(small, 1)
                        dve.wait_ge(std_done, g + 1)
                        wait(dve, n_done, g - 1)
                        dve.reciprocal(r[:, h, :], var[:, h, :]).then_inc(r1_done, 1)
                        dve.wait_ge(r1_done, g + 1)
                        dve.scalar_tensor_tensor(nmr[:, h, :], mv[:, h, :, 0], -1.0, r[:, h, :], ALU.mult,
                                                 ALU.mult).then_inc(r_done, 1)
                        dve.wait_ge(n_done, g + 1)
                        row = lambda a: a[:, :].rearrange("p (o d) -> p o d", o=1).to_broadcast([P, TH, D])
                        zz = z[:, h, :, :]
                        dve.tensor_tensor(zz, zz, row(g1_bc), ALU.mult).then_inc(zg, 1)
                        dve.wait_ge(zg, g + 1)
                        dve.tensor_tensor(zz, zz, row(be1_bc), ALU.add).then_inc(zb, 1)
                        dve.wait_ge(x1_done, g + 1)
                        wait(dve, kept[h], 16 * s)
                        for j in range(TH):
                            last = dve.tensor_tensor(x1b[:, h, j, :], x1[h * TH + j][:, :], b2_bc[:, :], ALU.add)
                        last.then_inc(x1b_done, 1)

                    def step(s, b, n, last=False):
                        half(s, 0, (s, 1, b, n))
                        half(s, 1, None if last else (s + 1, 0, 1 - b, n + b))
                    matches(0, 0, 0, 1)
                    step(0, 0, 1)
                    step(1, 1, 1)
                    with dve.Fori(1, STEPS // 2) as i:
                        step(2 * i, 0, i + 1)
                        step(2 * i + 1, 1, i + 1)
                    step(STEPS - 1, 0, STEPS // 2 + 1, last=True)

        with ExitStack() as st:
            def tb(name, shape, dt=f32):
                return st.enter_context(nc.sbuf_tensor(name, shape, dt))

            def ps(name):
                return st.enter_context(nc.psum_tensor(name, [P, 512], f32))
            idx = tb("idx_b", [P, TS], i32)
            pidx = tb("put_b", [P, TS], i32)
            xg = [tb(f"x1g{k}", [P, D]) for k in range(TS)]
            eg = [tb(f"eg{h}", [P, TH, DE]) for h in range(2)]
            x1r = [tb(f"x1r{h}", [P, TH, D]) for h in range(2)]
            drow = [tb(f"drow_b{j}", [P, STEP + 1], i32) for j in range(2)]
            S = [tb(f"S_b{h}", [P, TH, P]) for h in range(2)]
            Q = [tb(f"Q_b{h}", [P, TH, P]) for h in range(2)]
            aT = tb("aT_b", [P, TS, P])
            eT = tb("eT_b", [DE, TS, P])
            st6 = tb("st6b", [P, 2, TH, 6])
            mv = tb("mvb", [P, 2, TH, 2])
            var = tb("varb", [P, 2, TH])
            r = tb("rb", [P, 2, TH])
            nmr = tb("nmrb", [P, 2, TH])
            v = tb("vb", [P, 2, TH, D])
            n2 = [tb(f"n2_{k}", [P, D]) for k in range(TS)]
            x2T = [tb(f"x2T{h}", [P, TH, P]) for h in range(2)]
            ye = [tb(f"ye{k}", [P, YW]) for k in range(TS)]
            psA = [ps("psA0b"), ps("psA1b")]
            psZ = [ps("psZ0b"), ps("psZ1b")]
            psE = ps("psEb")
            psT = ps("psTb")
            psX = ps("psXb")
            psY = ps("psYb")

            row_in = [sem(f"b_dst_row_loaded{j}") for j in range(2)]
            e_in = [sem(f"b_edge_attr_loaded{h}") for h in range(2)]
            x1_in = [sem(f"b_x1_loaded{h}") for h in range(2)]
            gat = [sem(f"b_x1_gathered{k}") for k in range(TS)]
            put = [sem(f"b_rows_scattered{k}") for k in range(TS)]
            idx_copied = sem("b_idx_copied")
            pidx_copied = sem("b_put_idx_copied")
            match = sem("b_match_ready")
            summed = sem("b_tile_sums_ready")
            aT_done = sem("b_sums_with_carry")
            eT_done = sem("b_edge_sums_with_carry")
            z_done = sem("b_product_ready")
            et_done = sem("b_edge_sums_transposed")
            v_done = sem("b_residual_added")
            small = sem("b_small_steps")
            std_done = sem("b_std_ready")
            r1_done = sem("b_rstd_ready")
            r_done = sem("b_rstd_and_shift_ready")
            n_done = sem("b_normed")
            nt_done = sem("b_normed_transposed")
            x2_done = sem("b_x2_ready")
            y_done = sem("b_y_product_ready")
            ye_y = sem("b_row_y_part_ready")
            ye_e = sem("b_row_edge_part_ready")
            primed = sem("b_carry_zeroed")

            with nc.Block() as block:
                @block.sync
                def _(sp):
                    def load_rows(s, j):
                        wait(sp, match, 2 * s - 2)
                        sp.dma_start(drow[j][:, :], dst_s[bass.ds(s * STEP, STEP + 1)]
                                     .rearrange("(o n) -> o n", o=1).to_broadcast([P, STEP + 1])
                                     ).then_inc(row_in[j], 16)

                    def load_half(s, h):
                        g = 2 * s + h
                        wait(sp, summed, g - 1)
                        sp.dma_start(eg[h][:, :, :], ea_s[bass.ds(g * HALF, HALF), :]
                                     .rearrange("(t p) c -> p t c", p=P)).then_inc(e_in[h], 16)
                        wait(sp, v_done, g - 1)
                        hold(sp)
                        sp.dma_start(x1r[h][:, :, :].rearrange("p t d -> p (t d)"),
                                     x1_slot[bass.ds(g, 1), :, :].rearrange("o p n -> (o p) n")
                                     ).then_inc(x1_in[h], 16)
                    load_rows(0, 0)
                    load_rows(1, 1)
                    for h in range(2):
                        load_half(0, h)

                    def step(s, j, rows=True):
                        for h in range(2):
                            load_half(s + 1, h)
                        if rows:
                            load_rows(s + 2, j)
                    with sp.Fori(0, STEPS // 2 - 1) as i:
                        step(2 * i, 0)
                        step(2 * i + 1, 1)
                    step(STEPS - 3, 0)
                    step(STEPS - 2, 1, rows=False)

                @block.gpsimd
                def _(pool):
                    def gather(s, h):
                        for k in range(h * TH, h * TH + TH):
                            wait(pool, gat[k], 16 * s)
                        pool.tensor_copy(idx[:, h * TH:h * TH + TH],
                                         src_idx[:, bass.ds(s * TS + h * TH, TH)]).then_inc(idx_copied, 1)
                        pool.wait_ge(idx_copied, 2 * s + h + 1)
                        wait(pool, summed, 2 * s + h - 1)
                        hold(pool)
                        for k in range(h * TH, h * TH + TH):
                            pool.indirect_dma_start(
                                xg[k][:, :], None, x1_tab[:, :],
                                bass.IndirectOffsetOnAxis(ap=idx[:, k:k + 1], axis=0),
                                bounds_check=N - 1, oob_is_err=False).then_inc(gat[k], 16)

                    def scatter(s, h):
                        for k in range(h * TH, h * TH + TH):
                            wait(pool, put[k], 16 * s)
                        pool.tensor_copy(pidx[:, h * TH:h * TH + TH],
                                         put_idx[:, bass.ds(s * TS + h * TH, TH)]).then_inc(pidx_copied, 1)
                        pool.wait_ge(pidx_copied, 2 * s + h + 1)
                        pool.wait_ge(ye_y, 2 * s + h + 1)
                        pool.wait_ge(ye_e, 2 * s + h + 1)
                        pool.wait_ge(ye_filled, 16)
                        hold(pool)
                        for k in range(h * TH, h * TH + TH):
                            pool.indirect_dma_start(
                                ye_tab[:, :], bass.IndirectOffsetOnAxis(ap=pidx[:, k:k + 1], axis=0),
                                ye[k][:, :], None, bounds_check=N - 1,
                                oob_is_err=False).then_inc(put[k], 16)

                    for h in range(2):
                        gather(0, h)

                    def step(s, last=False):
                        for h in range(2):
                            if not last:
                                gather(s + 1, h)
                            scatter(s, h)
                    step(0)
                    with pool.Fori(1, STEPS - 1) as s:
                        step(s)
                    step(STEPS - 1, last=True)
                    for k in range(TS):
                        pool.wait_ge(put[k], 16 * STEPS)

                @block.tensor
                def _(pe):
                    def sums(s, h):
                        g = 2 * s + h
                        pe.wait_ge(match, g + 1)
                        pe.wait_ge(e_in[h], 16 * (s + 1))
                        wait(pe, aT_done, TS * s - TH + h * TH)
                        wait(pe, eT_done, TS * s + h * TH)
                        for j in range(TH):
                            k = h * TH + j
                            pe.wait_ge(gat[k], 16 * (s + 1))
                            pe.matmul(psA[h][:, j * P:(j + 1) * P], xg[k][:, :], S[h][:, j, :],
                                      start=True, stop=True)
                            last = pe.matmul(psE[0:DE, j * P:(j + 1) * P], eg[h][:, j, :], S[h][:, j, :],
                                             start=True, stop=True)
                        last.then_inc(summed, 1)

                    def product(s, h):
                        g = 2 * s + h
                        pe.wait_ge(aT_done, TS * s + h * TH + TH)
                        wait(pe, v_done, g - 1)
                        for j in range(TH):
                            last = pe.matmul(psZ[h][:, j * D:(j + 1) * D], aT[:, h * TH + j, :], w2[:, :],
                                             start=True, stop=True)
                        last.then_inc(z_done, 1)
                        pe.wait_ge(eT_done, TS * s + h * TH + TH)
                        wait(pe, ye_e, g)
                        for j in range(TH):
                            last = pe.transpose(psT[:, j * DE:(j + 1) * DE], eT[:, h * TH + j, :],
                                                ident[0:DE, 0:DE])
                        last.then_inc(et_done, 1)

                    def turn(s, h):
                        g = 2 * s + h
                        pe.wait_ge(n_done, g + 1)
                        wait(pe, x2_done, g)
                        for j in range(TH):
                            last = pe.transpose(psX[:, j * P:(j + 1) * P], n2[h * TH + j][:, :], ident[:, :])
                        last.then_inc(nt_done, 1)

                    def outp(s, h):
                        g = 2 * s + h
                        pe.wait_ge(x2_done, g + 1)
                        wait(pe, ye_y, g)
                        for j in range(TH):
                            last = pe.matmul(psY[:, j * D:(j + 1) * D], x2T[h][:, j, :], wo[:, :],
                                             start=True, stop=True)
                        last.then_inc(y_done, 1)

                    def half(s, h, before):
                        sums(s, h)
                        if before:
                            turn(*before)
                        product(s, h)
                        if before:
                            outp(*before)
                    half(0, 0, None)
                    half(0, 1, (0, 0))
                    with pe.Fori(1, STEPS) as s:
                        half(s, 0, (s - 1, 1))
                        half(s, 1, (s, 0))
                    turn(STEPS - 1, 1)
                    outp(STEPS - 1, 1)

                @block.scalar
                def _(act):
                    def step(s):
                        for h in range(2):
                            g = 2 * s + h
                            act.wait_ge(small, 3 * g + 3)
                            act.activation(var[:, h, :], var[:, h, :], ACT.Sqrt).then_inc(std_done, 1)
                            act.wait_ge(r_done, g + 1)
                            wait(act, nt_done, g - 1)
                            for j in range(TH):
                                last = act.activation(n2[h * TH + j][:, :], v[:, h, j, :], ACT.Identity,
                                                      bias=nmr[:, h, j:j + 1], scale=r[:, h, j:j + 1])
                            last.then_inc(n_done, 1)
                            act.wait_ge(et_done, g + 1)
                            for k in range(h * TH, h * TH + TH):
                                wait(act, put[k], 16 * s)
                            for j in range(TH):
                                last = act.activation(ye[h * TH + j][:, D:YW], psT[:, j * DE:(j + 1) * DE],
                                                      ACT.Copy, scale=rdeg[:, bass.ds(s * TS + h * TH + j, 1)])
                            last.then_inc(ye_e, 1)
                            act.wait_ge(nt_done, g + 1)
                            wait(act, y_done, g - 1)
                            act.activation(x2T[h][:, :, :].rearrange("p t n -> p (t n)"), psX[:, :], ACT.Relu,
                                           bias=be2_col[:, :], scale=g2_col[:, :]).then_inc(x2_done, 1)
                    step(0)
                    with act.Fori(1, STEPS) as s:
                        step(s)

                @block.vector
                def _(dve):
                    dve.memset(aT[:, TS - 1, :], 0.0)
                    dve.memset(eT[:, TS - 1, :], 0.0).then_inc(primed, 1)
                    dve.wait_ge(primed, 1)

                    def matches(s, h, b, n):
                        g = 2 * s + h
                        if h == 0:
                            dve.wait_ge(row_in[b], 16 * n)
                        wait(dve, summed, g - 1)
                        wait(dve, aT_done, TS * s - TH + h * TH)
                        wait(dve, eT_done, TS * s - TH + h * TH)
                        cur = drow[b][:, 1 + h * HALF:1 + (h + 1) * HALF].rearrange("p (t n) -> p t n", n=P)
                        own = dst_col[:, bass.ds(s * TS + h * TH, TH)].rearrange("p (t o) -> p t o", o=1)
                        before = drow[b][:, h * HALF:(h + 1) * HALF:P].rearrange("p (t o) -> p t o", o=1)
                        dve.tensor_tensor(S[h][:, :, :], cur, own.to_broadcast([P, TH, P]), ALU.is_equal)
                        dve.tensor_tensor(Q[h][:, :, :], cur, before.to_broadcast([P, TH, P]),
                                          ALU.is_equal).then_inc(match, 1)

                    def rows_y(s, h):
                        g = 2 * s + h
                        dve.wait_ge(y_done, g + 1)
                        for k in range(h * TH, h * TH + TH):
                            wait(dve, put[k], 16 * s)
                        for j in range(TH):
                            last = dve.tensor_tensor(ye[h * TH + j][:, 0:D], psY[:, j * D:(j + 1) * D],
                                                     bo_bc[:, :], ALU.add)
                        last.then_inc(ye_y, 1)

                    def half(s, h, before, after):
                        g = 2 * s + h
                        dve.wait_ge(match, g + 1)
                        dve.wait_ge(summed, g + 1)
                        wait(dve, z_done, g - 1)
                        wait(dve, et_done, g - 1)
                        for j in range(TH):
                            k = h * TH + j
                            b4 = (k - 1) % TS
                            wait(dve, aT_done, TS * s + k)
                            dve.scalar_tensor_tensor(aT[:, k, :], Q[h][:, j, :], aT[:, b4, P - 1:P],
                                                     psA[h][:, j * P:(j + 1) * P], ALU.mult,
                                                     ALU.add).then_inc(aT_done, 1)
                            wait(dve, eT_done, TS * s + k)
                            dve.scalar_tensor_tensor(eT[:, k, :], Q[h][0:DE, j, :], eT[:, b4, P - 1:P],
                                                     psE[0:DE, j * P:(j + 1) * P], ALU.mult,
                                                     ALU.add).then_inc(eT_done, 1)
                        if after:
                            matches(*after)
                        if before:
                            rows_y(*before)
                        dve.wait_ge(z_done, g + 1)
                        dve.wait_ge(x1_in[h], 16 * (s + 1))
                        wait(dve, n_done, g - 1)
                        for j in range(TH):
                            last = dve.scalar_tensor_tensor(
                                v[:, h, j, :], psZ[h][:, j * D:(j + 1) * D],
                                rdeg[:, bass.ds(s * TS + h * TH + j, 1)], x1r[h][:, j, :], ALU.mult, ALU.add)
                        last.then_inc(v_done, 1)
                        dve.wait_ge(v_done, g + 1)
                        for j in range(TH):
                            last = dve.bn_stats(st6[:, h, j, :], v[:, h, j, :])
                        last.then_inc(small, 1)
                        dve.wait_ge(small, 3 * g + 1)
                        hold(dve)
                        for j in range(TH):
                            last = dve.bn_aggr(mv[:, h, j, :], st6[:, h, j, :])
                        last.then_inc(small, 1)
                        dve.wait_ge(small, 3 * g + 2)
                        dve.tensor_scalar(var[:, h, :], mv[:, h, :, 1], EPS, None, ALU.add).then_inc(small, 1)
                        dve.wait_ge(std_done, g + 1)
                        dve.reciprocal(r[:, h, :], var[:, h, :]).then_inc(r1_done, 1)
                        dve.wait_ge(r1_done, g + 1)
                        dve.scalar_tensor_tensor(nmr[:, h, :], mv[:, h, :, 0], -1.0, r[:, h, :], ALU.mult,
                                                 ALU.mult).then_inc(r_done, 1)

                    def step(s, b, n, first=False, last=False):
                        half(s, 0, None if first else (s - 1, 1), (s, 1, b, n))
                        half(s, 1, (s, 0), None if last else (s + 1, 0, 1 - b, n + b))
                    matches(0, 0, 0, 1)
                    step(0, 0, 1, first=True)
                    step(1, 1, 1)
                    with dve.Fori(1, STEPS // 2) as i:
                        step(2 * i, 0, i + 1)
                        step(2 * i + 1, 1, i + 1)
                    step(STEPS - 1, 0, STEPS // 2 + 1, last=True)
                    rows_y(STEPS - 1, 1)
        fills.close()

        U = 3
        LOOPS = BLOCKS // U
        assert BLOCKS == U * LOOPS
        FW = YW + 1

        def rows_of(t, n, pr, rr, c0, c1_):
            return t[bass.ds(n * BLK, pr * rr), c0:c1_].rearrange("(p r) c -> p r c", r=rr)

        def blocks(eng, body):
            for b in range(U):
                body(b, b, 1, P, BR)
            with eng.Fori(1, LOOPS) as i:
                for b in range(U):
                    body(i * U + b, b, i + 1, P, BR)
            body(BLOCKS, 0, LOOPS + 1, REST, 1)

        gx = sb("gx", [P, FW])
        ge = sb("ge", [DE, DE + 1])
        bn_scale = sb("bn_scale", [P, 2])
        bn_shift = sb("bn_shift", [P, 2])
        with ExitStack() as st:
            def tb(name, shape, dt=f32):
                return st.enter_context(nc.sbuf_tensor(name, shape, dt))
            xb = [tb(f"xb{b}", [P, BR, D]) for b in range(U)]
            F = [tb(f"F{b}", [P, BR, FW]) for b in range(U)]
            st6 = tb("st6c", [P, U, BR, 6])
            mv = tb("mvc", [P, U, BR, 2])
            var = tb("varc", [P, U, BR])
            r = tb("rc", [P, U, BR])
            nmr = tb("nmrc", [P, U, BR])
            psG = st.enter_context(nc.psum_tensor("psG", [P, 512], f32))
            psH = st.enter_context(nc.psum_tensor("psH", [P, 512], f32))
            x_in = [sem(f"c_x_loaded{b}") for b in range(U)]
            f_in = [sem(f"c_table_loaded{b}") for b in range(U)]
            stored = [sem(f"c_h0_stored{b}") for b in range(U)]
            ones_set = sem("c_ones_set")
            s_done = sem("c_sum_ready")
            small = sem("c_small_steps")
            std_done = sem("c_std_ready")
            r1_done = sem("c_rstd_ready")
            r_done = sem("c_rstd_and_shift_ready")
            n_done = sem("c_h0_ready")
            m_done = sem("c_moments_added")
            with nc.Block() as block:
                @block.sync
                def _(sp):
                    def body(n, b, f, pr, rr):
                        wait(sp, s_done, n - U + 1)
                        hold(sp)
                        sp.dma_start(xb[b][0:pr, 0:rr, :], rows_of(x, n, pr, rr, 0, D)).then_inc(x_in[b], 16)
                        wait(sp, stored[b], 16 * (f - 1))
                        wait(sp, m_done, n - U + 1)
                        hold(sp)
                        sp.dma_start(F[b][0:pr, 0:rr, 0:YW], rows_of(ye_tab, n, pr, rr, 0, YW)
                                     ).then_inc(f_in[b], 16)
                    blocks(sp, body)

                @block.vector
                def _(dve):
                    for b in range(U):
                        last = dve.memset(F[b][:, :, YW:FW], 1.0)
                    last.then_inc(ones_set, 1)

                    def body(n, b, f, pr, rr):
                        dve.wait_ge(x_in[b], 16 * f)
                        dve.wait_ge(f_in[b], 16 * f)
                        y = F[b][0:pr, 0:rr, 0:D]
                        dve.scalar_tensor_tensor(y, xb[b][0:pr, 0:rr, :], 2.0, y, ALU.mult,
                                                 ALU.add).then_inc(s_done, 1)
                        dve.wait_ge(s_done, n + 1)
                        for j in range(rr):
                            last = dve.bn_stats(st6[0:pr, b, j, :], F[b][0:pr, j, 0:D])
                        last.then_inc(small, 1)
                        dve.wait_ge(small, 3 * n + 1)
                        hold(dve)
                        for j in range(rr):
                            last = dve.bn_aggr(mv[0:pr, b, j, :], st6[0:pr, b, j, :])
                        last.then_inc(small, 1)
                        dve.wait_ge(small, 3 * n + 2)
                        dve.tensor_scalar(var[0:pr, b, 0:rr], mv[0:pr, b, 0:rr, 1], EPS, None,
                                          ALU.add).then_inc(small, 1)
                        dve.wait_ge(std_done, n + 1)
                        wait(dve, n_done, n - U + 1)
                        dve.reciprocal(r[0:pr, b, 0:rr], var[0:pr, b, 0:rr]).then_inc(r1_done, 1)
                        dve.wait_ge(r1_done, n + 1)
                        dve.scalar_tensor_tensor(nmr[0:pr, b, 0:rr], mv[0:pr, b, 0:rr, 0], -1.0,
                                                 r[0:pr, b, 0:rr], ALU.mult, ALU.mult).then_inc(r_done, 1)
                    blocks(dve, body)

                @block.scalar
                def _(act):
                    def body(n, b, f, pr, rr):
                        act.wait_ge(small, 3 * n + 3)
                        act.activation(var[0:pr, b, 0:rr], var[0:pr, b, 0:rr], ACT.Sqrt).then_inc(std_done, 1)
                        act.wait_ge(r_done, n + 1)
                        for j in range(rr):
                            h0 = F[b][0:pr, j, 0:D]
                            last = act.activation(h0, h0, ACT.Identity, bias=nmr[0:pr, b, j:j + 1],
                                                  scale=r[0:pr, b, j:j + 1])
                        last.then_inc(n_done, 1)
                        act.wait_ge(n_done, n + 1)
                        act.dma_start(rows_of(ye_tab, n, pr, rr, 0, D), F[b][0:pr, 0:rr, 0:D]
                                      ).then_inc(stored[b], 16)
                    blocks(act, body)
                    for b in range(U):
                        act.wait_ge(stored[b], 16 * (LOOPS + (b == 0)))

                @block.tensor
                def _(pe):
                    pe.wait_ge(ones_set, 1)

                    def body(n, b, f, pr, rr):
                        pe.wait_ge(n_done, n + 1)
                        for j in range(rr):
                            first = isinstance(n, int) and n == 0 and j == 0
                            end = isinstance(n, int) and n == BLOCKS
                            pe.matmul(psG[:, 0:FW], F[b][0:pr, j, 0:D], F[b][0:pr, j, :], start=first, stop=end)
                            last = pe.matmul(psH[0:DE, 0:DE + 1], F[b][0:pr, j, D:YW], F[b][0:pr, j, D:FW],
                                             start=first, stop=end)
                        last.then_inc(m_done, 1)
                    blocks(pe, body)

                @block.gpsimd
                def _(pool):
                    pool.wait_ge(m_done, BLOCKS + 1)

            gex = tb("gex", [DE, P])
            vgx = tb("vgx", [P, H])
            vge = tb("vge", [DE, H])
            cc = tb("cc", [P, 2])
            mq = tb("mq", [P, 6])
            mu = tb("mu", [P, 2])
            bvar = tb("bvar", [P, 2])
            psT = st.enter_context(nc.psum_tensor("psT_bn", [P, 512], f32))
            psX = st.enter_context(nc.psum_tensor("psX_bn", [P, 512], f32))
            psE = st.enter_context(nc.psum_tensor("psE_bn", [P, 512], f32))
            psM = st.enter_context(nc.psum_tensor("psM_bn", [P, 512], f32))
            vs = sem("n_vector_steps")
            t_done = sem("n_cross_moments_transposed")
            vg_done = sem("n_moment_products")
            pr_done = sem("n_weighted")
            q_done = sem("n_sums_ready")
            std_done = sem("n_std_ready")
            with nc.Block() as block:
                @block.tensor
                def _(pe):
                    pe.wait_ge(vs, 2)
                    pe.transpose(psT[0:DE, 0:P], gx[:, D:YW], ident[:, :]).then_inc(t_done, 1)
                    pe.wait_ge(vs, 3)
                    pe.matmul(psX[:, 0:H], gx[:, 0:D], vx[:, :], start=True, stop=False)
                    pe.matmul(psX[:, 0:H], gex[:, :], ve[:, :], start=False, stop=True)
                    pe.matmul(psE[0:DE, 0:H], gx[:, D:YW], vx[:, :], start=True, stop=False)
                    pe.matmul(psE[0:DE, 0:H], ge[:, 0:DE], ve[:, :], start=False, stop=True).then_inc(vg_done, 1)
                    pe.wait_ge(pr_done, 1)
                    for k in range(2):
                        hk = slice(k * P, (k + 1) * P)
                        pe.matmul(psM[:, k:k + 1], vgx[:, hk], ones[:, :], start=True, stop=False)
                        pe.matmul(psM[:, k:k + 1], vge[:, hk], ones[0:DE, :], start=False, stop=True)
                        pe.matmul(psM[:, 2 + k:3 + k], vx[:, hk], gx[:, YW:FW], start=True, stop=False)
                        pe.matmul(psM[:, 2 + k:3 + k], ve[:, hk], ge[:, DE:DE + 1], start=False, stop=True)
                        last = pe.matmul(psM[:, 4 + k:5 + k], vu[:, hk], u_col[:, :], start=True, stop=True)
                    last.then_inc(q_done, 1)

                @block.scalar
                def _(act):
                    act.wait_ge(vs, 7)
                    act.activation(bvar[:, :], bvar[:, :], ACT.Sqrt).then_inc(std_done, 1)

                @block.vector
                def _(dve):
                    count = [0]

                    def step(ins):
                        count[0] += 1
                        ins.then_inc(vs, 1)
                        dve.wait_ge(vs, count[0])
                    step(dve.tensor_scalar(gx[:, :], psG[:, 0:FW], 1.0 / N, None, ALU.mult))
                    step(dve.tensor_scalar(ge[:, :], psH[0:DE, 0:DE + 1], 1.0 / N, None, ALU.mult))
                    dve.wait_ge(t_done, 1)
                    step(dve.tensor_copy(gex[:, :], psT[0:DE, 0:P]))
                    dve.wait_ge(vg_done, 1)
                    dve.tensor_tensor(vgx[:, :], psX[:, 0:H], vx[:, :], ALU.mult)
                    dve.tensor_tensor(vge[:, :], psE[0:DE, 0:H], ve[:, :], ALU.mult).then_inc(pr_done, 1)
                    dve.wait_ge(q_done, 1)
                    step(dve.tensor_copy(mq[:, :], psM[:, 0:6]))
                    step(dve.tensor_tensor(bvar[:, :], mq[:, 2:4], mq[:, 2:4], ALU.mult))
                    step(dve.tensor_tensor(bvar[:, :], mq[:, 0:2], bvar[:, :], ALU.subtract))
                    step(dve.tensor_scalar(bvar[:, :], bvar[:, :], EPS, None, ALU.add))
                    step(dve.tensor_tensor(cc[:, :], mq[:, 4:6], c1_col[:, :], ALU.add))
                    step(dve.tensor_tensor(mu[:, :], mq[:, 2:4], cc[:, :], ALU.add))
                    step(dve.tensor_tensor(cc[:, :], cc[:, :], mu[:, :], ALU.subtract))
                    dve.wait_ge(std_done, 1)
                    step(dve.reciprocal(bvar[:, :], bvar[:, :]))
                    step(dve.tensor_tensor(bn_scale[:, :], bvar[:, :], gamma_col[:, :], ALU.mult))
                    step(dve.tensor_tensor(bn_shift[:, :], bn_scale[:, :], cc[:, :], ALU.mult))
                    step(dve.tensor_tensor(bn_shift[:, :], bn_shift[:, :], beta_col[:, :], ALU.add))

        with ExitStack() as st:
            def tb(name, shape, dt=f32):
                return st.enter_context(nc.sbuf_tensor(name, shape, dt))
            CH = BLK // 2
            F = [tb(f"Fd{b}", [P, BR, YW]) for b in range(U)]
            hb = [tb(f"hb{b}", [P, BR, D]) for b in range(U)]
            hT = tb("hT", [P, BLK])
            eT = tb("eTd", [DE, BLK])
            aH = tb("aH", [P, 2, BLK])
            v = tb("vd", [P, U, BR, D])
            o = [tb(f"o{b}", [P, BR, D]) for b in range(U)]
            st6 = tb("st6d", [P, U, BR, 6])
            mv = tb("mvd", [P, U, BR, 2])
            var = tb("vard", [P, U, BR])
            r = tb("rd", [P, U, BR])
            nmr = tb("nmrd", [P, U, BR])
            psT = st.enter_context(nc.psum_tensor("psTd", [P, 1024], f32))
            psE = st.enter_context(nc.psum_tensor("psEd", [P, 1024], f32))
            psH = [st.enter_context(nc.psum_tensor(f"psHd{k}", [P, 512], f32)) for k in range(2)]
            psO = st.enter_context(nc.psum_tensor("psOd", [P, 1024], f32))
            f_in = [sem(f"d_rows_loaded{b}") for b in range(U)]
            hb_done = sem("d_h0_plus_b2")
            tr_done = sem("d_transposed")
            hT_done = sem("d_h0T_copied")
            eT_done = sem("d_eT_copied")
            h_done = sem("d_hidden_product")
            a_done = sem("d_hidden_relu")
            o_done = sem("d_output_product")
            v_done = sem("d_residual_added")
            small = sem("d_small_steps")
            std_done = sem("d_std_ready")
            r1_done = sem("d_rstd_ready")
            r_done = sem("d_rstd_and_shift_ready")
            n_done = sem("d_out_ready")
            stored = [sem(f"d_out_stored{b}") for b in range(U)]
            with nc.Block() as block:
                @block.sync
                def _(sp):
                    def body(n, b, f, pr, rr):
                        wait(sp, tr_done, n - U + 1)
                        wait(sp, hb_done, n - U + 1)
                        hold(sp)
                        sp.dma_start(F[b][0:pr, 0:rr, :], rows_of(ye_tab, n, pr, rr, 0, YW)
                                     ).then_inc(f_in[b], 16)
                    blocks(sp, body)

                @block.gpsimd
                def _(pool):
                    def body(n, b, f, pr, rr):
                        pool.wait_ge(f_in[b], 16 * f)
                        wait(pool, v_done, n - U + 1)
                        c2r = c2_bc[0:pr, :].rearrange("p (o d) -> p o d", o=1).to_broadcast([pr, rr, D])
                        pool.tensor_tensor(hb[b][0:pr, 0:rr, :], F[b][0:pr, 0:rr, 0:D], c2r,
                                           ALU.add).then_inc(hb_done, 1)
                    blocks(pool, body)

                @block.tensor
                def _(pe):
                    def turn(n, b, f, pr, rr):
                        pe.wait_ge(f_in[b], 16 * f)
                        wait(pe, hT_done, n)
                        wait(pe, eT_done, n)
                        for j in range(rr):
                            pe.transpose(psT[:, j * P:j * P + pr], F[b][0:pr, j, 0:D], ident[0:pr, 0:pr])
                            last = pe.transpose(psE[0:DE, j * P:j * P + pr], F[b][0:pr, j, D:YW],
                                                ident[0:pr, 0:pr])
                        last.then_inc(tr_done, 1)

                    def hidden(n, b, f, pr, rr):
                        pe.wait_ge(hT_done, n + 1)
                        pe.wait_ge(eT_done, n + 1)
                        nc_ = pr * rr // (2 if rr > 1 else 1)
                        q = 0
                        for c in range(2 if rr > 1 else 1):
                            for k in range(2):
                                m = psH[k][:, 0:nc_]
                                wait(pe, a_done, 4 * n + q - 1)
                                cs = slice(c * nc_, (c + 1) * nc_)
                                pe.matmul(m, vx[:, k * P:(k + 1) * P], hT[:, cs], start=True, stop=False)
                                pe.matmul(m, ve[:, k * P:(k + 1) * P], eT[:, cs], start=False,
                                          stop=True).then_inc(h_done, 1)
                                q += 1

                    def outp(n, b, f, pr, rr):
                        pe.wait_ge(a_done, 4 * n + (4 if rr > 1 else 2))
                        wait(pe, v_done, n)
                        for j in range(rr):
                            for k in range(2):
                                last = pe.matmul(psO[0:pr, j * D:(j + 1) * D], aH[:, k, j * P:j * P + pr],
                                                 v2[:, k, :], start=(k == 0), stop=(k == 1))
                        last.then_inc(o_done, 1)

                    whole = (P, BR)
                    turn(0, 0, 1, *whole)
                    for b in range(U):
                        hidden(b, b, 1, *whole)
                        turn(b + 1, (b + 1) % U, 1 + (b + 1) // U, *whole)
                        outp(b, b, 1, *whole)
                    with pe.Fori(1, LOOPS - 1) as i:
                        for b in range(U):
                            hidden(i * U + b, b, i + 1, *whole)
                            turn(i * U + b + 1, (b + 1) % U, i + 1 + (b + 1) // U, *whole)
                            outp(i * U + b, b, i + 1, *whole)
                    i = LOOPS - 1
                    for b in range(U):
                        hidden(i * U + b, b, i + 1, *whole)
                        nxt = whole if b < U - 1 else (REST, 1)
                        turn(i * U + b + 1, (b + 1) % U, i + 1 + (b + 1) // U, *nxt)
                        outp(i * U + b, b, i + 1, *whole)
                    hidden(BLOCKS, 0, LOOPS + 1, REST, 1)
                    outp(BLOCKS, 0, LOOPS + 1, REST, 1)

                @block.scalar
                def _(act):
                    def front(n, b, f, pr, rr):
                        act.wait_ge(tr_done, n + 1)
                        wait(act, h_done, 4 * n)
                        act.activation(eT[:, 0:pr * rr], psE[0:DE, 0:pr * rr], ACT.Copy).then_inc(eT_done, 1)
                        nc_ = pr * rr // (2 if rr > 1 else 1)
                        q = 0
                        wait(act, o_done, n)
                        for c in range(2 if rr > 1 else 1):
                            for k in range(2):
                                act.wait_ge(h_done, 4 * n + q + 1)
                                act.activation(aH[:, k, c * nc_:(c + 1) * nc_], psH[k][:, 0:nc_], ACT.Relu,
                                               bias=bn_shift[:, k:k + 1], scale=bn_scale[:, k:k + 1]
                                               ).then_inc(a_done, 1)
                                q += 1

                    def back(n, b, f, pr, rr):
                        act.wait_ge(small, 3 * n + 3)
                        act.activation(var[0:pr, b, 0:rr], var[0:pr, b, 0:rr], ACT.Sqrt).then_inc(std_done, 1)
                        act.wait_ge(r_done, n + 1)
                        wait(act, stored[b], 16 * (f - 1))
                        for j in range(rr):
                            last = act.activation(o[b][0:pr, j, :], v[0:pr, b, j, :], ACT.Identity,
                                                  bias=nmr[0:pr, b, j:j + 1], scale=r[0:pr, b, j:j + 1])
                        last.then_inc(n_done, 1)
                        act.wait_ge(n_done, n + 1)
                        act.dma_start(rows_of(out, n, pr, rr, 0, D), o[b][0:pr, 0:rr, :]).then_inc(stored[b], 16)

                    whole = (P, BR)
                    front(0, 0, 1, *whole)
                    for b in range(1, U):
                        front(b, b, 1, *whole)
                        back(b - 1, b - 1, 1, *whole)
                    with act.Fori(1, LOOPS) as i:
                        for b in range(U):
                            front(i * U + b, b, i + 1, *whole)
                            back(i * U + b - 1, (b - 1) % U, i + (0 if b == 0 else 1), *whole)
                    front(BLOCKS, 0, LOOPS + 1, REST, 1)
                    back(BLOCKS - 1, U - 1, LOOPS, *whole)
                    back(BLOCKS, 0, LOOPS + 1, REST, 1)
                    for b in range(U):
                        act.wait_ge(stored[b], 16 * (LOOPS + (b == 0)))

                @block.vector
                def _(dve):
                    def front(n, b, f, pr, rr):
                        dve.wait_ge(tr_done, n + 1)
                        wait(dve, h_done, 4 * n)
                        dve.tensor_copy(hT[:, 0:pr * rr], psT[:, 0:pr * rr]).then_inc(hT_done, 1)

                    def back(n, b, f, pr, rr):
                        dve.wait_ge(o_done, n + 1)
                        dve.wait_ge(hb_done, n + 1)
                        wait(dve, n_done, n - U + 1)
                        dve.tensor_tensor(v[0:pr, b, 0:rr, :],
                                          psO[0:pr, 0:rr * D].rearrange("p (r d) -> p r d", d=D),
                                          hb[b][0:pr, 0:rr, :], ALU.add).then_inc(v_done, 1)
                        dve.wait_ge(v_done, n + 1)
                        for j in range(rr):
                            last = dve.bn_stats(st6[0:pr, b, j, :], v[0:pr, b, j, :])
                        last.then_inc(small, 1)
                        dve.wait_ge(small, 3 * n + 1)
                        hold(dve)
                        for j in range(rr):
                            last = dve.bn_aggr(mv[0:pr, b, j, :], st6[0:pr, b, j, :])
                        last.then_inc(small, 1)
                        dve.wait_ge(small, 3 * n + 2)
                        dve.tensor_scalar(var[0:pr, b, 0:rr], mv[0:pr, b, 0:rr, 1], EPS, None,
                                          ALU.add).then_inc(small, 1)
                        dve.wait_ge(std_done, n + 1)
                        dve.reciprocal(r[0:pr, b, 0:rr], var[0:pr, b, 0:rr]).then_inc(r1_done, 1)
                        dve.wait_ge(r1_done, n + 1)
                        dve.scalar_tensor_tensor(nmr[0:pr, b, 0:rr], mv[0:pr, b, 0:rr, 0], -1.0,
                                                 r[0:pr, b, 0:rr], ALU.mult, ALU.mult).then_inc(r_done, 1)

                    whole = (P, BR)
                    front(0, 0, 1, *whole)
                    for b in range(1, U):
                        front(b, b, 1, *whole)
                        back(b - 1, b - 1, 1, *whole)
                    with dve.Fori(1, LOOPS) as i:
                        for b in range(U):
                            front(i * U + b, b, i + 1, *whole)
                            back(i * U + b - 1, (b - 1) % U, i + (0 if b == 0 else 1), *whole)
                    front(BLOCKS, 0, LOOPS + 1, REST, 1)
                    back(BLOCKS - 1, U - 1, LOOPS, *whole)
                    back(BLOCKS, 0, LOOPS + 1, REST, 1)


_NAMES = ['x', 'src', 'dst', 'edge_attr_96', 'L0_gnn_W1', 'L0_gnn_b1', 'L0_gnn_g1', 'L0_gnn_be1', 'L0_gnn_W2',
          'L0_gnn_b2', 'L0_gnn_g2', 'L0_gnn_be2', 'L0_gnn_Wo', 'L0_gnn_bo', 'L1_gnn_u', 'L1_gnn_W1', 'L1_gnn_b1',
          'L1_gnn_gamma', 'L1_gnn_beta', 'L1_gnn_W2', 'L1_gnn_b2']


def kernel(**inputs):
    import numpy as _np
    import concourse.bacc as _bacc
    from concourse import mybir as _mybir
    from concourse.bass_utils import run_bass_kernel_spmd as _run

    nc = _bacc.Bacc("TRN2", target_bir_lowering=False, num_devices=1)
    arrays, args = {}, []
    for name in _NAMES:
        a = _np.ascontiguousarray(inputs[name])
        arrays[f"in_{name}"] = a
        args.append(nc.dram_tensor(f"in_{name}", a.shape, _mybir.dt.from_np(a.dtype), kind="ExternalInput").ap())
    shape = arrays["in_x"].shape
    args.append(nc.dram_tensor("out_0", shape, _mybir.dt.float32, kind="ExternalOutput").ap())
    build_gnn(nc, *args)
    r = _run(nc, [arrays], core_ids=[0])
    return r.results[0]["out_0"]
```

```python
import concourse.bass as bass
from concourse import mybir
from contextlib import ExitStack


def wait(eng, sem, value):
    if isinstance(value, int) and value <= 0:
        return
    eng.wait_ge(sem, value)


NB = 4


def unit(n, nb=NB):
    return n, n % nb, n // nb + 1


def shift(t, d, nb=NB):
    n, b, f = t
    return n + d, (b + d) % nb, f + (b + d) // nb


def pipeline(eng, total, body, nb=NB):
    loops = total // nb
    for n in range(nb):
        body(unit(n, nb))
    with eng.Fori(1, loops - 1) as i:
        for b in range(nb):
            body((i * nb + b, b, i + 1))
    for n in range((loops - 1) * nb, total):
        body(unit(n, nb))


def staged(total, stage, t, d, nb=NB):
    n = t[0]
    if not isinstance(n, int) or 0 <= n + d < total:
        stage(*shift(t, d, nb))


def build_gnn(nc, x, src, dst, ea, W1, b1, g1, be1, W2, b2, g2, be2, Wo, bo,
              u, V1, c1, gamma, beta, V2, c2, out):
    f32, i32 = mybir.dt.float32, mybir.dt.int32
    ALU = mybir.AluOpType
    ACT = mybir.ActivationFunctionType

    P = 128
    N, D = x.shape
    E, DE = ea.shape
    H = V1.shape[1]
    DU = u.shape[1]
    EPS = 1e-5

    TG = 4
    GE = TG * P
    GROUPS = -(-E // GE)
    EP = GROUPS * GE
    TILES = GROUPS * TG
    TQ = TILES // 2
    SKIP = 60000
    FILL_A, FILL_R = 23, 17
    NT = P * FILL_R * FILL_A
    assert NT >= N and E < EP and TILES % 2 == 0 and (EP - E) * DE % P == 0
    YW = D + DE

    BR = 5
    BLK = P * BR
    BLOCKS = N // BLK
    REST = N - BLOCKS * BLK
    UNITS = BLOCKS + 1
    assert 0 < REST <= P

    src_s = nc.dram_tensor("src_sorted", [EP], i32).ap()
    dst_s = nc.dram_tensor("dst_sorted", [EP + 2], i32).ap()
    ea_s = nc.dram_tensor("edge_attr_sorted", [EP, DE], f32).ap()
    x1_tab = nc.dram_tensor("x1_by_node", [NT, D], f32).ap()
    x1_slot = nc.dram_tensor("x1_by_slot", [GROUPS, P, TG * D], f32).ap()
    ye_tab = nc.dram_tensor("y_e_by_node", [NT, YW], f32).ap()

    def bc(a, p, n):
        return a.rearrange("p (o d) -> p o d", o=1).to_broadcast([p, n, a.shape[1]])

    ctx = ExitStack()
    with ctx:
        def sb(name, shape, dt=f32):
            return ctx.enter_context(nc.sbuf_tensor(name, shape, dt))

        def sem(name):
            return ctx.enter_context(nc.semaphore(name))

        def sems(name, nb=NB):
            return [sem(f"{name}{b}") for b in range(nb)]

        ident = sb("ident", [P, P])
        ones = sb("ones", [P, 1])
        w1 = sb("w1", [P, D])
        w2 = sb("w2", [P, D])
        wo = sb("wo", [P, D])
        b1_row = sb("b1_row", [1, D])
        g1_bc = sb("g1_bc", [P, D])
        be1_bc = sb("be1_bc", [P, D])
        b2_bc = sb("b2_bc", [P, D])
        bo_bc = sb("bo_bc", [P, D])
        c2_bc = sb("c2_bc", [P, D])
        g2_col = sb("g2_col", [P, 1])
        be2_col = sb("be2_col", [P, 1])
        vx = sb("vx", [P, H])
        ve = sb("ve", [DE, H])
        vu = sb("vu", [DU, H])
        v2 = sb("v2", [P, 2, D])
        u_col = sb("u_col", [DU, 1])
        c1_col = sb("c1_col", [P, 2])
        gamma_col = sb("gamma_col", [P, 2])
        beta_col = sb("beta_col", [P, 2])
        src_idx = sb("src_idx", [P, TILES], i32)
        put_idx = sb("put_idx", [P, TILES], i32)
        dst_col = sb("dst_col", [P, TILES], i32)
        rdeg = sb("rdeg", [P, TILES])

        turns = sem("turns")

        def hold(eng):
            eng.sem_inc(turns, 1)

        x1_filled = sem("x1_table_filled")
        ye_filled = sem("ye_table_filled")
        ea_copied = sem("edge_attr_copied")
        fills = ExitStack()
        fill_x1 = fills.enter_context(nc.sbuf_tensor("fill_x1", [P, FILL_R, D], f32))
        fill_ye = fills.enter_context(nc.sbuf_tensor("fill_ye", [P, FILL_R, YW], f32))
        pad_ea = fills.enter_context(nc.sbuf_tensor("pad_ea", [P, (EP - E) * DE // P], f32))

        with ExitStack() as st:
            def tb(name, shape, dt=f32):
                return st.enter_context(nc.sbuf_tensor(name, shape, dt))

            def ps(name):
                return st.enter_context(nc.psum_tensor(name, [P, 512], f32))
            pad_src = tb("pad_src", [1, EP - E], i32)
            pad_dst = tb("pad_dst", [1, EP - E + 1], i32)
            pad_front = tb("pad_front", [1, 1], i32)
            src_t = tb("src_t", [TQ, 2 * P], i32)
            dst_t = tb("dst_t", [TQ, 2 * P], i32)
            nxt_t = tb("nxt_t", [TQ, 2 * P], i32)
            src_f = tb("src_f", [TQ, 2 * P])
            dst_f = tb("dst_f", [TQ, 2 * P])
            put_f = tb("put_f", [TQ, 2 * P])
            same = tb("same", [TQ, 2 * P])
            x1c = tb("x1c", [P, D])
            yc = tb("yc", [P, D])
            x2n = tb("x2n", [P, D])
            x2t = tb("x2t", [P, D])
            st6 = tb("st6", [P, 6])
            mv = tb("mv", [P, 2])
            rs = tb("rs", [P, 1])
            ps_i = [ps(f"ps_i{k}") for k in range(6)]
            ps_t = ps("ps_t")
            ps_y = ps("ps_y")

            be1_in = sem("be1_loaded")
            loaded = sem("weights_loaded")
            zeroed = sem("ident_zeroed")
            ident_ok = sem("ident_ready")
            pads_ok = sem("pads_ready")
            copied = sem("edges_copied")
            idx_loaded = sem("indices_loaded")
            idx_f = sem("indices_float")
            idx_t = sem("indices_transposed")
            v_step = sem("prologue_vector_steps")
            c_var = sem("const_row_variance")
            c_std = sem("const_row_std")
            c_norm = sem("const_row_normed")
            c_tr = sem("const_row_transposed")
            c_act = sem("const_row_relu")
            c_y = sem("const_row_y")
            c_x1 = sem("const_fill_x1")
            line = lambda a: a.rearrange("(o n) -> o n", o=1)
            col = lambda a: a.rearrange("(p o) -> p o", o=1)
            bcast = lambda a: line(a).to_broadcast([P, D])
            weights = [
                (wo[:, :], Wo), (bo_bc[:, :], bcast(bo)), (g2_col[:, :], col(g2)), (be2_col[:, :], col(be2)),
                (w1[:, :], W1), (w2[:, :], W2), (b1_row[:, :], line(b1)), (g1_bc[:, :], bcast(g1)),
                (b2_bc[:, :], bcast(b2)), (c2_bc[:, :], bcast(c2)),
                (vx[:, :], V1[0:D, :]), (ve[:, :], V1[D:D + DE, :]), (vu[:, :], V1[D + DE:, :]),
                (v2[:, :, :], V2.rearrange("(k p) d -> p k d", p=P)),
                (u_col[:, :], u[0:1, :].rearrange("o d -> d o")),
                (c1_col[:, :], c1.rearrange("(k p) -> p k", p=P)),
                (gamma_col[:, :], gamma.rearrange("(k p) -> p k", p=P)),
                (beta_col[:, :], beta.rearrange("(k p) -> p k", p=P)),
            ]

            with nc.Block() as block:
                @block.sync
                def _(sp):
                    sp.dma_start(be1_bc[:, :], bcast(be1)).then_inc(be1_in, 16)
                    with nc.allow_non_contiguous_dma(reason="small columns"):
                        for to, frm in weights:
                            sp.dma_start(to, frm).then_inc(loaded, 16)
                    sp.wait_ge(c_x1, 1)
                    for a in range(FILL_A):
                        sp.dma_start(x1_tab.rearrange("(a p r) d -> a p (r d)", p=P, r=FILL_R)[a, :, :],
                                     fill_x1[:, :, :].rearrange("p r d -> p (r d)")).then_inc(x1_filled, 16)
                    sp.wait_ge(loaded, 16 * len(weights))

                @block.gpsimd
                def _(pool):
                    pool.memset(pad_src[:, :], 0)
                    pool.memset(pad_dst[:, :], N)
                    pool.memset(pad_front[:, :], -1)
                    pool.memset(pad_ea[:, :], 0.0).then_inc(pads_ok, 1)
                    pool.memset(ident[:, :], 0.0).then_inc(zeroed, 1)
                    pool.memset(ones[:, :], 1.0)
                    pool.wait_ge(zeroed, 1)
                    pool.affine_select(out=ident[:, :], in_=ident[:, :], compare_op=ALU.not_equal, fill=1.0,
                                       base=0, pattern=[[-1, P]], channel_multiplier=1).then_inc(ident_ok, 1)

                @block.scalar
                def _(act):
                    act.dma_start(src_s[0:E], src).then_inc(copied, 16)
                    act.dma_start(dst_s[1:E + 1], dst).then_inc(copied, 16)
                    act.wait_ge(pads_ok, 1)
                    act.dma_start(line(src_s[E:EP]), pad_src[:, :]).then_inc(copied, 16)
                    act.dma_start(line(dst_s[E + 1:EP + 2]), pad_dst[:, :]).then_inc(copied, 16)
                    act.dma_start(line(dst_s[0:1]), pad_front[:, :]).then_inc(copied, 16)
                    act.wait_ge(copied, 16 * 5)
                    rows = lambda a: a.rearrange("(q n) -> q n", n=2 * P)
                    act.dma_start(src_t[:, :], rows(src_s)).then_inc(idx_loaded, 16)
                    act.dma_start(dst_t[:, :], rows(dst_s[1:EP + 1])).then_inc(idx_loaded, 16)
                    act.dma_start(nxt_t[:, :], rows(dst_s[2:EP + 2])).then_inc(idx_loaded, 16)
                    act.wait_ge(c_var, 1)
                    act.activation(rs[:, :], rs[:, :], ACT.Sqrt).then_inc(c_std, 1)
                    act.wait_ge(c_tr, 1)
                    act.activation(x2t[:, :], ps_t[:, 0:D], ACT.Relu, bias=be2_col[:, :],
                                   scale=g2_col[:, :]).then_inc(c_act, 1)
                    act.dma_start(ea_s[0:E, :], ea).then_inc(ea_copied, 16)
                    act.dma_start(ea_s[E:EP, :].rearrange("r d -> (r d)").rearrange("(p n) -> p n", p=P),
                                  pad_ea[:, :]).then_inc(ea_copied, 16)

                @block.tensor
                def _(pe):
                    pe.wait_ge(ident_ok, 1)
                    pe.wait_ge(c_norm, 1)
                    pe.transpose(ps_t[:, 0:D], x2n[:, :], ident[:, :]).then_inc(c_tr, 1)
                    pe.wait_ge(c_act, 1)
                    pe.matmul(ps_y[:, 0:D], x2t[:, :], wo[:, :], start=True, stop=True).then_inc(c_y, 1)
                    pe.wait_ge(idx_f, 1)
                    for k, t in enumerate((src_f, dst_f, put_f)):
                        for j in range(2):
                            last = pe.transpose(ps_i[2 * k + j][:, 0:TQ], t[:, j * P:(j + 1) * P],
                                                ident[0:TQ, 0:TQ])
                    last.then_inc(idx_t, 1)

                @block.vector
                def _(dve):
                    done = [0]

                    def step(ins):
                        done[0] += 1
                        ins.then_inc(v_step, 1)
                        dve.wait_ge(v_step, done[0])

                    dve.wait_ge(be1_in, 16)
                    step(dve.tensor_scalar(x1c[:, :], be1_bc[:, :], 0.0, None, ALU.max))
                    dve.tensor_copy(fill_x1[:, :, :], bc(x1c[:, :], P, FILL_R)).then_inc(c_x1, 1)
                    step(dve.bn_stats(st6[:, :], x1c[:, :]))
                    step(dve.bn_aggr(mv[:, :], st6[:, :]))
                    dve.tensor_scalar(rs[:, :], mv[:, 1:2], EPS, None, ALU.add).then_inc(c_var, 1)
                    dve.memset(fill_ye[:, :, D:YW], 0.0)
                    dve.wait_ge(loaded, 16 * len(weights))
                    dve.wait_ge(c_std, 1)
                    step(dve.reciprocal(rs[:, :], rs[:, :]))
                    dve.tensor_scalar(x2n[:, :], x1c[:, :], mv[:, 0:1], rs[:, :], ALU.subtract,
                                      ALU.mult).then_inc(c_norm, 1)
                    dve.wait_ge(c_y, 1)
                    step(dve.tensor_tensor(yc[:, :], ps_y[:, 0:D], bo_bc[:, :], ALU.add))
                    dve.tensor_copy(fill_ye[:, :, 0:D], bc(yc[:, :], P, FILL_R))
                    dve.wait_ge(idx_loaded, 16 * 3)
                    dve.tensor_copy(src_f[:, :], src_t[:, :])
                    dve.tensor_copy(dst_f[:, :], dst_t[:, :])
                    step(dve.tensor_tensor(same[:, :], dst_t[:, :], nxt_t[:, :], ALU.is_equal))
                    dve.scalar_tensor_tensor(put_f[:, :], same[:, :], float(SKIP), dst_f[:, :], ALU.mult,
                                             ALU.add).then_inc(idx_f, 1)
                    dve.wait_ge(idx_t, 1)
                    for k, t in enumerate((src_idx, dst_col, put_idx)):
                        for j in range(2):
                            dve.tensor_copy(t[:, j:TILES:2], ps_i[2 * k + j][:, 0:TQ])

        def load_rows(eng, drow, row_in, match, n, b, f):
            wait(eng, match, n - NB + 1)
            hold(eng)
            eng.dma_start(drow[b][:, :], dst_s[bass.ds(n * GE, GE + 1)].rearrange("(o n) -> o n", o=1)
                          .to_broadcast([P, GE + 1])).then_inc(row_in[b], 16)

        def matches(dve, drow, row_in, S, Q, summed, carried, match, n, b, f):
            dve.wait_ge(row_in[b], 16 * f)
            wait(dve, summed, n - NB + 1)
            for c in carried:
                wait(dve, c, TG * (n - NB + 1))
            cur = drow[b][:, 1:1 + GE].rearrange("p (t n) -> p t n", n=P)
            own = dst_col[:, bass.ds(n * TG, TG)].rearrange("p (t o) -> p t o", o=1)
            before = drow[b][:, 0:GE:P].rearrange("p (t o) -> p t o", o=1)
            dve.tensor_tensor(S[b][:, :, :], cur, own.to_broadcast([P, TG, P]), ALU.is_equal)
            dve.tensor_tensor(Q[b][:, :, :], cur, before.to_broadcast([P, TG, P]),
                              ALU.is_equal).then_inc(match, 1)

        def carry(dve, sums, Q, psum, done, parts, n, b):
            def tile(j):
                prev = sums[b][0:parts, j - 1, P - 1:P] if j else sums[b - 1][0:parts, TG - 1, P - 1:P]
                wait(dve, done, TG * n + j)
                dve.scalar_tensor_tensor(sums[b][0:parts, j, :], Q[b][0:parts, j, :], prev,
                                         psum[0:parts, j * P:(j + 1) * P], ALU.mult, ALU.add
                                         ).then_inc(done, 1)
            return tile

        def gather(pool, table, idx, idx_copied, rows, gat, summed, n, b, f):
            wait(pool, gat[b], 64 * (f - 1))
            pool.tensor_copy(idx[b][:, :], src_idx[:, bass.ds(n * TG, TG)]).then_inc(idx_copied, 1)
            wait(pool, summed, n - NB + 1)
            pool.wait_ge(idx_copied, n + 1)
            hold(pool)
            for j in range(TG):
                pool.indirect_dma_start(rows[b][:, j, :], None, table,
                                        bass.IndirectOffsetOnAxis(ap=idx[b][:, j:j + 1], axis=0),
                                        bounds_check=N - 1, oob_is_err=False).then_inc(gat[b], 16)

        def scatter(pool, table, idx, idx_copied, rows, put, ready, filled, n, b, f):
            wait(pool, put[b], 64 * (f - 1))
            pool.tensor_copy(idx[b][:, :], put_idx[:, bass.ds(n * TG, TG)]).then_inc(idx_copied, 1)
            pool.wait_ge(filled, 16 * FILL_A)
            for r in ready:
                pool.wait_ge(r, n + 1)
            pool.wait_ge(idx_copied, n + 1)
            hold(pool)
            for j in range(TG):
                pool.indirect_dma_start(table, bass.IndirectOffsetOnAxis(ap=idx[b][:, j:j + 1], axis=0),
                                        rows[b][:, j, :], None, bounds_check=N - 1,
                                        oob_is_err=False).then_inc(put[b], 16)

        last_b, last_f = (GROUPS - 1) % NB, (GROUPS - 1) // NB + 1
        fills_of = lambda b: last_f if b <= last_b else last_f - 1

        with ExitStack() as st:
            def tb(name, shape, dt=f32):
                return [st.enter_context(nc.sbuf_tensor(f"{name}_a{b}", shape, dt)) for b in range(NB)]

            def ps(name):
                return [st.enter_context(nc.psum_tensor(f"{name}_a{b}", [P, 512], f32)) for b in range(2)]
            idx = tb("idx", [P, TG], i32)
            pidx = tb("pidx", [P, TG], i32)
            xg = tb("xg", [P, TG, D])
            drow = tb("drow", [P, GE + 1], i32)
            S = tb("S", [P, TG, P])
            Q = tb("Q", [P, TG, P])
            aT = tb("aT", [P, TG, P])
            degr = tb("degr", [1, TG, P])
            degc = tb("degc", [P, TG])
            de2 = tb("de2", [P, TG])
            st6 = tb("st6", [P, TG, 6])
            mv = tb("mv", [P, TG, 2])
            var = tb("var", [P, TG])
            r = tb("r", [P, TG])
            nmr = tb("nmr", [P, TG])
            z = tb("z", [P, TG, D])
            x1 = tb("x1", [P, TG, D])
            x1b = tb("x1b", [P, TG, D])
            psA, psR, psZ, psC = ps("psA"), ps("psR"), ps("psZ"), ps("psC")

            row_in = sems("a_dst_row_loaded")
            gat = sems("a_rows_gathered")
            put = sems("a_x1_scattered")
            kept = sems("a_x1_slot_stored")
            idx_copied = sem("a_idx_copied")
            pidx_copied = sem("a_put_idx_copied")
            match = sem("a_match_ready")
            summed = sem("a_tile_sums_ready")
            aT_done = sem("a_sums_with_carry")
            dg_done = sem("a_degrees_with_carry")
            z_done = sem("a_product_ready")
            deg_out = sem("a_degree_column")
            small = sem("a_small_steps")
            std_done = sem("a_std_ready")
            r1_done = sem("a_rstd_ready")
            r_done = sem("a_rstd_and_shift_ready")
            n_done = sem("a_normed")
            zg = sem("a_scaled")
            zb = sem("a_shifted")
            x1_done = sem("a_x1_ready")
            x1b_done = sem("a_x1_plus_b2_ready")
            primed = sem("a_carry_zeroed")
            SMALL = 4

            with nc.Block() as block:
                @block.sync
                def _(sp):
                    def rows(n, b, f):
                        load_rows(sp, drow, row_in, match, n, b, f)

                    def store(n, b, f):
                        sp.wait_ge(x1b_done, n + 1)
                        hold(sp)
                        sp.dma_start(x1_slot[bass.ds(n, 1), :, :].rearrange("o p n -> (o p) n"),
                                     x1b[b][:, :, :].rearrange("p t d -> p (t d)")).then_inc(kept[b], 16)

                    def fill(n, b, f):
                        if b % 2 == 0 and not (isinstance(n, int) and n // 2 >= FILL_A):
                            chunk = ye_tab.rearrange("(a q) d -> a (q d)", a=FILL_A)
                            sp.dma_start(chunk[bass.ds((f - 1) * (NB // 2) + b // 2, 1), :]
                                         .rearrange("o (p m) -> (o p) m", p=P),
                                         fill_ye[:, :, :].rearrange("p r d -> p (r d)")).then_inc(ye_filled, 16)

                    def body(t):
                        staged(GROUPS, rows, t, 3)
                        fill(*t)
                        staged(GROUPS, store, t, -1)
                    assert GROUPS // 2 + 1 >= FILL_A
                    for n in range(3):
                        rows(*unit(n))
                    pipeline(sp, GROUPS, body)
                    store(*unit(GROUPS - 1))
                    for b in range(NB):
                        sp.wait_ge(kept[b], 16 * fills_of(b))

                @block.gpsimd
                def _(pool):
                    def get(n, b, f):
                        gather(pool, x[:, :], idx, idx_copied, xg, gat, summed, n, b, f)

                    def save(n, b, f):
                        scatter(pool, x1_tab[:, :], pidx, pidx_copied, x1, put, [x1_done], x1_filled, n, b, f)

                    def body(t):
                        staged(GROUPS, get, t, 3)
                        staged(GROUPS, save, t, -1)
                    for n in range(3):
                        get(*unit(n))
                    pipeline(pool, GROUPS, body)
                    save(*unit(GROUPS - 1))
                    for b in range(NB):
                        pool.wait_ge(put[b], 64 * fills_of(b))

                @block.tensor
                def _(pe):
                    def sums(n, b, f):
                        pe.wait_ge(match, n + 1)
                        pe.wait_ge(gat[b], 64 * f)
                        wait(pe, aT_done, TG * (n - 1))
                        wait(pe, dg_done, TG * (n - 1))
                        for j in range(TG):
                            pe.matmul(psA[b % 2][:, j * P:(j + 1) * P], xg[b][:, j, :], S[b][:, j, :],
                                      start=True, stop=True)
                        pe.matmul(psR[b % 2][0:1, :], ones[:, :], S[b][:, :, :].rearrange("p t n -> p (t n)"),
                                  start=True, stop=True).then_inc(summed, 1)

                    def product(n, b, f):
                        pe.wait_ge(aT_done, TG * (n + 1))
                        pe.wait_ge(dg_done, TG * (n + 1))
                        wait(pe, n_done, n - 1)
                        wait(pe, deg_out, n - 1)
                        for j in range(TG):
                            o = psZ[b % 2][:, j * D:(j + 1) * D]
                            pe.matmul(o, aT[b][:, j, :], w1[:, :], start=True, stop=False)
                            pe.matmul(o, degr[b][:, j, :], b1_row[:, :], start=False, stop=True)
                            last = pe.matmul(psC[b % 2][:, j:j + 1], degr[b][:, j, :], ones[0:1, :],
                                             start=True, stop=True)
                        last.then_inc(z_done, 1)

                    def body(t):
                        staged(GROUPS, sums, t, 1)
                        product(*t)
                    sums(*unit(0))
                    pipeline(pe, GROUPS, body)

                @block.scalar
                def _(act):
                    def norm(n, b, f):
                        act.wait_ge(r_done, n + 1)
                        wait(act, x1_done, n - NB + 1)
                        for j in range(TG):
                            last = act.activation(z[b][:, j, :], psZ[b % 2][:, j * D:(j + 1) * D], ACT.Identity,
                                                  bias=nmr[b][:, j:j + 1], scale=r[b][:, j:j + 1])
                        last.then_inc(n_done, 1)

                    def relu(n, b, f):
                        wait(act, put[b], 64 * (f - 1))
                        act.wait_ge(zb, n + 1)
                        wait(act, x1b_done, n - NB + 1)
                        act.activation(x1[b][:, :, :], z[b][:, :, :], ACT.Relu).then_inc(x1_done, 1)

                    def root(n, b, f):
                        act.wait_ge(small, SMALL * (n + 1))
                        act.activation(var[b][:, :], var[b][:, :], ACT.Sqrt).then_inc(std_done, 1)

                    def body(t):
                        staged(GROUPS, norm, t, -1)
                        staged(GROUPS, relu, t, -1)
                        root(*t)
                    pipeline(act, GROUPS, body)
                    norm(*unit(GROUPS - 1))
                    relu(*unit(GROUPS - 1))

                @block.vector
                def _(dve):
                    dve.memset(aT[NB - 1][:, TG - 1, :], 0.0)
                    dve.memset(degr[NB - 1][:, TG - 1, :], 0.0).then_inc(primed, 1)
                    dve.wait_ge(primed, 1)

                    def match_up(n, b, f):
                        matches(dve, drow, row_in, S, Q, summed, [aT_done, dg_done], match, n, b, f)

                    def chain(n, b, f):
                        dve.wait_ge(match, n + 1)
                        dve.wait_ge(summed, n + 1)
                        wait(dve, z_done, n - NB + 1)
                        a = carry(dve, aT, Q, psA[b % 2], aT_done, P, n, b)
                        d = carry(dve, degr, Q, psR[b % 2], dg_done, 1, n, b)
                        for j in range(TG):
                            a(j)
                            d(j)

                    def affine(n, b, f):
                        dve.wait_ge(n_done, n + 1)
                        dve.tensor_tensor(z[b][:, :, :], z[b][:, :, :], bc(g1_bc[:, :], P, TG),
                                          ALU.mult).then_inc(zg, 1)
                        dve.wait_ge(zg, n + 1)
                        dve.tensor_tensor(z[b][:, :, :], z[b][:, :, :], bc(be1_bc[:, :], P, TG),
                                          ALU.add).then_inc(zb, 1)

                    def moments(n, b, f):
                        dve.wait_ge(z_done, n + 1)
                        dve.tensor_copy(degc[b][:, :], psC[b % 2][:, 0:TG]).then_inc(deg_out, 1)
                        for j in range(TG):
                            last = dve.bn_stats(st6[b][:, j, :], psZ[b % 2][:, j * D:(j + 1) * D])
                        last.then_inc(small, 1)
                        dve.wait_ge(small, SMALL * n + 1)
                        dve.wait_ge(deg_out, n + 1)
                        dve.reciprocal(rdeg[:, bass.ds(n * TG, TG)], degc[b][:, :])
                        dve.scalar_tensor_tensor(de2[b][:, :], degc[b][:, :], EPS, degc[b][:, :], ALU.mult,
                                                 ALU.mult).then_inc(small, 1)
                        for j in range(TG):
                            last = dve.bn_aggr(mv[b][:, j, :], st6[b][:, j, :])
                        last.then_inc(small, 1)
                        dve.wait_ge(small, SMALL * n + 3)
                        dve.tensor_tensor(var[b][:, :], mv[b][:, :, 1], de2[b][:, :], ALU.add).then_inc(small, 1)

                    def plus_b2(n, b, f):
                        dve.wait_ge(x1_done, n + 1)
                        wait(dve, kept[b], 16 * (f - 1))
                        dve.tensor_tensor(x1b[b][:, :, :], x1[b][:, :, :], bc(b2_bc[:, :], P, TG),
                                          ALU.add).then_inc(x1b_done, 1)

                    def rstd(n, b, f):
                        dve.wait_ge(std_done, n + 1)
                        dve.reciprocal(r[b][:, :], var[b][:, :]).then_inc(r1_done, 1)
                        dve.wait_ge(r1_done, n + 1)
                        dve.scalar_tensor_tensor(nmr[b][:, :], mv[b][:, :, 0], -1.0, r[b][:, :], ALU.mult,
                                                 ALU.mult).then_inc(r_done, 1)

                    def body(t):
                        chain(*t)
                        staged(GROUPS, affine, t, -1)
                        staged(GROUPS, match_up, t, 2)
                        moments(*t)
                        staged(GROUPS, plus_b2, t, -1)
                        rstd(*t)
                    match_up(*unit(0))
                    match_up(*unit(1))
                    pipeline(dve, GROUPS, body)
                    affine(*unit(GROUPS - 1))
                    plus_b2(*unit(GROUPS - 1))

        with ExitStack() as st:
            def tb(name, shape, dt=f32):
                return [st.enter_context(nc.sbuf_tensor(f"{name}_b{b}", shape, dt)) for b in range(NB)]

            def ps(name, n=1):
                return [st.enter_context(nc.psum_tensor(f"{name}_b{b}", [P, 512], f32)) for b in range(n)]
            idx = tb("idx", [P, TG], i32)
            pidx = tb("pidx", [P, TG], i32)
            xg = tb("xg", [P, TG, D])
            eg = tb("eg", [P, TG, DE])
            x1r = tb("x1r", [P, TG, D])
            drow = tb("drow", [P, GE + 1], i32)
            S = tb("S", [P, TG, P])
            Q = tb("Q", [P, TG, P])
            aT = tb("aT", [P, TG, P])
            eT = tb("eT", [DE, TG, P])
            st6 = tb("st6", [P, TG, 6])
            mv = tb("mv", [P, TG, 2])
            var = tb("var", [P, TG])
            r = tb("r", [P, TG])
            nmr = tb("nmr", [P, TG])
            v = tb("v", [P, TG, D])
            n2 = tb("n2", [P, TG, D])
            x2T = tb("x2T", [P, TG, P])
            ye = tb("ye", [P, TG, YW])
            psA, psE = ps("psA", 2), ps("psE", 2)
            psZ, psT, psX, psY = ps("psZ")[0], ps("psT")[0], ps("psX")[0], ps("psY")[0]

            row_in = sems("b_dst_row_loaded")
            e_in = sems("b_edge_attr_loaded")
            x1_in = sems("b_x1_loaded")
            gat = sems("b_x1_gathered")
            put = sems("b_rows_scattered")
            idx_copied = sem("b_idx_copied")
            pidx_copied = sem("b_put_idx_copied")
            match = sem("b_match_ready")
            summed = sem("b_tile_sums_ready")
            aT_done = sem("b_sums_with_carry")
            eT_done = sem("b_edge_sums_with_carry")
            z_done = sem("b_product_ready")
            et_done = sem("b_edge_sums_transposed")
            v_done = sem("b_residual_added")
            small = sem("b_small_steps")
            std_done = sem("b_std_ready")
            r1_done = sem("b_rstd_ready")
            r_done = sem("b_rstd_and_shift_ready")
            n_done = sem("b_normed")
            nt_done = sem("b_normed_transposed")
            x2_done = sem("b_x2_ready")
            y_done = sem("b_y_product_ready")
            ye_y = sem("b_row_y_part_ready")
            ye_e = sem("b_row_edge_part_ready")
            primed = sem("b_carry_zeroed")

            with nc.Block() as block:
                @block.sync
                def _(sp):
                    sp.wait_ge(ea_copied, 16 * 2)

                    def loads(n, b, f):
                        load_rows(sp, drow, row_in, match, n, b, f)
                        wait(sp, summed, n - NB + 1)
                        wait(sp, v_done, n - NB + 1)
                        hold(sp)
                        sp.dma_start(eg[b][:, :, :], ea_s[bass.ds(n * GE, GE), :]
                                     .rearrange("(t p) c -> p t c", p=P)).then_inc(e_in[b], 16)
                        sp.dma_start(x1r[b][:, :, :].rearrange("p t d -> p (t d)"),
                                     x1_slot[bass.ds(n, 1), :, :].rearrange("o p n -> (o p) n")
                                     ).then_inc(x1_in[b], 16)
                    for n in range(3):
                        loads(*unit(n))
                    pipeline(sp, GROUPS, lambda t: staged(GROUPS, loads, t, 3))

                @block.gpsimd
                def _(pool):
                    def get(n, b, f):
                        gather(pool, x1_tab[:, :], idx, idx_copied, xg, gat, summed, n, b, f)

                    def save(n, b, f):
                        scatter(pool, ye_tab[:, :], pidx, pidx_copied, ye, put, [ye_e, ye_y], ye_filled, n, b, f)

                    def body(t):
                        staged(GROUPS, get, t, 3)
                        staged(GROUPS, save, t, -1)
                    for n in range(3):
                        get(*unit(n))
                    pipeline(pool, GROUPS, body)
                    save(*unit(GROUPS - 1))
                    for b in range(NB):
                        pool.wait_ge(put[b], 64 * fills_of(b))

                @block.tensor
                def _(pe):
                    def sums(n, b, f):
                        pe.wait_ge(match, n + 1)
                        pe.wait_ge(e_in[b], 16 * f)
                        pe.wait_ge(gat[b], 64 * f)
                        wait(pe, aT_done, TG * (n - 1))
                        wait(pe, eT_done, TG * (n - 1))
                        for j in range(TG):
                            pe.matmul(psA[b % 2][:, j * P:(j + 1) * P], xg[b][:, j, :], S[b][:, j, :],
                                      start=True, stop=True)
                            last = pe.matmul(psE[b % 2][0:DE, j * P:(j + 1) * P], eg[b][:, j, :], S[b][:, j, :],
                                             start=True, stop=True)
                        last.then_inc(summed, 1)

                    def product(n, b, f):
                        pe.wait_ge(aT_done, TG * (n + 1))
                        wait(pe, v_done, n)
                        for j in range(TG):
                            last = pe.matmul(psZ[:, j * D:(j + 1) * D], aT[b][:, j, :], w2[:, :],
                                             start=True, stop=True)
                        last.then_inc(z_done, 1)
                        pe.wait_ge(eT_done, TG * (n + 1))
                        wait(pe, ye_e, n)
                        for j in range(TG):
                            last = pe.transpose(psT[:, j * DE:(j + 1) * DE], eT[b][:, j, :], ident[0:DE, 0:DE])
                        last.then_inc(et_done, 1)

                    def turn(n, b, f):
                        pe.wait_ge(n_done, n + 1)
                        wait(pe, x2_done, n)
                        for j in range(TG):
                            last = pe.transpose(psX[:, j * P:(j + 1) * P], n2[b][:, j, :], ident[:, :])
                        last.then_inc(nt_done, 1)

                    def outp(n, b, f):
                        pe.wait_ge(x2_done, n + 1)
                        wait(pe, ye_y, n)
                        for j in range(TG):
                            last = pe.matmul(psY[:, j * D:(j + 1) * D], x2T[b][:, j, :], wo[:, :],
                                             start=True, stop=True)
                        last.then_inc(y_done, 1)

                    def body(t):
                        staged(GROUPS, turn, t, -1)
                        staged(GROUPS, sums, t, 1)
                        product(*t)
                        staged(GROUPS, outp, t, -1)
                    sums(*unit(0))
                    pipeline(pe, GROUPS, body)
                    turn(*unit(GROUPS - 1))
                    outp(*unit(GROUPS - 1))

                @block.scalar
                def _(act):
                    def norm(n, b, f):
                        act.wait_ge(r_done, n + 1)
                        wait(act, nt_done, n - NB + 1)
                        for j in range(TG):
                            last = act.activation(n2[b][:, j, :], v[b][:, j, :], ACT.Identity,
                                                  bias=nmr[b][:, j:j + 1], scale=r[b][:, j:j + 1])
                        last.then_inc(n_done, 1)

                    def relu(n, b, f):
                        act.wait_ge(nt_done, n + 1)
                        wait(act, y_done, n - NB + 1)
                        act.activation(x2T[b][:, :, :].rearrange("p t n -> p (t n)"), psX[:, :], ACT.Relu,
                                       bias=be2_col[:, :], scale=g2_col[:, :]).then_inc(x2_done, 1)

                    def edge_mean(n, b, f):
                        wait(act, put[b], 64 * (f - 1))
                        act.wait_ge(et_done, n + 1)
                        for j in range(TG):
                            last = act.activation(ye[b][:, j, D:YW], psT[:, j * DE:(j + 1) * DE], ACT.Copy,
                                                  scale=rdeg[:, bass.ds(n * TG + j, 1)])
                        last.then_inc(ye_e, 1)

                    def root(n, b, f):
                        act.wait_ge(small, 3 * (n + 1))
                        act.activation(var[b][:, :], var[b][:, :], ACT.Sqrt).then_inc(std_done, 1)

                    def body(t):
                        staged(GROUPS, norm, t, -1)
                        staged(GROUPS, relu, t, -1)
                        edge_mean(*t)
                        root(*t)
                    pipeline(act, GROUPS, body)
                    norm(*unit(GROUPS - 1))
                    relu(*unit(GROUPS - 1))

                @block.vector
                def _(dve):
                    dve.memset(aT[NB - 1][:, TG - 1, :], 0.0)
                    dve.memset(eT[NB - 1][:, TG - 1, :], 0.0).then_inc(primed, 1)
                    dve.wait_ge(primed, 1)

                    def match_up(n, b, f):
                        matches(dve, drow, row_in, S, Q, summed, [aT_done, eT_done], match, n, b, f)

                    def chain(n, b, f):
                        dve.wait_ge(match, n + 1)
                        dve.wait_ge(summed, n + 1)
                        wait(dve, z_done, n - NB + 1)
                        wait(dve, et_done, n - NB + 1)
                        a = carry(dve, aT, Q, psA[b % 2], aT_done, P, n, b)
                        e = carry(dve, eT, Q, psE[b % 2], eT_done, DE, n, b)
                        for j in range(TG):
                            a(j)
                            e(j)

                    def moments(n, b, f):
                        dve.wait_ge(x1_in[b], 16 * f)
                        dve.wait_ge(z_done, n + 1)
                        wait(dve, n_done, n - NB + 1)
                        for j in range(TG):
                            last = dve.scalar_tensor_tensor(
                                v[b][:, j, :], psZ[:, j * D:(j + 1) * D], rdeg[:, bass.ds(n * TG + j, 1)],
                                x1r[b][:, j, :], ALU.mult, ALU.add)
                        last.then_inc(v_done, 1)
                        dve.wait_ge(v_done, n + 1)
                        for j in range(TG):
                            last = dve.bn_stats(st6[b][:, j, :], v[b][:, j, :])
                        last.then_inc(small, 1)
                        dve.wait_ge(small, 3 * n + 1)
                        hold(dve)
                        for j in range(TG):
                            last = dve.bn_aggr(mv[b][:, j, :], st6[b][:, j, :])
                        last.then_inc(small, 1)
                        dve.wait_ge(small, 3 * n + 2)
                        dve.tensor_scalar(var[b][:, :], mv[b][:, :, 1], EPS, None, ALU.add).then_inc(small, 1)

                    def rows_y(n, b, f):
                        dve.wait_ge(y_done, n + 1)
                        wait(dve, put[b], 64 * (f - 1))
                        dve.tensor_tensor(ye[b][:, :, 0:D], psY[:, :].rearrange("p (t d) -> p t d", d=D),
                                          bc(bo_bc[:, :], P, TG), ALU.add).then_inc(ye_y, 1)

                    def rstd(n, b, f):
                        dve.wait_ge(std_done, n + 1)
                        dve.reciprocal(r[b][:, :], var[b][:, :]).then_inc(r1_done, 1)
                        dve.wait_ge(r1_done, n + 1)
                        dve.scalar_tensor_tensor(nmr[b][:, :], mv[b][:, :, 0], -1.0, r[b][:, :], ALU.mult,
                                                 ALU.mult).then_inc(r_done, 1)

                    def body(t):
                        chain(*t)
                        staged(GROUPS, match_up, t, 2)
                        moments(*t)
                        staged(GROUPS, rows_y, t, -1)
                        rstd(*t)
                    match_up(*unit(0))
                    match_up(*unit(1))
                    pipeline(dve, GROUPS, body)
                    rows_y(*unit(GROUPS - 1))
        fills.close()

        FW = YW + 1

        def size(n):
            return (REST, 1) if isinstance(n, int) and n == BLOCKS else (P, BR)

        def rows_of(t, n, c):
            pr, rr = size(n)
            return t[bass.ds(n * BLK, pr * rr), 0:c].rearrange("(p r) c -> p r c", r=rr)

        gx = sb("gx", [P, FW])
        ge = sb("ge", [DE, DE + 1])
        bn_scale = sb("bn_scale", [P, 2])
        bn_shift = sb("bn_shift", [P, 2])
        h0_r = sb("h0_r", [P, UNITS * BR])
        h0_s = sb("h0_s", [P, UNITS * BR])
        CB = 6
        with ExitStack() as st:
            def tb(name, shape, dt=f32):
                return [st.enter_context(nc.sbuf_tensor(f"{name}_c{b}", shape, dt)) for b in range(CB)]

            def t1(name, shape):
                return st.enter_context(nc.sbuf_tensor(name, shape, f32))
            xb = tb("xb", [P, BR, D])
            F = tb("F", [P, BR, FW])
            st6 = tb("st6", [P, BR, 6])
            mv = tb("mv", [P, BR, 2])
            var = tb("var", [P, BR])
            psG = st.enter_context(nc.psum_tensor("psG", [P, 512], f32))
            psH = st.enter_context(nc.psum_tensor("psH", [P, 512], f32))
            x_in = sems("c_x_loaded", CB)
            f_in = sems("c_table_loaded", CB)
            ones_set = sem("c_ones_set")
            s_done = sem("c_sum_ready")
            small = sem("c_small_steps")
            std_done = sem("c_std_ready")
            r1_done = sem("c_rstd_ready")
            r_done = sem("c_rstd_and_shift_ready")
            n_done = sem("c_h0_ready")
            m_done = sem("c_moments_added")
            with nc.Block() as block:
                @block.sync
                def _(sp):
                    def load(n, b, f):
                        pr, rr = size(n)
                        wait(sp, m_done, n - CB + 1)
                        hold(sp)
                        sp.dma_start(xb[b][0:pr, 0:rr, :], rows_of(x, n, D)).then_inc(x_in[b], 16)
                        sp.dma_start(F[b][0:pr, 0:rr, 0:YW], rows_of(ye_tab, n, YW)).then_inc(f_in[b], 16)
                    pipeline(sp, UNITS, lambda t: load(*t), CB)

                @block.vector
                def _(dve):
                    for b in range(CB):
                        last = dve.memset(F[b][:, :, YW:FW], 1.0)
                    last.then_inc(ones_set, 1)

                    def moments(n, b, f):
                        pr, rr = size(n)
                        dve.wait_ge(x_in[b], 16 * f)
                        dve.wait_ge(f_in[b], 16 * f)
                        y = F[b][0:pr, 0:rr, 0:D]
                        dve.scalar_tensor_tensor(y, xb[b][0:pr, 0:rr, :], 2.0, y, ALU.mult,
                                                 ALU.add).then_inc(s_done, 1)
                        dve.wait_ge(s_done, n + 1)
                        for j in range(rr):
                            last = dve.bn_stats(st6[b][0:pr, j, :], F[b][0:pr, j, 0:D])
                        last.then_inc(small, 1)
                        dve.wait_ge(small, 3 * n + 1)
                        hold(dve)
                        for j in range(rr):
                            last = dve.bn_aggr(mv[b][0:pr, j, :], st6[b][0:pr, j, :])
                        last.then_inc(small, 1)
                        dve.wait_ge(small, 3 * n + 2)
                        dve.tensor_scalar(var[b][0:pr, 0:rr], mv[b][0:pr, 0:rr, 1], EPS, None,
                                          ALU.add).then_inc(small, 1)

                    def rstd(n, b, f):
                        pr, rr = size(n)
                        r = h0_r[0:pr, bass.ds(n * BR, rr)]
                        dve.wait_ge(std_done, n + 1)
                        dve.reciprocal(r, var[b][0:pr, 0:rr]).then_inc(r1_done, 1)
                        dve.wait_ge(r1_done, n + 1)
                        dve.scalar_tensor_tensor(h0_s[0:pr, bass.ds(n * BR, rr)], mv[b][0:pr, 0:rr, 0], -1.0,
                                                 r, ALU.mult, ALU.mult).then_inc(r_done, 1)

                    def body(t):
                        moments(*t)
                        staged(UNITS, rstd, t, -1, CB)
                    pipeline(dve, UNITS, body, CB)
                    rstd(*unit(UNITS - 1, CB))

                @block.scalar
                def _(act):
                    def root(n, b, f):
                        pr, rr = size(n)
                        act.wait_ge(small, 3 * n + 3)
                        act.activation(var[b][0:pr, 0:rr], var[b][0:pr, 0:rr], ACT.Sqrt).then_inc(std_done, 1)

                    def norm(n, b, f):
                        pr, rr = size(n)
                        act.wait_ge(r_done, n + 1)
                        for j in range(rr):
                            h0 = F[b][0:pr, j, 0:D]
                            last = act.activation(h0, h0, ACT.Identity, bias=h0_s[0:pr, bass.ds(n * BR + j, 1)],
                                                  scale=h0_r[0:pr, bass.ds(n * BR + j, 1)])
                        last.then_inc(n_done, 1)

                    def body(t):
                        root(*t)
                        staged(UNITS, norm, t, -1, CB)
                    pipeline(act, UNITS, body, CB)
                    norm(*unit(UNITS - 1, CB))

                @block.tensor
                def _(pe):
                    pe.wait_ge(ones_set, 1)

                    def gram(n, b, f):
                        pr, rr = size(n)
                        pe.wait_ge(n_done, n + 1)
                        for j in range(rr):
                            first = isinstance(n, int) and n == 0 and j == 0
                            end = isinstance(n, int) and n == BLOCKS
                            pe.matmul(psG[:, 0:FW], F[b][0:pr, j, 0:D], F[b][0:pr, j, :], start=first, stop=end)
                            last = pe.matmul(psH[0:DE, 0:DE + 1], F[b][0:pr, j, D:YW], F[b][0:pr, j, D:FW],
                                             start=first, stop=end)
                        last.then_inc(m_done, 1)
                    pipeline(pe, UNITS, lambda t: gram(*t), CB)

                @block.gpsimd
                def _(pool):
                    pool.wait_ge(m_done, UNITS)

            gex = t1("gex", [DE, P])
            vgx = t1("vgx", [P, H])
            vge = t1("vge", [DE, H])
            cc = t1("cc", [P, 2])
            mq = t1("mq", [P, 6])
            mu = t1("mu", [P, 2])
            bvar = t1("bvar", [P, 2])
            psT = st.enter_context(nc.psum_tensor("psT_bn", [P, 512], f32))
            psX = st.enter_context(nc.psum_tensor("psX_bn", [P, 512], f32))
            psE = st.enter_context(nc.psum_tensor("psE_bn", [P, 512], f32))
            psM = st.enter_context(nc.psum_tensor("psM_bn", [P, 512], f32))
            vs = sem("n_vector_steps")
            t_done = sem("n_cross_moments_transposed")
            vg_done = sem("n_moment_products")
            pr_done = sem("n_weighted")
            q_done = sem("n_sums_ready")
            std_done = sem("n_std_ready")
            with nc.Block() as block:
                @block.tensor
                def _(pe):
                    pe.wait_ge(vs, 2)
                    pe.transpose(psT[0:DE, 0:P], gx[:, D:YW], ident[:, :]).then_inc(t_done, 1)
                    pe.wait_ge(vs, 3)
                    pe.matmul(psX[:, 0:H], gx[:, 0:D], vx[:, :], start=True, stop=False)
                    pe.matmul(psX[:, 0:H], gex[:, :], ve[:, :], start=False, stop=True)
                    pe.matmul(psE[0:DE, 0:H], gx[:, D:YW], vx[:, :], start=True, stop=False)
                    pe.matmul(psE[0:DE, 0:H], ge[:, 0:DE], ve[:, :], start=False, stop=True).then_inc(vg_done, 1)
                    pe.wait_ge(pr_done, 1)
                    for k in range(2):
                        hk = slice(k * P, (k + 1) * P)
                        pe.matmul(psM[:, k:k + 1], vgx[:, hk], ones[:, :], start=True, stop=False)
                        pe.matmul(psM[:, k:k + 1], vge[:, hk], ones[0:DE, :], start=False, stop=True)
                        pe.matmul(psM[:, 2 + k:3 + k], vx[:, hk], gx[:, YW:FW], start=True, stop=False)
                        pe.matmul(psM[:, 2 + k:3 + k], ve[:, hk], ge[:, DE:DE + 1], start=False, stop=True)
                        last = pe.matmul(psM[:, 4 + k:5 + k], vu[:, hk], u_col[:, :], start=True, stop=True)
                    last.then_inc(q_done, 1)

                @block.scalar
                def _(act):
                    act.wait_ge(vs, 7)
                    act.activation(bvar[:, :], bvar[:, :], ACT.Sqrt).then_inc(std_done, 1)

                @block.vector
                def _(dve):
                    count = [0]

                    def step(ins):
                        count[0] += 1
                        ins.then_inc(vs, 1)
                        dve.wait_ge(vs, count[0])
                    step(dve.tensor_scalar(gx[:, :], psG[:, 0:FW], 1.0 / N, None, ALU.mult))
                    step(dve.tensor_scalar(ge[:, :], psH[0:DE, 0:DE + 1], 1.0 / N, None, ALU.mult))
                    dve.wait_ge(t_done, 1)
                    step(dve.tensor_copy(gex[:, :], psT[0:DE, 0:P]))
                    dve.wait_ge(vg_done, 1)
                    dve.tensor_tensor(vgx[:, :], psX[:, 0:H], vx[:, :], ALU.mult)
                    dve.tensor_tensor(vge[:, :], psE[0:DE, 0:H], ve[:, :], ALU.mult).then_inc(pr_done, 1)
                    dve.wait_ge(q_done, 1)
                    step(dve.tensor_copy(mq[:, :], psM[:, 0:6]))
                    step(dve.tensor_tensor(bvar[:, :], mq[:, 2:4], mq[:, 2:4], ALU.mult))
                    step(dve.tensor_tensor(bvar[:, :], mq[:, 0:2], bvar[:, :], ALU.subtract))
                    step(dve.tensor_scalar(bvar[:, :], bvar[:, :], EPS, None, ALU.add))
                    step(dve.tensor_tensor(cc[:, :], mq[:, 4:6], c1_col[:, :], ALU.add))
                    step(dve.tensor_tensor(mu[:, :], mq[:, 2:4], cc[:, :], ALU.add))
                    step(dve.tensor_tensor(cc[:, :], cc[:, :], mu[:, :], ALU.subtract))
                    dve.wait_ge(std_done, 1)
                    step(dve.reciprocal(bvar[:, :], bvar[:, :]))
                    step(dve.tensor_tensor(bn_scale[:, :], bvar[:, :], gamma_col[:, :], ALU.mult))
                    step(dve.tensor_tensor(bn_shift[:, :], bn_scale[:, :], cc[:, :], ALU.mult))
                    step(dve.tensor_tensor(bn_shift[:, :], bn_shift[:, :], beta_col[:, :], ALU.add))

        with ExitStack() as st:
            def tb(name, shape, n=NB):
                return [st.enter_context(nc.sbuf_tensor(f"{name}_d{b}", shape, f32)) for b in range(n)]
            xb = tb("xb", [P, BR, D])
            F = tb("F", [P, BR, YW])
            hb = tb("hb", [P, BR, D])
            hT = tb("hT", [P, BLK], 2)
            eT = tb("eT", [DE, BLK], 2)
            aH = tb("aH", [P, 2, BLK], 2)
            v = tb("v", [P, BR, D])
            o = tb("o", [P, BR, D])
            st6 = tb("st6", [P, BR, 6])
            mv = tb("mv", [P, BR, 2])
            var = tb("var", [P, BR])
            r = tb("r", [P, BR])
            nmr = tb("nmr", [P, BR])
            psT = st.enter_context(nc.psum_tensor("psT_d", [P, 1024], f32))
            psE = st.enter_context(nc.psum_tensor("psE_d", [P, 1024], f32))
            psH = [st.enter_context(nc.psum_tensor(f"psH_d{k}", [P, 512], f32)) for k in range(2)]
            psO = st.enter_context(nc.psum_tensor("psO_d", [P, 1024], f32))
            x_in = sems("d_x_loaded")
            f_in = sems("d_rows_loaded")
            s_done = sem("d_sum_ready")
            h0_done = sem("d_h0_ready")
            hb_done = sem("d_h0_plus_b2")
            tr_done = sem("d_transposed")
            hT_done = sem("d_h0T_copied")
            eT_done = sem("d_eT_copied")
            h_done = sem("d_hidden_product")
            a_done = sem("d_hidden_relu")
            o_done = sem("d_output_product")
            v_done = sem("d_residual_added")
            small = sem("d_small_steps")
            std_done = sem("d_std_ready")
            r1_done = sem("d_rstd_ready")
            r_done = sem("d_rstd_and_shift_ready")
            n_done = sem("d_out_ready")
            stored = sems("d_out_stored")

            def products(n):
                pr, rr = size(n)
                parts = 2 if rr > 1 else 1
                w = pr * rr // parts
                return [(q, q % 2, slice(q // 2 * w, (q // 2 + 1) * w), w) for q in range(2 * parts)]

            with nc.Block() as block:
                @block.sync
                def _(sp):
                    def load(n, b, f):
                        pr, rr = size(n)
                        wait(sp, s_done, n - NB + 1)
                        wait(sp, tr_done, n - NB + 1)
                        wait(sp, hb_done, n - NB + 1)
                        hold(sp)
                        sp.dma_start(xb[b][0:pr, 0:rr, :], rows_of(x, n, D)).then_inc(x_in[b], 16)
                        sp.dma_start(F[b][0:pr, 0:rr, :], rows_of(ye_tab, n, YW)).then_inc(f_in[b], 16)
                    pipeline(sp, UNITS, lambda t: load(*t))

                @block.gpsimd
                def _(pool):
                    def plus_b2(n, b, f):
                        pr, rr = size(n)
                        pool.wait_ge(h0_done, n + 1)
                        wait(pool, v_done, n - NB + 1)
                        pool.tensor_tensor(hb[b][0:pr, 0:rr, :], F[b][0:pr, 0:rr, 0:D], bc(c2_bc[0:pr, :], pr, rr),
                                           ALU.add).then_inc(hb_done, 1)
                    pipeline(pool, UNITS, lambda t: plus_b2(*t))

                @block.tensor
                def _(pe):
                    def turn(n, b, f):
                        pr, rr = size(n)
                        pe.wait_ge(h0_done, n + 1)
                        wait(pe, hT_done, n)
                        wait(pe, eT_done, n)
                        for j in range(rr):
                            pe.transpose(psT[:, j * P:j * P + pr], F[b][0:pr, j, 0:D], ident[0:pr, 0:pr])
                            last = pe.transpose(psE[0:DE, j * P:j * P + pr], F[b][0:pr, j, D:YW],
                                                ident[0:pr, 0:pr])
                        last.then_inc(tr_done, 1)

                    def hidden(n, b, f):
                        pe.wait_ge(hT_done, n + 1)
                        pe.wait_ge(eT_done, n + 1)
                        for q, k, cols, w in products(n):
                            wait(pe, a_done, 4 * n + q - 1)
                            pe.matmul(psH[k][:, 0:w], vx[:, k * P:(k + 1) * P], hT[b % 2][:, cols],
                                      start=True, stop=False)
                            pe.matmul(psH[k][:, 0:w], ve[:, k * P:(k + 1) * P], eT[b % 2][:, cols],
                                      start=False, stop=True).then_inc(h_done, 1)

                    def outp(n, b, f):
                        pr, rr = size(n)
                        pe.wait_ge(a_done, 4 * n + len(products(n)))
                        wait(pe, v_done, n)
                        for j in range(rr):
                            for k in range(2):
                                last = pe.matmul(psO[0:pr, j * D:(j + 1) * D], aH[b % 2][:, k, j * P:j * P + pr],
                                                 v2[:, k, :], start=(k == 0), stop=(k == 1))
                        last.then_inc(o_done, 1)

                    def body(t):
                        hidden(*t)
                        staged(UNITS, turn, t, 1)
                        outp(*t)
                    turn(*unit(0))
                    pipeline(pe, UNITS, body)

                @block.scalar
                def _(act):
                    def relu(n, b, f, some):
                        wait(act, o_done, n - 1)
                        for q, k, cols, w in products(n)[some]:
                            act.wait_ge(h_done, 4 * n + q + 1)
                            act.activation(aH[b % 2][:, k, cols], psH[k][:, 0:w], ACT.Relu,
                                           bias=bn_shift[:, k:k + 1], scale=bn_scale[:, k:k + 1]
                                           ).then_inc(a_done, 1)

                    def root(n, b, f):
                        pr, rr = size(n)
                        act.wait_ge(small, 3 * n + 3)
                        act.activation(var[b][0:pr, 0:rr], var[b][0:pr, 0:rr], ACT.Sqrt).then_inc(std_done, 1)

                    def edges(n, b, f):
                        pr, rr = size(n)
                        act.wait_ge(tr_done, n + 1)
                        wait(act, h_done, 4 * (n - 1))
                        act.activation(eT[b % 2][:, 0:pr * rr], psE[0:DE, 0:pr * rr], ACT.Copy
                                       ).then_inc(eT_done, 1)

                    def norm(n, b, f):
                        pr, rr = size(n)
                        wait(act, stored[b], 16 * (f - 1))
                        act.wait_ge(r_done, n + 1)
                        for j in range(rr):
                            last = act.activation(o[b][0:pr, j, :], v[b][0:pr, j, :], ACT.Identity,
                                                  bias=nmr[b][0:pr, j:j + 1], scale=r[b][0:pr, j:j + 1])
                        last.then_inc(n_done, 1)
                        act.wait_ge(n_done, n + 1)
                        act.dma_start(rows_of(out, n, D), o[b][0:pr, 0:rr, :]).then_inc(stored[b], 16)

                    def body(t):
                        relu(*t, slice(0, 2))
                        staged(UNITS, root, t, -1)
                        relu(*t, slice(2, 4))
                        staged(UNITS, edges, t, 1)
                        staged(UNITS, norm, t, -1)
                    edges(*unit(0))
                    pipeline(act, UNITS, body)
                    root(*unit(UNITS - 1))
                    norm(*unit(UNITS - 1))
                    for b in range(NB):
                        act.wait_ge(stored[b], 16 * ((UNITS - 1 - b) // NB + 1))

                @block.vector
                def _(dve):
                    def prepare(n, b, f):
                        pr, rr = size(n)
                        dve.wait_ge(x_in[b], 16 * f)
                        dve.wait_ge(f_in[b], 16 * f)
                        y = F[b][0:pr, 0:rr, 0:D]
                        dve.scalar_tensor_tensor(y, xb[b][0:pr, 0:rr, :], 2.0, y, ALU.mult,
                                                 ALU.add).then_inc(s_done, 1)
                        dve.wait_ge(s_done, n + 1)
                        for j in range(rr):
                            h0 = F[b][0:pr, j, 0:D]
                            last = dve.tensor_scalar(h0, h0, h0_r[0:pr, bass.ds(n * BR + j, 1)],
                                                     h0_s[0:pr, bass.ds(n * BR + j, 1)], ALU.mult, ALU.add)
                        last.then_inc(h0_done, 1)

                    def copy_T(n, b, f):
                        pr, rr = size(n)
                        dve.wait_ge(tr_done, n + 1)
                        wait(dve, h_done, 4 * (n - 1))
                        dve.tensor_copy(hT[b % 2][:, 0:pr * rr], psT[:, 0:pr * rr]).then_inc(hT_done, 1)

                    def moments(n, b, f):
                        pr, rr = size(n)
                        dve.wait_ge(o_done, n + 1)
                        dve.wait_ge(hb_done, n + 1)
                        wait(dve, n_done, n - NB + 1)
                        dve.tensor_tensor(v[b][0:pr, 0:rr, :],
                                          psO[0:pr, 0:rr * D].rearrange("p (r d) -> p r d", d=D),
                                          hb[b][0:pr, 0:rr, :], ALU.add).then_inc(v_done, 1)
                        dve.wait_ge(v_done, n + 1)
                        for j in range(rr):
                            last = dve.bn_stats(st6[b][0:pr, j, :], v[b][0:pr, j, :])
                        last.then_inc(small, 1)
                        dve.wait_ge(small, 3 * n + 1)
                        hold(dve)
                        for j in range(rr):
                            last = dve.bn_aggr(mv[b][0:pr, j, :], st6[b][0:pr, j, :])
                        last.then_inc(small, 1)
                        dve.wait_ge(small, 3 * n + 2)
                        dve.tensor_scalar(var[b][0:pr, 0:rr], mv[b][0:pr, 0:rr, 1], EPS, None,
                                          ALU.add).then_inc(small, 1)

                    def rstd(n, b, f):
                        pr, rr = size(n)
                        dve.wait_ge(std_done, n + 1)
                        dve.reciprocal(r[b][0:pr, 0:rr], var[b][0:pr, 0:rr]).then_inc(r1_done, 1)
                        dve.wait_ge(r1_done, n + 1)
                        dve.scalar_tensor_tensor(nmr[b][0:pr, 0:rr], mv[b][0:pr, 0:rr, 0], -1.0,
                                                 r[b][0:pr, 0:rr], ALU.mult, ALU.mult).then_inc(r_done, 1)

                    def body(t):
                        staged(UNITS, moments, t, -1)
                        staged(UNITS, prepare, t, 2)
                        staged(UNITS, rstd, t, -1)
                        staged(UNITS, copy_T, t, 1)
                    prepare(*unit(0))
                    prepare(*unit(1))
                    copy_T(*unit(0))
                    pipeline(dve, UNITS, body)
                    moments(*unit(UNITS - 1))
                    rstd(*unit(UNITS - 1))


_NAMES = ['x', 'src', 'dst', 'edge_attr_96', 'L0_gnn_W1', 'L0_gnn_b1', 'L0_gnn_g1', 'L0_gnn_be1', 'L0_gnn_W2',
          'L0_gnn_b2', 'L0_gnn_g2', 'L0_gnn_be2', 'L0_gnn_Wo', 'L0_gnn_bo', 'L1_gnn_u', 'L1_gnn_W1', 'L1_gnn_b1',
          'L1_gnn_gamma', 'L1_gnn_beta', 'L1_gnn_W2', 'L1_gnn_b2']


def kernel(**inputs):
    import numpy as _np
    import concourse.bacc as _bacc
    from concourse import mybir as _mybir
    from concourse.bass_utils import run_bass_kernel_spmd as _run

    nc = _bacc.Bacc("TRN2", target_bir_lowering=False, num_devices=1)
    arrays, args = {}, []
    for name in _NAMES:
        a = _np.ascontiguousarray(inputs[name])
        arrays[f"in_{name}"] = a
        args.append(nc.dram_tensor(f"in_{name}", a.shape, _mybir.dt.from_np(a.dtype), kind="ExternalInput").ap())
    shape = arrays["in_x"].shape
    args.append(nc.dram_tensor("out_0", shape, _mybir.dt.float32, kind="ExternalOutput").ap())
    build_gnn(nc, *args)
    r = _run(nc, [arrays], core_ids=[0])
    return r.results[0]["out_0"]
```

```python
import concourse.bass as bass
from concourse import mybir
from contextlib import ExitStack


def wait(eng, sem, value):
    if isinstance(value, int) and value <= 0:
        return
    eng.wait_ge(sem, value)


NB = 4


def unit(n, nb=NB):
    return n, n % nb, n // nb + 1


def shift(t, d, nb=NB):
    n, b, f = t
    return n + d, (b + d) % nb, f + (b + d) // nb


def pipeline(eng, total, body, nb=NB):
    loops = total // nb
    for n in range(nb):
        body(unit(n, nb))
    with eng.Fori(1, loops - 1) as i:
        for b in range(nb):
            body((i * nb + b, b, i + 1))
    for n in range((loops - 1) * nb, total):
        body(unit(n, nb))


def staged(total, stage, t, d, nb=NB):
    n = t[0]
    if not isinstance(n, int) or 0 <= n + d < total:
        stage(*shift(t, d, nb))


def build_gnn(nc, x, src, dst, ea, W1, b1, g1, be1, W2, b2, g2, be2, Wo, bo,
              u, V1, c1, gamma, beta, V2, c2, out):
    f32, i32, bf16, f32r = mybir.dt.float32, mybir.dt.int32, mybir.dt.bfloat16, mybir.dt.float32r
    ALU = mybir.AluOpType
    ACT = mybir.ActivationFunctionType

    P = 128
    N, D = x.shape
    E, DE = ea.shape
    H = V1.shape[1]
    DU = u.shape[1]
    EPS = 1e-5

    TG = 4
    GE = TG * P
    GROUPS = -(-E // GE)
    EP = GROUPS * GE
    TILES = GROUPS * TG
    TQ = TILES // 2
    SKIP = 60000
    FILL_A, FILL_R = 23, 17
    NT = P * FILL_R * FILL_A
    assert N <= 1 << 16 and EP < 1 << 20
    assert NT >= N and E < EP and TILES % 2 == 0
    YW = D + DE

    BR = 5
    BLK = P * BR
    BLOCKS = N // BLK
    REST = N - BLOCKS * BLK
    UNITS = BLOCKS + 1
    assert 0 < REST <= P

    src_s = nc.dram_tensor("src_sorted", [EP], i32).ap()
    dst_s = nc.dram_tensor("dst_sorted", [EP + 2], i32).ap()
    deg_s = nc.dram_tensor("degree_by_slot", [EP], f32).ap()
    NO_EDGE = EP
    x1_slot = nc.dram_tensor("x1_by_slot", [EP + 1, D], f32).ap()
    ye_tab = nc.dram_tensor("y_e_by_node", [NT, YW], f32).ap()

    def bc(a, p, n):
        return a.rearrange("p (o d) -> p o d", o=1).to_broadcast([p, n, a.shape[1]])

    ctx = ExitStack()
    with ctx:
        def sb(name, shape, dt=f32):
            return ctx.enter_context(nc.sbuf_tensor(name, shape, dt))

        def sem(name):
            return ctx.enter_context(nc.semaphore(name))

        def sems(name, nb=NB):
            return [sem(f"{name}{b}") for b in range(nb)]

        ident = sb("ident", [P, P])
        ones = sb("ones", [P, 1])
        w1 = sb("w1", [P, D])
        w2 = sb("w2", [P, D])
        wo = sb("wo", [P, D])
        b1_row = sb("b1_row", [1, D])
        g1_bc = sb("g1_bc", [P, D])
        be1_bc = sb("be1_bc", [P, D])
        b2_row = sb("b2_row", [1, D])
        bo_bc = sb("bo_bc", [P, D])
        c2_bc = sb("c2_bc", [P, D])
        g2_col = sb("g2_col", [P, 1])
        be2_col = sb("be2_col", [P, 1])
        vx = sb("vx", [P, H])
        ve = sb("ve", [DE, H])
        vu = sb("vu", [DU, H])
        v2 = sb("v2", [P, 2, D])
        u_col = sb("u_col", [DU, 1])
        c1_col = sb("c1_col", [P, 2])
        gamma_col = sb("gamma_col", [P, 2])
        beta_col = sb("beta_col", [P, 2])
        src_idx = sb("src_idx", [P, TILES], i32)
        src_col = sb("src_col", [P, TILES])
        src_neg = sb("src_neg", [P, TILES])
        x1_idx = sb("x1_idx", [P, TILES], i32)
        put_idx = sb("put_idx", [P, TILES], i32)
        dst_col = sb("dst_col", [P, TILES], i32)
        rdeg = sb("rdeg", [P, TILES])
        de2 = sb("de2", [P, TILES])

        turns = sem("turns")

        def hold(eng):
            eng.sem_inc(turns, 1)

        ye_filled = sem("ye_table_filled")
        fills = ExitStack()
        fill_ye = fills.enter_context(nc.sbuf_tensor("fill_ye", [P, FILL_R, YW], f32))
        deg = fills.enter_context(nc.sbuf_tensor("deg", [TQ, 2 * P], f32))
        x1c = fills.enter_context(nc.sbuf_tensor("x1c", [P, D], f32))
        tile_dst = fills.enter_context(nc.sbuf_tensor("tile_dst", [TQ, 2, P + 1], i32))
        diff_hi = fills.enter_context(nc.sbuf_tensor("diff_hi", [TQ, 2, P + 1], bf16))
        diff_lo = fills.enter_context(nc.sbuf_tensor("diff_lo", [TQ, 2, P + 1], bf16))

        with ExitStack() as st:
            def tb(name, shape, dt=f32):
                return st.enter_context(nc.sbuf_tensor(name, shape, dt))

            def ps(name):
                return st.enter_context(nc.psum_tensor(name, [P, 512], f32))
            pad_src = tb("pad_src", [1, EP - E], i32)
            pad_dst = tb("pad_dst", [1, EP - E + 1], i32)
            pad_front = tb("pad_front", [1, 1], i32)
            src_t = tb("src_t", [TQ, 2 * P], i32)
            dst_t = tb("dst_t", [TQ, 2 * P], i32)
            nxt_t = tb("nxt_t", [TQ, 2 * P], i32)
            src_f = tb("src_f", [TQ, 2 * P])
            dst_f = tb("dst_f", [TQ, 2 * P])
            put_f = tb("put_f", [TQ, 2 * P])
            same = tb("same", [TQ, 2 * P])
            prv_t = tb("prv_t", [TQ, 2 * P], i32)
            before_t = tb("before_t", [TQ, 2, P], i32)
            diff = tb("diff", [TQ, 2, P])
            pos = tb("pos", [TQ, 2 * P], i32)
            first = [tb(f"first{k}", [TQ, 2 * P]) for k in range(2)]
            firstT = [tb(f"firstT{k}", [1, TQ]) for k in range(2)]
            first_in = tb("first_in", [TQ, 1])
            degc = tb("degc", [P, TILES])
            yc = tb("yc", [P, D])
            x2n = tb("x2n", [P, D])
            x2t = tb("x2t", [P, D])
            st6 = tb("st6", [P, 6])
            mv = tb("mv", [P, 2])
            rs = tb("rs", [P, 1])
            ps_i = [ps(f"ps_i{k}") for k in range(6)]
            ps_t = ps("ps_t")
            ps_y = ps("ps_y")
            zero_front = sem("differences_zeroed")

            be1_in = sem("be1_loaded")
            loaded = sem("weights_loaded")
            zeroed = sem("ident_zeroed")
            ident_ok = sem("ident_ready")
            pads_ok = sem("pads_ready")
            copied = sem("edges_copied")
            idx_loaded = sem("indices_loaded")
            idx_f = sem("indices_float")
            idx_t = sem("indices_transposed")
            v_step = sem("prologue_vector_steps")
            c_var = sem("const_row_variance")
            c_std = sem("const_row_std")
            c_norm = sem("const_row_normed")
            c_tr = sem("const_row_transposed")
            c_act = sem("const_row_relu")
            c_y = sem("const_row_y")
            c_x1 = sem("const_row_x1")
            c_kept = sem("const_row_stored")
            pos_ok = sem("positions_ready")
            runs_ok = sem("run_starts_of_rows")
            runs_t = sem("run_starts_transposed")
            carry_ok = sem("run_starts_carried")
            carry_t = sem("carried_starts_transposed")
            deg_ok = sem("degrees_ready")
            deg_t = sem("degrees_transposed")
            deg_kept = sem("degrees_stored")
            RT = (TQ - 1).bit_length() % 2
            line = lambda a: a.rearrange("(o n) -> o n", o=1)
            col = lambda a: a.rearrange("(p o) -> p o", o=1)
            bcast = lambda a: line(a).to_broadcast([P, D])
            weights = [
                (wo[:, :], Wo), (bo_bc[:, :], bcast(bo)), (g2_col[:, :], col(g2)), (be2_col[:, :], col(be2)),
                (w1[:, :], W1), (w2[:, :], W2), (b1_row[:, :], line(b1)), (g1_bc[:, :], bcast(g1)),
                (b2_row[:, :], line(b2)), (c2_bc[:, :], bcast(c2)),
                (vx[:, :], V1[0:D, :]), (ve[:, :], V1[D:D + DE, :]), (vu[:, :], V1[D + DE:, :]),
                (v2[:, :, :], V2.rearrange("(k p) d -> p k d", p=P)),
                (u_col[:, :], u[0:1, :].rearrange("o d -> d o")),
                (c1_col[:, :], c1.rearrange("(k p) -> p k", p=P)),
                (gamma_col[:, :], gamma.rearrange("(k p) -> p k", p=P)),
                (beta_col[:, :], beta.rearrange("(k p) -> p k", p=P)),
            ]

            with nc.Block() as block:
                @block.sync
                def _(sp):
                    sp.dma_start(be1_bc[:, :], bcast(be1)).then_inc(be1_in, 16)
                    with nc.allow_non_contiguous_dma(reason="small columns"):
                        for to, frm in weights:
                            sp.dma_start(to, frm).then_inc(loaded, 16)
                    sp.wait_ge(c_x1, 1)
                    sp.dma_start(x1_slot[NO_EDGE:NO_EDGE + 1, :], x1c[0:1, :]).then_inc(c_kept, 16)
                    sp.wait_ge(deg_ok, 1)
                    sp.dma_start(deg_s.rearrange("(q n) -> q n", n=2 * P), deg[:, :]).then_inc(deg_kept, 16)
                    sp.wait_ge(loaded, 16 * len(weights))

                @block.gpsimd
                def _(pool):
                    pool.memset(pad_src[:, :], 0)
                    pool.memset(pad_dst[:, :], N)
                    pool.memset(pad_front[:, :], -1).then_inc(pads_ok, 1)
                    pool.memset(before_t[:, :, :], 0).then_inc(zero_front, 1)
                    pool.memset(ident[:, :], 0.0).then_inc(zeroed, 1)
                    pool.iota(pos[:, :], [[1, 2 * P]], base=0, channel_multiplier=2 * P).then_inc(pos_ok, 1)
                    pool.memset(ones[:, :], 1.0)
                    pool.wait_ge(zeroed, 1)
                    pool.affine_select(out=ident[:, :], in_=ident[:, :], compare_op=ALU.not_equal, fill=1.0,
                                       base=0, pattern=[[-1, P]], channel_multiplier=1).then_inc(ident_ok, 1)

                @block.scalar
                def _(act):
                    act.dma_start(src_s[0:E], src).then_inc(copied, 16)
                    act.dma_start(dst_s[1:E + 1], dst).then_inc(copied, 16)
                    act.wait_ge(pads_ok, 1)
                    act.dma_start(line(src_s[E:EP]), pad_src[:, :]).then_inc(copied, 16)
                    act.dma_start(line(dst_s[E + 1:EP + 2]), pad_dst[:, :]).then_inc(copied, 16)
                    act.dma_start(line(dst_s[0:1]), pad_front[:, :]).then_inc(copied, 16)
                    act.wait_ge(copied, 16 * 5)
                    rows = lambda a: a.rearrange("(q n) -> q n", n=2 * P)
                    act.dma_start(src_t[:, :], rows(src_s)).then_inc(idx_loaded, 16)
                    act.dma_start(dst_t[:, :], rows(dst_s[1:EP + 1])).then_inc(idx_loaded, 16)
                    act.dma_start(nxt_t[:, :], rows(dst_s[2:EP + 2])).then_inc(idx_loaded, 16)
                    act.dma_start(prv_t[:, :], rows(dst_s[0:EP])).then_inc(idx_loaded, 16)
                    act.dma_start(tile_dst[:, :, 0:P], dst_s[0:EP].rearrange("(c q n) -> q c n", c=2, n=P)
                                  ).then_inc(idx_loaded, 16)
                    act.wait_ge(zero_front, 1)
                    act.dma_start(before_t[1:TQ, 0, :], dst_s[0:(TQ - 1) * P].rearrange("(q n) -> q n", n=P)
                                  ).then_inc(idx_loaded, 16)
                    act.dma_start(before_t[:, 1, :], dst_s[(TQ - 1) * P:(2 * TQ - 1) * P]
                                  .rearrange("(q n) -> q n", n=P)).then_inc(idx_loaded, 16)
                    act.wait_ge(c_var, 1)
                    act.activation(rs[:, :], rs[:, :], ACT.Sqrt).then_inc(c_std, 1)
                    act.wait_ge(c_tr, 1)
                    act.activation(x2t[:, :], ps_t[:, 0:D], ACT.Relu, bias=be2_col[:, :],
                                   scale=g2_col[:, :]).then_inc(c_act, 1)

                @block.tensor
                def _(pe):
                    pe.wait_ge(ident_ok, 1)
                    pe.wait_ge(c_norm, 1)
                    pe.transpose(ps_t[:, 0:D], x2n[:, :], ident[:, :]).then_inc(c_tr, 1)
                    pe.wait_ge(c_act, 1)
                    pe.matmul(ps_y[:, 0:D], x2t[:, :], wo[:, :], start=True, stop=True).then_inc(c_y, 1)
                    pe.wait_ge(idx_f, 1)
                    for k, t in enumerate((src_f, dst_f, put_f)):
                        for j in range(2):
                            last = pe.transpose(ps_i[2 * k + j][:, 0:TQ], t[:, j * P:(j + 1) * P],
                                                ident[0:TQ, 0:TQ])
                    last.then_inc(idx_t, 1)
                    pe.wait_ge(runs_ok, 1)
                    pe.transpose(ps_t[0:1, P:P + TQ], first[0][:, 2 * P - 1:2 * P], ident[0:TQ, 0:TQ]
                                 ).then_inc(runs_t, 1)
                    pe.wait_ge(carry_ok, 1)
                    pe.transpose(ps_t[0:TQ, 2 * P:2 * P + 1], firstT[RT][:, :], ident[0:1, 0:1]
                                 ).then_inc(carry_t, 1)
                    pe.wait_ge(deg_ok, 1)
                    for j in range(2):
                        last = pe.transpose(ps_y[:, (1 + j) * P:(1 + j) * P + TQ], deg[:, j * P:(j + 1) * P],
                                            ident[0:TQ, 0:TQ])
                    last.then_inc(deg_t, 1)

                @block.vector
                def _(dve):
                    done = [0]

                    def step(ins):
                        done[0] += 1
                        ins.then_inc(v_step, 1)
                        dve.wait_ge(v_step, done[0])

                    def running_max(bufs, width):
                        k, d = 0, 1
                        while d < width:
                            dve.tensor_copy(bufs[1 - k][:, 0:d], bufs[k][:, 0:d])
                            step(dve.tensor_tensor(bufs[1 - k][:, d:width], bufs[k][:, d:width],
                                                   bufs[k][:, 0:width - d], ALU.max))
                            k, d = 1 - k, 2 * d
                        return k

                    dve.wait_ge(be1_in, 16)
                    step(dve.tensor_scalar(x1c[:, :], be1_bc[:, :], 0.0, None, ALU.max))
                    dve.sem_inc(c_x1, 1)
                    step(dve.bn_stats(st6[:, :], x1c[:, :]))
                    step(dve.bn_aggr(mv[:, :], st6[:, :]))
                    dve.tensor_scalar(rs[:, :], mv[:, 1:2], EPS, None, ALU.add).then_inc(c_var, 1)
                    dve.memset(fill_ye[:, :, D:YW], 0.0)
                    dve.wait_ge(loaded, 16 * len(weights))
                    dve.wait_ge(c_std, 1)
                    step(dve.reciprocal(rs[:, :], rs[:, :]))
                    dve.tensor_scalar(x2n[:, :], x1c[:, :], mv[:, 0:1], rs[:, :], ALU.subtract,
                                      ALU.mult).then_inc(c_norm, 1)
                    dve.wait_ge(c_y, 1)
                    step(dve.tensor_tensor(yc[:, :], ps_y[:, 0:D], bo_bc[:, :], ALU.add))
                    dve.tensor_copy(fill_ye[:, :, 0:D], bc(yc[:, :], P, FILL_R))
                    dve.wait_ge(idx_loaded, 16 * 7)
                    dve.tensor_copy(src_f[:, :], src_t[:, :])
                    dve.tensor_copy(dst_f[:, :], dst_t[:, :])
                    step(dve.tensor_tensor(same[:, :], dst_t[:, :], nxt_t[:, :], ALU.is_equal))
                    dve.scalar_tensor_tensor(put_f[:, :], same[:, :], float(SKIP), dst_f[:, :], ALU.mult,
                                             ALU.add).then_inc(idx_f, 1)
                    dve.wait_ge(idx_t, 1)
                    for k, t in enumerate((src_idx, dst_col, put_idx)):
                        for j in range(2):
                            dve.tensor_copy(t[:, j:TILES:2], ps_i[2 * k + j][:, 0:TQ])
                    for j in range(2):
                        dve.tensor_copy(src_col[:, j:TILES:2], ps_i[j][:, 0:TQ])
                        dve.tensor_scalar(src_neg[:, j:TILES:2], ps_i[j][:, 0:TQ], -1.0, None, ALU.mult)
                    step(dve.tensor_tensor(diff[:, :, :], tile_dst[:, :, 0:P], before_t[:, :, :],
                                           ALU.subtract))
                    dve.memset(diff_lo[:, :, P:P + 1], 0.0)
                    dve.memset(diff_hi[:, :, P:P + 1], float(P))
                    step(dve.tensor_copy(diff_hi[:, :, 0:P], diff[:, :, :]))
                    dve.tensor_tensor(diff_lo[:, :, 0:P], diff[:, :, :], diff_hi[:, :, 0:P], ALU.subtract)
                    dve.wait_ge(pos_ok, 1)
                    step(dve.tensor_tensor(same[:, :], dst_t[:, :], prv_t[:, :], ALU.is_equal))
                    step(dve.tensor_tensor(first[1][:, :], same[:, :], pos[:, :], ALU.mult))
                    step(dve.tensor_tensor(first[0][:, :], pos[:, :], first[1][:, :], ALU.subtract))
                    k = running_max(first, 2 * P)
                    assert k == 0
                    dve.sem_inc(runs_ok, 1)
                    dve.wait_ge(runs_t, 1)
                    dve.memset(firstT[0][:, 0:1], 0.0)
                    step(dve.tensor_copy(firstT[0][:, 1:TQ], ps_t[0:1, P:P + TQ - 1]))
                    k = running_max(firstT, TQ)
                    assert k == RT
                    dve.sem_inc(carry_ok, 1)
                    dve.wait_ge(carry_t, 1)
                    step(dve.tensor_copy(first_in[:, :], ps_t[0:TQ, 2 * P:2 * P + 1]))
                    step(dve.tensor_scalar(first[1][:, :], first[0][:, :], first_in[:, :], -1.0, ALU.max,
                                           ALU.mult))
                    dve.scalar_tensor_tensor(deg[:, :], first[1][:, :], 1.0, pos[:, :], ALU.add, ALU.add
                                             ).then_inc(deg_ok, 1)
                    dve.wait_ge(deg_t, 1)
                    for j in range(2):
                        last = dve.tensor_copy(degc[:, j:TILES:2], ps_y[:, (1 + j) * P:(1 + j) * P + TQ])
                    step(last)
                    dve.reciprocal(rdeg[:, :], degc[:, :])
                    dve.scalar_tensor_tensor(de2[:, :], degc[:, :], EPS, degc[:, :], ALU.mult, ALU.mult)

        def load_rows(eng, drow, row_in, match, n, b, f):
            wait(eng, match, n - NB + 1)
            hold(eng)
            eng.dma_start(drow[b][:, :], dst_s[bass.ds(n * GE, GE + 1)].rearrange("(o n) -> o n", o=1)
                          .to_broadcast([P, GE + 1])).then_inc(row_in[b], 16)

        def matches(dve, drow, row_in, S, Q, summed, carried, match, n, b, f):
            dve.wait_ge(row_in[b], 16 * f)
            wait(dve, summed, n - NB + 1)
            for c in carried:
                wait(dve, c, TG * (n - NB + 1))
            cur = drow[b][:, 1:1 + GE].rearrange("p (t n) -> p t n", n=P)
            own = dst_col[:, bass.ds(n * TG, TG)].rearrange("p (t o) -> p t o", o=1)
            before = drow[b][:, 0:GE:P].rearrange("p (t o) -> p t o", o=1)
            dve.tensor_tensor(S[b][:, :, :], cur, own.to_broadcast([P, TG, P]), ALU.is_equal)
            dve.tensor_tensor(Q[b][:, :, :], cur, before.to_broadcast([P, TG, P]),
                              ALU.is_equal).then_inc(match, 1)

        def carry(dve, sums, Q, psum, done, parts, n, b):
            def tile(j):
                prev = sums[b][0:parts, j - 1, P - 1:P] if j else sums[b - 1][0:parts, TG - 1, P - 1:P]
                wait(dve, done, TG * n + j)
                dve.scalar_tensor_tensor(sums[b][0:parts, j, :], Q[b][0:parts, j, :], prev,
                                         psum[0:parts, j * P:(j + 1) * P], ALU.mult, ALU.add
                                         ).then_inc(done, 1)
            return tile

        def copy_idx(act, at, idx, used, idx_copied, n, b, f):
            wait(act, used[b], 64 * (f - 1))
            act.activation(idx[b][:, :], at[:, bass.ds(n * TG, TG)], ACT.Copy).then_inc(idx_copied, 1)

        def gather(pool, table, top, idx, idx_copied, rows, gat, summed, n, b, f):
            wait(pool, summed, n - NB + 1)
            pool.wait_ge(idx_copied, n + 1)
            hold(pool)
            for j in range(TG):
                pool.indirect_dma_start(rows[b][:, j, :], None, table,
                                        bass.IndirectOffsetOnAxis(ap=idx[b][:, j:j + 1], axis=0),
                                        bounds_check=top, oob_is_err=False).then_inc(gat[b], 16)

        def scatter(pool, table, idx, idx_copied, rows, put, ready, n, b, f):
            pool.wait_ge(ye_filled, 16 * FILL_A)
            for r in ready:
                pool.wait_ge(r, n + 1)
            pool.wait_ge(idx_copied, n + 1)
            hold(pool)
            for j in range(TG):
                pool.indirect_dma_start(table, bass.IndirectOffsetOnAxis(ap=idx[b][:, j:j + 1], axis=0),
                                        rows[b][:, j, :], None, bounds_check=N - 1,
                                        oob_is_err=False).then_inc(put[b], 16)

        last_b, last_f = (GROUPS - 1) % NB, (GROUPS - 1) // NB + 1
        fills_of = lambda b: last_f if b <= last_b else last_f - 1

        with ExitStack() as st:
            def tb(name, shape, dt=f32):
                return [st.enter_context(nc.sbuf_tensor(f"{name}_a{b}", shape, dt)) for b in range(NB)]

            def ps(name):
                return [st.enter_context(nc.psum_tensor(f"{name}_a{b}", [P, 512], f32)) for b in range(2)]
            idx = tb("idx", [P, TG], i32)
            xg = tb("xg", [P, TG, D])
            drow = tb("drow", [P, GE + 1], i32)
            srow = tb("srow", [TQ, GE], i32)
            degr = tb("degr", [1, GE])
            S = tb("S", [P, TG, P])
            Q = tb("Q", [P, TG, P])
            G = tb("G", [TQ, 2, GE], bf16)
            aT = tb("aT", [P, TG, P])
            le = tb("le", [P, TG, P], bf16)
            sg = tb("sg", [P, TG, P], bf16)
            n_le = tb("n_le", [P, TG])
            n_sg = tb("n_sg", [P, TG])
            slots = tb("slots", [P, TG])
            hit = tb("hit", [P, TG])
            st6 = tb("st6", [P, TG, 6])
            mv = tb("mv", [P, TG, 2])
            var = tb("var", [P, TG])
            r = tb("r", [P, TG])
            nmr = tb("nmr", [P, TG])
            z = tb("z", [P, TG, D])
            x1 = tb("x1", [P, TG, D])
            psA, psZ = ps("psA"), ps("psZ")
            psV = [st.enter_context(nc.psum_tensor(f"psV_a{b}", [P, 1024], f32)) for b in range(2)]

            row_in = sems("a_dst_row_loaded")
            gat = sems("a_rows_gathered")
            more_in = sems("a_src_and_degree_rows_loaded")
            kept = sems("a_x1_slot_stored")
            idx_copied = sem("a_idx_copied")
            match = sem("a_match_ready")
            summed = sem("a_tile_sums_ready")
            aT_done = sem("a_sums_with_carry")
            ge_done = sem("a_tiles_compared")
            tiles_done = sem("a_destinations_looked_up")
            le_done = sem("a_counted")
            sg_done = sem("a_signs_summed")
            look = sem("a_search_steps")
            z_done = sem("a_product_ready")
            small = sem("a_small_steps")
            std_done = sem("a_std_ready")
            r1_done = sem("a_rstd_ready")
            r_done = sem("a_rstd_and_shift_ready")
            n_done = sem("a_normed")
            zg = sem("a_scaled")
            zb = sem("a_shifted")
            x1_done = sem("a_x1_ready")
            primed = sem("a_carry_zeroed")
            SEARCH = 5

            def tile_of(psum, j, w):
                at = j // 2 * 512 + j % 2 * (P + 1)
                return psum[:, at:at + w]

            with nc.Block() as block:
                @block.sync
                def _(sp):
                    def rows(n, b, f):
                        load_rows(sp, drow, row_in, match, n, b, f)

                    def more_rows(n, b, f):
                        wait(sp, ge_done, n - NB + 1)
                        wait(sp, z_done, n - NB + 1)
                        hold(sp)
                        sp.dma_start(srow[b][:, :], src_s[bass.ds(n * GE, GE)].rearrange("(o n) -> o n", o=1)
                                     .to_broadcast([TQ, GE])).then_inc(more_in[b], 16)
                        sp.dma_start(degr[b][:, :], deg_s[bass.ds(n * GE, GE)].rearrange("(o n) -> o n", o=1)
                                     ).then_inc(more_in[b], 16)

                    def store(n, b, f):
                        sp.wait_ge(x1_done, n + 1)
                        hold(sp)
                        sp.dma_start(x1_slot[bass.ds(n * GE, GE), :].rearrange("(t p) d -> p t d", p=P),
                                     x1[b][:, :, :]).then_inc(kept[b], 16)

                    def fill(n, b, f):
                        if b % 2 == 0 and not (isinstance(n, int) and n // 2 >= FILL_A):
                            chunk = ye_tab.rearrange("(a q) d -> a (q d)", a=FILL_A)
                            sp.dma_start(chunk[bass.ds((f - 1) * (NB // 2) + b // 2, 1), :]
                                         .rearrange("o (p m) -> (o p) m", p=P),
                                         fill_ye[:, :, :].rearrange("p r d -> p (r d)")).then_inc(ye_filled, 16)

                    def body(t):
                        staged(GROUPS, rows, t, 3)
                        staged(GROUPS, more_rows, t, 3)
                        fill(*t)
                        staged(GROUPS, store, t, -3)
                    assert GROUPS // 2 + 1 >= FILL_A
                    for n in range(3):
                        rows(*unit(n))
                    sp.wait_ge(deg_kept, 16)
                    for n in range(3):
                        more_rows(*unit(n))
                    pipeline(sp, GROUPS, body)
                    for n in range(GROUPS - 3, GROUPS):
                        store(*unit(n))
                    for b in range(NB):
                        sp.wait_ge(kept[b], 16 * fills_of(b))

                @block.gpsimd
                def _(pool):
                    def get(n, b, f):
                        gather(pool, x[:, :], N - 1, idx, idx_copied, xg, gat, summed, n, b, f)

                    def affine(n, b, f):
                        pool.wait_ge(n_done, n + 1)
                        hold(pool)
                        pool.tensor_tensor(z[b][:, :, :], z[b][:, :, :], bc(g1_bc[:, :], P, TG),
                                           ALU.mult).then_inc(zg, 1)
                        pool.wait_ge(zg, n + 1)
                        hold(pool)
                        pool.tensor_tensor(z[b][:, :, :], z[b][:, :, :], bc(be1_bc[:, :], P, TG),
                                           ALU.add).then_inc(zb, 1)

                    def body(t):
                        staged(GROUPS, get, t, 3)
                        staged(GROUPS, affine, t, -3)
                    for n in range(3):
                        get(*unit(n))
                    pipeline(pool, GROUPS, body)
                    for n in range(GROUPS - 3, GROUPS):
                        affine(*unit(n))

                @block.tensor
                def _(pe):
                    def sums(n, b, f):
                        pe.wait_ge(match, n + 1)
                        pe.wait_ge(gat[b], 64 * f)
                        wait(pe, aT_done, TG * (n - 1))
                        for j in range(TG):
                            last = pe.matmul(psA[b % 2][:, j * P:(j + 1) * P], xg[b][:, j, :], S[b][:, j, :],
                                             start=True, stop=True)
                        last.then_inc(summed, 1)

                    def look_up(n, b, f):
                        pe.wait_ge(ge_done, n + 1)
                        wait(pe, look, SEARCH * (n - 1))
                        wait(pe, sg_done, n - 1)
                        for j in range(TG):
                            for k in range(4):
                                c, part = k // 2, (diff_hi, diff_lo)[k % 2]
                                last = pe.matmul(tile_of(psV[b % 2], j, P + 1), G[b][:, c, j * P:(j + 1) * P],
                                                 part[:, c, :], start=(k == 0), stop=(k == 3))
                        last.then_inc(tiles_done, 1)

                    def product(n, b, f):
                        pe.wait_ge(aT_done, TG * (n + 1))
                        pe.wait_ge(more_in[b], 32 * f)
                        wait(pe, n_done, n - 1)
                        for j in range(TG):
                            o = psZ[b % 2][:, j * D:(j + 1) * D]
                            pe.matmul(o, aT[b][:, j, :], w1[:, :], start=True, stop=False)
                            last = pe.matmul(o, degr[b][:, j * P:(j + 1) * P], b1_row[:, :], start=False,
                                             stop=True)
                        last.then_inc(z_done, 1)

                    def body(t):
                        staged(GROUPS, sums, t, 1)
                        look_up(*t)
                        product(*t)
                    sums(*unit(0))
                    pipeline(pe, GROUPS, body)

                @block.scalar
                def _(act):
                    def norm(n, b, f):
                        act.wait_ge(r_done, n + 1)
                        wait(act, x1_done, n - NB + 1)
                        for j in range(TG):
                            last = act.activation(z[b][:, j, :], psZ[b % 2][:, j * D:(j + 1) * D], ACT.Identity,
                                                  bias=nmr[b][:, j:j + 1], scale=r[b][:, j:j + 1])
                        last.then_inc(n_done, 1)

                    def relu(n, b, f):
                        wait(act, kept[b], 16 * (f - 1))
                        act.wait_ge(zb, n + 1)
                        act.activation(x1[b][:, :, :], z[b][:, :, :], ACT.Relu).then_inc(x1_done, 1)

                    def root(n, b, f):
                        act.wait_ge(small, 3 * (n + 1))
                        act.activation(var[b][:, :], var[b][:, :], ACT.Sqrt).then_inc(std_done, 1)

                    def signs(n, b, f):
                        act.wait_ge(le_done, n + 1)
                        wait(act, look, SEARCH * (n - NB + 1))
                        for j in range(TG):
                            last = act.activation(sg[b][:, j, :], tile_of(psV[b % 2], j, P), ACT.Sign,
                                                  bias=src_neg[:, bass.ds(n * TG + j, 1)], scale=1.0,
                                                  accum_out=n_sg[b][:, j:j + 1])
                        last.then_inc(sg_done, 1)

                    def body(t):
                        staged(GROUPS, indices, t, NB + 1)
                        staged(GROUPS, relu, t, -3)
                        staged(GROUPS, root, t, -1)
                        staged(GROUPS, norm, t, -1)
                        signs(*t)

                    def indices(n, b, f):
                        copy_idx(act, src_idx, idx, gat, idx_copied, n, b, f)
                    for n in range(NB + 1):
                        indices(*unit(n))
                    pipeline(act, GROUPS, body)
                    root(*unit(GROUPS - 1))
                    norm(*unit(GROUPS - 1))
                    for n in range(GROUPS - 3, GROUPS):
                        relu(*unit(n))

                @block.vector
                def _(dve):
                    dve.memset(aT[NB - 1][:, TG - 1, :], 0.0).then_inc(primed, 1)
                    dve.wait_ge(primed, 1)

                    def match_up(n, b, f):
                        matches(dve, drow, row_in, S, Q, summed, [aT_done], match, n, b, f)

                    def chain(n, b, f, between=None):
                        dve.wait_ge(match, n + 1)
                        dve.wait_ge(summed, n + 1)
                        wait(dve, z_done, n - NB + 1)
                        tile = carry(dve, aT, Q, psA[b % 2], aT_done, P, n, b)
                        for j in range(TG):
                            tile(j)
                            if between:
                                between(j)

                    def compare(n, b, f):
                        dve.wait_ge(more_in[b], 32 * f)
                        wait(dve, tiles_done, n - NB + 1)
                        dve.tensor_tensor(G[b][:, :, :], bc(srow[b][:, :], TQ, 2),
                                          tile_dst[:, :, 0:1].to_broadcast([TQ, 2, GE]),
                                          ALU.is_ge).then_inc(ge_done, 1)

                    def stats(n, b, f, j):
                        if j == 0:
                            dve.wait_ge(z_done, n + 1)
                        ins = dve.bn_stats(st6[b][:, j, :], psZ[b % 2][:, j * D:(j + 1) * D])
                        if j == TG - 1:
                            ins.then_inc(small, 1)

                    def moments(n, b, f):
                        dve.wait_ge(small, 3 * n + 1)
                        hold(dve)
                        for j in range(TG):
                            last = dve.bn_aggr(mv[b][:, j, :], st6[b][:, j, :])
                        last.then_inc(small, 1)

                    def variance(n, b, f):
                        dve.wait_ge(small, 3 * n + 2)
                        dve.tensor_tensor(var[b][:, :], mv[b][:, :, 1], de2[:, bass.ds(n * TG, TG)],
                                          ALU.add).then_inc(small, 1)

                    def rstd(n, b, f):
                        dve.wait_ge(std_done, n + 1)
                        dve.reciprocal(r[b][:, :], var[b][:, :]).then_inc(r1_done, 1)
                        dve.wait_ge(r1_done, n + 1)
                        dve.scalar_tensor_tensor(nmr[b][:, :], mv[b][:, :, 0], -1.0, r[b][:, :], ALU.mult,
                                                 ALU.mult).then_inc(r_done, 1)

                    def count(n, b, f):
                        dve.wait_ge(tiles_done, n + 1)
                        for j in range(TG):
                            last = dve.tensor_scalar(le[b][:, j, :], tile_of(psV[b % 2], j, P),
                                                     src_col[:, bass.ds(n * TG + j, 1)], 0.0, ALU.is_le,
                                                     ALU.add, accum_out=n_le[b][:, j:j + 1])
                        last.then_inc(le_done, 1)

                    def find_sums(n, b, f):
                        dve.wait_ge(le_done, n + 1)
                        dve.wait_ge(sg_done, n + 1)
                        dve.scalar_tensor_tensor(hit[b][:, :], n_le[b][:, :], 2.0, n_sg[b][:, :], ALU.mult,
                                                 ALU.add).then_inc(look, 1)
                        for h in range(2):
                            at = h * 512 + P
                            last = dve.scalar_tensor_tensor(
                                slots[b][:, 2 * h:2 * h + 2], n_le[b][:, 2 * h:2 * h + 2],
                                float(-P - 2 - NO_EDGE), psV[b % 2][:, at:at + P + 2:P + 1], ALU.add, ALU.add)
                        last.then_inc(look, 1)

                    def find_hits(n, b, f):
                        dve.wait_ge(look, SEARCH * n + 1)
                        dve.tensor_scalar(hit[b][:, :], hit[b][:, :], P + 0.5, None, ALU.is_ge).then_inc(look, 1)

                    def find_slots(n, b, f):
                        dve.wait_ge(look, SEARCH * n + 3)
                        dve.tensor_tensor(slots[b][:, :], slots[b][:, :], hit[b][:, :], ALU.mult
                                          ).then_inc(look, 1)

                    def find_end(n, b, f):
                        dve.wait_ge(look, SEARCH * n + 4)
                        dve.tensor_scalar(x1_idx[:, bass.ds(n * TG, TG)], slots[b][:, :], float(NO_EDGE), None,
                                          ALU.add).then_inc(look, 1)

                    def body(t):
                        chain(*t, between=lambda j: staged(GROUPS, lambda *m: stats(*m, j), t, -1))
                        staged(GROUPS, find_sums, t, -1)
                        staged(GROUPS, moments, t, -1)
                        staged(GROUPS, find_hits, t, -1)
                        staged(GROUPS, variance, t, -1)
                        staged(GROUPS, match_up, t, 2)
                        staged(GROUPS, find_slots, t, -1)
                        staged(GROUPS, rstd, t, -1)
                        staged(GROUPS, compare, t, 1)
                        staged(GROUPS, find_end, t, -1)
                        count(*t)
                    match_up(*unit(0))
                    match_up(*unit(1))
                    compare(*unit(0))
                    pipeline(dve, GROUPS, body)
                    for j in range(TG):
                        stats(*unit(GROUPS - 1), j)
                    for step in (moments, variance, rstd, find_sums, find_hits, find_slots, find_end):
                        step(*unit(GROUPS - 1))

        with ExitStack() as st:
            def tb(name, shape, dt=f32):
                return [st.enter_context(nc.sbuf_tensor(f"{name}_b{b}", shape, dt)) for b in range(NB)]

            def ps(name, n=1):
                return [st.enter_context(nc.psum_tensor(f"{name}_b{b}", [P, 512], f32)) for b in range(n)]
            idx = tb("idx", [P, TG], i32)
            pidx = tb("pidx", [P, TG], i32)
            xg = tb("xg", [P, TG, D])
            eg = tb("eg", [P, TG, DE])
            x1r = tb("x1r", [P, TG, D])
            drow = tb("drow", [P, GE + 1], i32)
            degr = tb("degr", [1, GE])
            S = tb("S", [P, TG, P])
            Q = tb("Q", [P, TG, P])
            aT = tb("aT", [P, TG, P])
            eT = tb("eT", [DE, TG, P])
            st6 = tb("st6", [P, TG, 6])
            mv = tb("mv", [P, TG, 2])
            var = tb("var", [P, TG])
            r = tb("r", [P, TG])
            nmr = tb("nmr", [P, TG])
            v = tb("v", [P, TG, D])
            n2 = tb("n2", [P, TG, D])
            x2T = tb("x2T", [P, TG, P])
            ye = tb("ye", [P, TG, YW])
            psA, psE = ps("psA", 2), ps("psE", 2)
            psZ, psT, psX, psY = ps("psZ")[0], ps("psT")[0], ps("psX")[0], ps("psY")[0]

            row_in = sems("b_dst_row_loaded")
            more_in = sems("b_edge_attr_x1_degree_loaded")
            gat = sems("b_x1_gathered")
            put = sems("b_rows_scattered")
            idx_copied = sem("b_idx_copied")
            pidx_copied = sem("b_put_idx_copied")
            match = sem("b_match_ready")
            summed = sem("b_tile_sums_ready")
            aT_done = sem("b_sums_with_carry")
            eT_done = sem("b_edge_sums_with_carry")
            z_done = sem("b_product_ready")
            et_done = sem("b_edge_sums_transposed")
            v_done = sem("b_residual_added")
            small = sem("b_small_steps")
            std_done = sem("b_std_ready")
            r1_done = sem("b_rstd_ready")
            r_done = sem("b_rstd_and_shift_ready")
            n_done = sem("b_normed")
            nt_done = sem("b_normed_transposed")
            x2_done = sem("b_x2_ready")
            y_done = sem("b_y_product_ready")
            ye_y = sem("b_row_y_part_ready")
            ye_e = sem("b_row_edge_part_ready")
            primed = sem("b_carry_zeroed")
            WHOLE, PART = divmod(E - (GROUPS - 1) * GE, P)
            assert WHOLE > 0 and PART > 0 and GROUPS > NB

            def is_last(n):
                return isinstance(n, int) and n == GROUPS - 1

            with nc.Block() as block:
                @block.sync
                def _(sp):
                    def loads(n, b, f):
                        load_rows(sp, drow, row_in, match, n, b, f)
                        wait(sp, summed, n - NB + 1)
                        wait(sp, v_done, n - NB + 1)
                        hold(sp)
                        if is_last(n):
                            sp.dma_start(eg[b][:, 0:WHOLE, :], ea[n * GE:n * GE + WHOLE * P, :]
                                         .rearrange("(t p) c -> p t c", p=P)).then_inc(more_in[b], 16)
                            sp.dma_start(eg[b][0:PART, WHOLE, :], ea[E - PART:E, :]).then_inc(more_in[b], 16)
                        else:
                            sp.dma_start(eg[b][:, :, :], ea[bass.ds(n * GE, GE), :]
                                         .rearrange("(t p) c -> p t c", p=P)).then_inc(more_in[b], 16)
                        sp.dma_start(x1r[b][:, :, :], x1_slot[bass.ds(n * GE, GE), :]
                                     .rearrange("(t p) d -> p t d", p=P)).then_inc(more_in[b], 16)
                        wait(sp, z_done, n - NB + 1)
                        hold(sp)
                        sp.dma_start(degr[b][:, :], deg_s[bass.ds(n * GE, GE)].rearrange("(o n) -> o n", o=1)
                                     ).then_inc(more_in[b], 16)
                    for n in range(3):
                        loads(*unit(n))
                    pipeline(sp, GROUPS, lambda t: staged(GROUPS, loads, t, 3))

                @block.gpsimd
                def _(pool):
                    def get(n, b, f):
                        gather(pool, x1_slot[:, :], NO_EDGE, idx, idx_copied, xg, gat, summed, n, b, f)

                    def save(n, b, f):
                        scatter(pool, ye_tab[:, :], pidx, pidx_copied, ye, put, [ye_e, ye_y], n, b, f)

                    def body(t):
                        staged(GROUPS, get, t, 3)
                        staged(GROUPS, save, t, -3)
                    pool.wait_ge(c_kept, 16)
                    for n in range(3):
                        get(*unit(n))
                    pipeline(pool, GROUPS, body)
                    for n in range(GROUPS - 3, GROUPS):
                        save(*unit(n))
                    for b in range(NB):
                        pool.wait_ge(put[b], 64 * fills_of(b))

                @block.tensor
                def _(pe):
                    def sums(n, b, f):
                        pe.wait_ge(match, n + 1)
                        pe.wait_ge(more_in[b], 48 * f + (16 if is_last(n) else 0))
                        pe.wait_ge(gat[b], 64 * f)
                        wait(pe, aT_done, TG * (n - 1))
                        wait(pe, eT_done, TG * (n - 1))
                        for j in range(TG):
                            pe.matmul(psA[b % 2][:, j * P:(j + 1) * P], xg[b][:, j, :], S[b][:, j, :],
                                      start=True, stop=True)
                            last = pe.matmul(psE[b % 2][0:DE, j * P:(j + 1) * P], eg[b][:, j, :], S[b][:, j, :],
                                             start=True, stop=True)
                        last.then_inc(summed, 1)

                    def product(n, b, f):
                        pe.wait_ge(aT_done, TG * (n + 1))
                        pe.wait_ge(more_in[b], 48 * f + (16 if is_last(n) else 0))
                        wait(pe, v_done, n)
                        for j in range(TG):
                            o = psZ[:, j * D:(j + 1) * D]
                            pe.matmul(o, aT[b][:, j, :], w2[:, :], start=True, stop=False)
                            last = pe.matmul(o, degr[b][:, j * P:(j + 1) * P], b2_row[:, :], start=False,
                                             stop=True)
                        last.then_inc(z_done, 1)
                        pe.wait_ge(eT_done, TG * (n + 1))
                        wait(pe, ye_e, n)
                        for j in range(TG):
                            last = pe.transpose(psT[:, j * DE:(j + 1) * DE], eT[b][:, j, :], ident[0:DE, 0:DE])
                        last.then_inc(et_done, 1)

                    def turn(n, b, f):
                        pe.wait_ge(n_done, n + 1)
                        wait(pe, x2_done, n)
                        for j in range(TG):
                            last = pe.transpose(psX[:, j * P:(j + 1) * P], n2[b][:, j, :], ident[:, :])
                        last.then_inc(nt_done, 1)

                    def outp(n, b, f):
                        pe.wait_ge(x2_done, n + 1)
                        wait(pe, ye_y, n)
                        for j in range(TG):
                            last = pe.matmul(psY[:, j * D:(j + 1) * D], x2T[b][:, j, :], wo[:, :],
                                             start=True, stop=True)
                        last.then_inc(y_done, 1)

                    def body(t):
                        staged(GROUPS, turn, t, -2)
                        staged(GROUPS, sums, t, 1)
                        staged(GROUPS, outp, t, -2)
                        product(*t)
                    sums(*unit(0))
                    pipeline(pe, GROUPS, body)
                    for n in range(GROUPS - 2, GROUPS):
                        turn(*unit(n))
                        outp(*unit(n))

                @block.scalar
                def _(act):
                    def norm(n, b, f):
                        act.wait_ge(r_done, n + 1)
                        wait(act, nt_done, n - NB + 1)
                        for j in range(TG):
                            last = act.activation(n2[b][:, j, :], v[b][:, j, :], ACT.Identity,
                                                  bias=nmr[b][:, j:j + 1], scale=r[b][:, j:j + 1])
                        last.then_inc(n_done, 1)

                    def relu(n, b, f):
                        act.wait_ge(nt_done, n + 1)
                        act.activation(x2T[b][:, :, :].rearrange("p t n -> p (t n)"), psX[:, :], ACT.Relu,
                                       bias=be2_col[:, :], scale=g2_col[:, :]).then_inc(x2_done, 1)

                    def edge_mean(n, b, f):
                        wait(act, put[b], 64 * (f - 1))
                        act.wait_ge(et_done, n + 1)
                        for j in range(TG):
                            last = act.activation(ye[b][:, j, D:YW], psT[:, j * DE:(j + 1) * DE], ACT.Copy,
                                                  scale=rdeg[:, bass.ds(n * TG + j, 1)])
                        last.then_inc(ye_e, 1)

                    def root(n, b, f):
                        act.wait_ge(small, 3 * (n + 1))
                        act.activation(var[b][:, :], var[b][:, :], ACT.Sqrt).then_inc(std_done, 1)

                    def body(t):
                        staged(GROUPS, relu, t, -2)
                        staged(GROUPS, edge_mean, t, -1)
                        staged(GROUPS, root, t, -1)
                        staged(GROUPS, norm, t, -1)
                        staged(GROUPS, get_indices, t, NB)
                        staged(GROUPS, put_indices, t, -1)

                    def get_indices(n, b, f):
                        copy_idx(act, x1_idx, idx, gat, idx_copied, n, b, f)

                    def put_indices(n, b, f):
                        copy_idx(act, put_idx, pidx, put, pidx_copied, n, b, f)
                    for n in range(NB):
                        get_indices(*unit(n))
                    pipeline(act, GROUPS, body)
                    put_indices(*unit(GROUPS - 1))
                    edge_mean(*unit(GROUPS - 1))
                    root(*unit(GROUPS - 1))
                    norm(*unit(GROUPS - 1))
                    for n in range(GROUPS - 2, GROUPS):
                        relu(*unit(n))

                @block.vector
                def _(dve):
                    dve.memset(aT[NB - 1][:, TG - 1, :], 0.0)
                    dve.memset(eT[NB - 1][:, TG - 1, :], 0.0).then_inc(primed, 1)
                    dve.wait_ge(primed, 1)

                    def match_up(n, b, f):
                        matches(dve, drow, row_in, S, Q, summed, [aT_done, eT_done], match, n, b, f)

                    def chain(n, b, f):
                        dve.wait_ge(match, n + 1)
                        dve.wait_ge(summed, n + 1)
                        wait(dve, z_done, n - NB + 1)
                        wait(dve, et_done, n - NB + 1)
                        a = carry(dve, aT, Q, psA[b % 2], aT_done, P, n, b)
                        e = carry(dve, eT, Q, psE[b % 2], eT_done, DE, n, b)
                        for j in range(TG):
                            a(j)
                            e(j)

                    def moments(n, b, f):
                        dve.wait_ge(more_in[b], 48 * f + (16 if is_last(n) else 0))
                        dve.wait_ge(z_done, n + 1)
                        wait(dve, n_done, n - NB + 1)
                        for j in range(TG):
                            last = dve.scalar_tensor_tensor(
                                v[b][:, j, :], psZ[:, j * D:(j + 1) * D], rdeg[:, bass.ds(n * TG + j, 1)],
                                x1r[b][:, j, :], ALU.mult, ALU.add)
                        last.then_inc(v_done, 1)
                        dve.wait_ge(v_done, n + 1)
                        for j in range(TG):
                            last = dve.bn_stats(st6[b][:, j, :], v[b][:, j, :])
                        last.then_inc(small, 1)
                        dve.wait_ge(small, 3 * n + 1)
                        hold(dve)
                        for j in range(TG):
                            last = dve.bn_aggr(mv[b][:, j, :], st6[b][:, j, :])
                        last.then_inc(small, 1)
                        dve.wait_ge(small, 3 * n + 2)
                        dve.tensor_scalar(var[b][:, :], mv[b][:, :, 1], EPS, None, ALU.add).then_inc(small, 1)

                    def rows_y(n, b, f):
                        dve.wait_ge(y_done, n + 1)
                        wait(dve, put[b], 64 * (f - 1))
                        dve.tensor_tensor(ye[b][:, :, 0:D], psY[:, :].rearrange("p (t d) -> p t d", d=D),
                                          bc(bo_bc[:, :], P, TG), ALU.add).then_inc(ye_y, 1)

                    def rstd(n, b, f):
                        dve.wait_ge(std_done, n + 1)
                        dve.reciprocal(r[b][:, :], var[b][:, :]).then_inc(r1_done, 1)
                        dve.wait_ge(r1_done, n + 1)
                        dve.scalar_tensor_tensor(nmr[b][:, :], mv[b][:, :, 0], -1.0, r[b][:, :], ALU.mult,
                                                 ALU.mult).then_inc(r_done, 1)

                    def body(t):
                        chain(*t)
                        staged(GROUPS, moments, t, -1)
                        staged(GROUPS, rows_y, t, -2)
                        staged(GROUPS, rstd, t, -1)
                        staged(GROUPS, match_up, t, 2)
                    match_up(*unit(0))
                    match_up(*unit(1))
                    pipeline(dve, GROUPS, body)
                    moments(*unit(GROUPS - 1))
                    rstd(*unit(GROUPS - 1))
                    rows_y(*unit(GROUPS - 2))
                    rows_y(*unit(GROUPS - 1))
        fills.close()

        FW = YW + 1

        def size(n):
            return (REST, 1) if isinstance(n, int) and n == BLOCKS else (P, BR)

        def rows_of(t, n, c):
            pr, rr = size(n)
            return t[bass.ds(n * BLK, pr * rr), 0:c].rearrange("(p r) c -> p r c", r=rr)

        gx = sb("gx", [P, FW])
        ge = sb("ge", [DE, DE + 1])
        vx_hi, vx_lo = sb("vx_hi", [P, H], f32r), sb("vx_lo", [P, H], f32r)
        ve_hi, ve_lo = sb("ve_hi", [DE, H], f32r), sb("ve_lo", [DE, H], f32r)
        bn_scale = sb("bn_scale", [P, 2])
        bn_shift = sb("bn_shift", [P, 2])
        h0_r = sb("h0_r", [P, UNITS * BR])
        h0_s = sb("h0_s", [P, UNITS * BR])
        CB = 6
        with ExitStack() as st:
            def tb(name, shape, dt=f32):
                return [st.enter_context(nc.sbuf_tensor(f"{name}_c{b}", shape, dt)) for b in range(CB)]

            def t1(name, shape):
                return st.enter_context(nc.sbuf_tensor(name, shape, f32))
            xb = tb("xb", [P, BR, D])
            F = tb("F", [P, BR, FW])
            st6 = tb("st6", [P, BR, 6])
            mv = tb("mv", [P, BR, 2])
            var = tb("var", [P, BR])
            psG = st.enter_context(nc.psum_tensor("psG", [P, 512], f32))
            psH = st.enter_context(nc.psum_tensor("psH", [P, 512], f32))
            blk_in = sems("c_block_loaded", CB)
            ones_set = sem("c_ones_set")
            s_done = sem("c_sum_ready")
            small = sem("c_small_steps")
            std_done = sem("c_std_ready")
            r1_done = sem("c_rstd_ready")
            r_done = sem("c_rstd_and_shift_ready")
            n_done = sem("c_h0_ready")
            m_done = sem("c_moments_added")
            with nc.Block() as block:
                @block.sync
                def _(sp):
                    def load(n, b, f):
                        pr, rr = size(n)
                        wait(sp, m_done, n - CB + 1)
                        hold(sp)
                        sp.dma_start(xb[b][0:pr, 0:rr, :], rows_of(x, n, D)).then_inc(blk_in[b], 16)
                        sp.dma_start(F[b][0:pr, 0:rr, 0:YW], rows_of(ye_tab, n, YW)).then_inc(blk_in[b], 16)
                    pipeline(sp, UNITS, lambda t: load(*t), CB)

                @block.vector
                def _(dve):
                    for b in range(CB):
                        last = dve.memset(F[b][:, :, YW:FW], 1.0)
                    last.then_inc(ones_set, 1)

                    def add(n, b, f):
                        pr, rr = size(n)
                        dve.wait_ge(blk_in[b], 32 * f)
                        y = F[b][0:pr, 0:rr, 0:D]
                        dve.scalar_tensor_tensor(y, xb[b][0:pr, 0:rr, :], 2.0, y, ALU.mult,
                                                 ALU.add).then_inc(s_done, 1)

                    def stats(n, b, f):
                        pr, rr = size(n)
                        dve.wait_ge(s_done, n + 1)
                        hold(dve)
                        for j in range(rr):
                            last = dve.bn_stats(st6[b][0:pr, j, :], F[b][0:pr, j, 0:D])
                        last.then_inc(small, 1)

                    def moments(n, b, f):
                        pr, rr = size(n)
                        dve.wait_ge(small, 3 * n + 1)
                        hold(dve)
                        for j in range(rr):
                            last = dve.bn_aggr(mv[b][0:pr, j, :], st6[b][0:pr, j, :])
                        last.then_inc(small, 1)

                    def variance(n, b, f):
                        pr, rr = size(n)
                        dve.wait_ge(small, 3 * n + 2)
                        dve.tensor_scalar(var[b][0:pr, 0:rr], mv[b][0:pr, 0:rr, 1], EPS, None,
                                          ALU.add).then_inc(small, 1)

                    def invert(n, b, f):
                        pr, rr = size(n)
                        dve.wait_ge(std_done, n + 1)
                        dve.reciprocal(h0_r[0:pr, bass.ds(n * BR, rr)], var[b][0:pr, 0:rr]).then_inc(r1_done, 1)

                    def offset(n, b, f):
                        pr, rr = size(n)
                        dve.wait_ge(r1_done, n + 1)
                        dve.scalar_tensor_tensor(h0_s[0:pr, bass.ds(n * BR, rr)], mv[b][0:pr, 0:rr, 0], -1.0,
                                                 h0_r[0:pr, bass.ds(n * BR, rr)], ALU.mult, ALU.mult
                                                 ).then_inc(r_done, 1)

                    def body(t):
                        stats(*t)
                        staged(UNITS, invert, t, -1, CB)
                        staged(UNITS, add, t, 1, CB)
                        staged(UNITS, offset, t, -1, CB)
                        moments(*t)
                        variance(*t)
                    add(*unit(0, CB))
                    pipeline(dve, UNITS, body, CB)
                    invert(*unit(UNITS - 1, CB))
                    offset(*unit(UNITS - 1, CB))

                @block.scalar
                def _(act):
                    def root(n, b, f):
                        pr, rr = size(n)
                        act.wait_ge(small, 3 * n + 3)
                        act.activation(var[b][0:pr, 0:rr], var[b][0:pr, 0:rr], ACT.Sqrt).then_inc(std_done, 1)

                    def norm(n, b, f):
                        pr, rr = size(n)
                        act.wait_ge(r_done, n + 1)
                        for j in range(rr):
                            h0 = F[b][0:pr, j, 0:D]
                            last = act.activation(h0, h0, ACT.Identity, bias=h0_s[0:pr, bass.ds(n * BR + j, 1)],
                                                  scale=h0_r[0:pr, bass.ds(n * BR + j, 1)])
                        last.then_inc(n_done, 1)

                    def body(t):
                        root(*t)
                        staged(UNITS, norm, t, -1, CB)
                    pipeline(act, UNITS, body, CB)
                    norm(*unit(UNITS - 1, CB))

                @block.tensor
                def _(pe):
                    pe.wait_ge(ones_set, 1)

                    def gram(n, b, f):
                        pr, rr = size(n)
                        pe.wait_ge(n_done, n + 1)
                        for j in range(rr):
                            first = isinstance(n, int) and n == 0 and j == 0
                            end = isinstance(n, int) and n == BLOCKS
                            pe.matmul(psG[:, 0:FW], F[b][0:pr, j, 0:D], F[b][0:pr, j, :], start=first, stop=end)
                            last = pe.matmul(psH[0:DE, 0:DE + 1], F[b][0:pr, j, D:YW], F[b][0:pr, j, D:FW],
                                             start=first, stop=end)
                        last.then_inc(m_done, 1)
                    pipeline(pe, UNITS, lambda t: gram(*t), CB)

                @block.gpsimd
                def _(pool):
                    pool.wait_ge(m_done, UNITS)

            gex = t1("gex", [DE, P])
            vgx = t1("vgx", [P, H])
            vge = t1("vge", [DE, H])
            cc = t1("cc", [P, 2])
            mq = t1("mq", [P, 6])
            mu = t1("mu", [P, 2])
            bvar = t1("bvar", [P, 2])
            psT = st.enter_context(nc.psum_tensor("psT_bn", [P, 512], f32))
            psX = st.enter_context(nc.psum_tensor("psX_bn", [P, 512], f32))
            psE = st.enter_context(nc.psum_tensor("psE_bn", [P, 512], f32))
            psM = st.enter_context(nc.psum_tensor("psM_bn", [P, 512], f32))
            vs = sem("n_vector_steps")
            t_done = sem("n_cross_moments_transposed")
            vg_done = sem("n_moment_products")
            pr_done = sem("n_weighted")
            q_done = sem("n_sums_ready")
            std_done = sem("n_std_ready")
            with nc.Block() as block:
                @block.tensor
                def _(pe):
                    pe.wait_ge(vs, 2)
                    pe.transpose(psT[0:DE, 0:P], gx[:, D:YW], ident[:, :]).then_inc(t_done, 1)
                    pe.wait_ge(vs, 7)
                    pe.matmul(psX[:, 0:H], gx[:, 0:D], vx[:, :], start=True, stop=False)
                    pe.matmul(psX[:, 0:H], gex[:, :], ve[:, :], start=False, stop=True)
                    pe.matmul(psE[0:DE, 0:H], gx[:, D:YW], vx[:, :], start=True, stop=False)
                    pe.matmul(psE[0:DE, 0:H], ge[:, 0:DE], ve[:, :], start=False, stop=True).then_inc(vg_done, 1)
                    pe.wait_ge(pr_done, 1)
                    for k in range(2):
                        hk = slice(k * P, (k + 1) * P)
                        pe.matmul(psM[:, k:k + 1], vgx[:, hk], ones[:, :], start=True, stop=False)
                        pe.matmul(psM[:, k:k + 1], vge[:, hk], ones[0:DE, :], start=False, stop=True)
                        pe.matmul(psM[:, 2 + k:3 + k], vx[:, hk], gx[:, YW:FW], start=True, stop=False)
                        pe.matmul(psM[:, 2 + k:3 + k], ve[:, hk], ge[:, DE:DE + 1], start=False, stop=True)
                        last = pe.matmul(psM[:, 4 + k:5 + k], vu[:, hk], u_col[:, :], start=True, stop=True)
                    last.then_inc(q_done, 1)

                @block.scalar
                def _(act):
                    act.wait_ge(vs, 11)
                    act.activation(bvar[:, :], bvar[:, :], ACT.Sqrt).then_inc(std_done, 1)

                @block.vector
                def _(dve):
                    count = [0]

                    def step(ins):
                        count[0] += 1
                        ins.then_inc(vs, 1)
                        dve.wait_ge(vs, count[0])
                    step(dve.tensor_scalar(gx[:, :], psG[:, 0:FW], 1.0 / N, None, ALU.mult))
                    step(dve.tensor_scalar(ge[:, :], psH[0:DE, 0:DE + 1], 1.0 / N, None, ALU.mult))
                    for w, hi, lo in ((vx, vx_hi, vx_lo), (ve, ve_hi, ve_lo)):
                        step(dve.tensor_copy(hi[:, :], w[:, :]))
                        step(dve.tensor_tensor(lo[:, :], w[:, :], hi[:, :].bitcast(f32), ALU.subtract))
                    dve.wait_ge(t_done, 1)
                    step(dve.tensor_copy(gex[:, :], psT[0:DE, 0:P]))
                    dve.wait_ge(vg_done, 1)
                    dve.tensor_tensor(vgx[:, :], psX[:, 0:H], vx[:, :], ALU.mult)
                    dve.tensor_tensor(vge[:, :], psE[0:DE, 0:H], ve[:, :], ALU.mult).then_inc(pr_done, 1)
                    dve.wait_ge(q_done, 1)
                    step(dve.tensor_copy(mq[:, :], psM[:, 0:6]))
                    step(dve.tensor_tensor(bvar[:, :], mq[:, 2:4], mq[:, 2:4], ALU.mult))
                    step(dve.tensor_tensor(bvar[:, :], mq[:, 0:2], bvar[:, :], ALU.subtract))
                    step(dve.tensor_scalar(bvar[:, :], bvar[:, :], EPS, None, ALU.add))
                    step(dve.tensor_tensor(cc[:, :], mq[:, 4:6], c1_col[:, :], ALU.add))
                    step(dve.tensor_tensor(mu[:, :], mq[:, 2:4], cc[:, :], ALU.add))
                    step(dve.tensor_tensor(cc[:, :], cc[:, :], mu[:, :], ALU.subtract))
                    dve.wait_ge(std_done, 1)
                    step(dve.reciprocal(bvar[:, :], bvar[:, :]))
                    step(dve.tensor_tensor(bn_scale[:, :], bvar[:, :], gamma_col[:, :], ALU.mult))
                    step(dve.tensor_tensor(bn_shift[:, :], bn_scale[:, :], cc[:, :], ALU.mult))
                    step(dve.tensor_tensor(bn_shift[:, :], bn_shift[:, :], beta_col[:, :], ALU.add))

        with ExitStack() as st:
            def tb(name, shape, n=NB, dt=f32):
                return [st.enter_context(nc.sbuf_tensor(f"{name}_d{b}", shape, dt)) for b in range(n)]
            xb = tb("xb", [P, BR, D])
            F = tb("F", [P, BR, YW])
            hb = tb("hb", [P, BR, D])
            hT_hi, hT_lo = tb("hT_hi", [P, BLK], 2, f32r), tb("hT_lo", [P, BLK], 2, f32r)
            eT_hi, eT_lo = tb("eT_hi", [DE, BLK], 2, f32r), tb("eT_lo", [DE, BLK], 2, f32r)
            aH = tb("aH", [P, 2, BLK], 2)
            v = tb("v", [P, BR, D])
            o = tb("o", [P, BR, D])
            st6 = tb("st6", [P, BR, 6])
            mv = tb("mv", [P, BR, 2])
            var = tb("var", [P, BR])
            r = tb("r", [P, BR])
            nmr = tb("nmr", [P, BR])
            psT = st.enter_context(nc.psum_tensor("psT_d", [P, 1024], f32))
            psE = st.enter_context(nc.psum_tensor("psE_d", [P, 1024], f32))
            psH = [st.enter_context(nc.psum_tensor(f"psH_d{k}", [P, 512], f32)) for k in range(2)]
            psO = st.enter_context(nc.psum_tensor("psO_d", [P, 1024], f32))
            blk_in = sems("d_block_loaded")
            s_done = sem("d_sum_ready")
            h0_done = sem("d_h0_ready")
            hb_done = sem("d_h0_plus_b2")
            tr_done = sem("d_transposed")
            hi_h = sem("d_h0T_upper_ready")
            hi_e = sem("d_eT_upper_ready")
            lo_h = sem("d_h0T_lower_ready")
            lo_e = sem("d_eT_lower_ready")
            h_done = sem("d_hidden_product")
            a_done = sem("d_hidden_relu")
            o_done = sem("d_output_product")
            v_done = sem("d_residual_added")
            small = sem("d_small_steps")
            std_done = sem("d_std_ready")
            r1_done = sem("d_rstd_ready")
            r_done = sem("d_rstd_and_shift_ready")
            n_done = sem("d_out_ready")
            stored = sems("d_out_stored")

            def products(n):
                pr, rr = size(n)
                parts = 2 if rr > 1 else 1
                w = pr * rr // parts
                return [(q, q % 2, slice(q // 2 * w, (q // 2 + 1) * w), w) for q in range(2 * parts)]

            with nc.Block() as block:
                @block.sync
                def _(sp):
                    def load(n, b, f):
                        pr, rr = size(n)
                        wait(sp, s_done, n - NB + 1)
                        wait(sp, tr_done, n - NB + 1)
                        wait(sp, hb_done, n - NB + 1)
                        hold(sp)
                        sp.dma_start(xb[b][0:pr, 0:rr, :], rows_of(x, n, D)).then_inc(blk_in[b], 16)
                        sp.dma_start(F[b][0:pr, 0:rr, :], rows_of(ye_tab, n, YW)).then_inc(blk_in[b], 16)
                    pipeline(sp, UNITS, lambda t: load(*t))

                @block.gpsimd
                def _(pool):
                    def plus_b2(n, b, f):
                        pr, rr = size(n)
                        pool.wait_ge(h0_done, n + 1)
                        wait(pool, v_done, n - NB + 1)
                        pool.tensor_tensor(hb[b][0:pr, 0:rr, :], F[b][0:pr, 0:rr, 0:D], bc(c2_bc[0:pr, :], pr, rr),
                                           ALU.add).then_inc(hb_done, 1)
                    pipeline(pool, UNITS, lambda t: plus_b2(*t))

                @block.tensor
                def _(pe):
                    def turn(n, b, f):
                        pr, rr = size(n)
                        pe.wait_ge(h0_done, n + 1)
                        wait(pe, lo_h, n)
                        wait(pe, lo_e, n)
                        for j in range(rr):
                            pe.transpose(psT[:, j * P:j * P + pr], F[b][0:pr, j, 0:D], ident[0:pr, 0:pr])
                            last = pe.transpose(psE[0:DE, j * P:j * P + pr], F[b][0:pr, j, D:YW],
                                                ident[0:pr, 0:pr])
                        last.then_inc(tr_done, 1)

                    def hidden(n, b, f, some):
                        pe.wait_ge(lo_h, n + 1)
                        pe.wait_ge(lo_e, n + 1)
                        for q, k, cols, w in products(n)[some]:
                            wait(pe, a_done, 4 * n + q - 1)
                            half = slice(k * P, (k + 1) * P)
                            pe.matmul(psH[k][:, 0:w], vx_hi[:, half], hT_hi[b % 2][:, cols], start=True, stop=False)
                            pe.matmul(psH[k][:, 0:w], vx_hi[:, half], hT_lo[b % 2][:, cols], start=False, stop=False)
                            pe.matmul(psH[k][:, 0:w], vx_lo[:, half], hT_hi[b % 2][:, cols], start=False, stop=False)
                            pe.matmul(psH[k][:, 0:w], ve_hi[:, half], eT_hi[b % 2][:, cols], start=False, stop=False)
                            pe.matmul(psH[k][:, 0:w], ve_hi[:, half], eT_lo[b % 2][:, cols], start=False, stop=False)
                            pe.matmul(psH[k][:, 0:w], ve_lo[:, half], eT_hi[b % 2][:, cols], start=False,
                                      stop=True).then_inc(h_done, 1)

                    def outp(n, b, f):
                        pr, rr = size(n)
                        wait(pe, v_done, n)
                        for j in range(rr):
                            if (j + 1) * pr > products(n)[0][3]:
                                pe.wait_ge(a_done, 4 * n + len(products(n)))
                            elif j == 0:
                                pe.wait_ge(a_done, 4 * n + 2)
                            for k in range(2):
                                last = pe.matmul(psO[0:pr, j * D:(j + 1) * D], aH[b % 2][:, k, j * P:j * P + pr],
                                                 v2[:, k, :], start=(k == 0), stop=(k == 1))
                        last.then_inc(o_done, 1)

                    def body(t):
                        hidden(*t, slice(0, 2))
                        staged(UNITS, turn, t, 1)
                        hidden(*t, slice(2, 4))
                        outp(*t)
                    turn(*unit(0))
                    pipeline(pe, UNITS, body)

                @block.scalar
                def _(act):
                    def relu(n, b, f, some):
                        wait(act, o_done, n - 1)
                        for q, k, cols, w in products(n)[some]:
                            act.wait_ge(h_done, 4 * n + q + 1)
                            act.activation(aH[b % 2][:, k, cols], psH[k][:, 0:w], ACT.Relu,
                                           bias=bn_shift[:, k:k + 1], scale=bn_scale[:, k:k + 1]
                                           ).then_inc(a_done, 1)

                    def root(n, b, f):
                        pr, rr = size(n)
                        act.wait_ge(small, 3 * n + 3)
                        act.activation(var[b][0:pr, 0:rr], var[b][0:pr, 0:rr], ACT.Sqrt).then_inc(std_done, 1)

                    def upper(n, b, f):
                        pr, rr = size(n)
                        act.wait_ge(tr_done, n + 1)
                        wait(act, h_done, 4 * (n - 1))
                        act.activation(hT_hi[b % 2][:, 0:pr * rr], psT[:, 0:pr * rr], ACT.Copy).then_inc(hi_h, 1)
                        act.activation(eT_hi[b % 2][:, 0:pr * rr], psE[0:DE, 0:pr * rr], ACT.Copy
                                       ).then_inc(hi_e, 1)

                    def norm(n, b, f):
                        pr, rr = size(n)
                        wait(act, stored[b], 16 * (f - 1))
                        act.wait_ge(r_done, n + 1)
                        for j in range(rr):
                            last = act.activation(o[b][0:pr, j, :], v[b][0:pr, j, :], ACT.Identity,
                                                  bias=nmr[b][0:pr, j:j + 1], scale=r[b][0:pr, j:j + 1])
                        last.then_inc(n_done, 1)
                        act.wait_ge(n_done, n + 1)
                        act.dma_start(rows_of(out, n, D), o[b][0:pr, 0:rr, :]).then_inc(stored[b], 16)

                    def body(t):
                        relu(*t, slice(0, 2))
                        staged(UNITS, upper, t, 1)
                        relu(*t, slice(2, 4))
                        staged(UNITS, root, t, -1)
                        staged(UNITS, norm, t, -1)
                    upper(*unit(0))
                    pipeline(act, UNITS, body)
                    root(*unit(UNITS - 1))
                    norm(*unit(UNITS - 1))
                    for b in range(NB):
                        act.wait_ge(stored[b], 16 * ((UNITS - 1 - b) // NB + 1))

                @block.vector
                def _(dve):
                    def prepare(n, b, f):
                        pr, rr = size(n)
                        dve.wait_ge(blk_in[b], 32 * f)
                        y = F[b][0:pr, 0:rr, 0:D]
                        dve.scalar_tensor_tensor(y, xb[b][0:pr, 0:rr, :], 2.0, y, ALU.mult,
                                                 ALU.add).then_inc(s_done, 1)
                        dve.wait_ge(s_done, n + 1)
                        for j in range(rr):
                            h0 = F[b][0:pr, j, 0:D]
                            last = dve.tensor_scalar(h0, h0, h0_r[0:pr, bass.ds(n * BR + j, 1)],
                                                     h0_s[0:pr, bass.ds(n * BR + j, 1)], ALU.mult, ALU.add)
                        last.then_inc(h0_done, 1)

                    def lower(n, b, f):
                        pr, rr = size(n)
                        wait(dve, h_done, 4 * (n - 1))
                        c = slice(0, pr * rr)
                        dve.wait_ge(hi_h, n + 1)
                        dve.tensor_tensor(hT_lo[b % 2][:, c], psT[:, c], hT_hi[b % 2][:, c].bitcast(f32),
                                          ALU.subtract).then_inc(lo_h, 1)
                        dve.wait_ge(hi_e, n + 1)
                        dve.tensor_tensor(eT_lo[b % 2][:, c], psE[0:DE, c], eT_hi[b % 2][:, c].bitcast(f32),
                                          ALU.subtract).then_inc(lo_e, 1)

                    def moments(n, b, f):
                        pr, rr = size(n)
                        dve.wait_ge(o_done, n + 1)
                        dve.wait_ge(hb_done, n + 1)
                        wait(dve, n_done, n - NB + 1)
                        dve.tensor_tensor(v[b][0:pr, 0:rr, :],
                                          psO[0:pr, 0:rr * D].rearrange("p (r d) -> p r d", d=D),
                                          hb[b][0:pr, 0:rr, :], ALU.add).then_inc(v_done, 1)
                        dve.wait_ge(v_done, n + 1)
                        for j in range(rr):
                            last = dve.bn_stats(st6[b][0:pr, j, :], v[b][0:pr, j, :])
                        last.then_inc(small, 1)
                        dve.wait_ge(small, 3 * n + 1)
                        hold(dve)
                        for j in range(rr):
                            last = dve.bn_aggr(mv[b][0:pr, j, :], st6[b][0:pr, j, :])
                        last.then_inc(small, 1)
                        dve.wait_ge(small, 3 * n + 2)
                        dve.tensor_scalar(var[b][0:pr, 0:rr], mv[b][0:pr, 0:rr, 1], EPS, None,
                                          ALU.add).then_inc(small, 1)

                    def rstd(n, b, f):
                        pr, rr = size(n)
                        dve.wait_ge(std_done, n + 1)
                        dve.reciprocal(r[b][0:pr, 0:rr], var[b][0:pr, 0:rr]).then_inc(r1_done, 1)
                        dve.wait_ge(r1_done, n + 1)
                        dve.scalar_tensor_tensor(nmr[b][0:pr, 0:rr], mv[b][0:pr, 0:rr, 0], -1.0,
                                                 r[b][0:pr, 0:rr], ALU.mult, ALU.mult).then_inc(r_done, 1)

                    def body(t):
                        staged(UNITS, moments, t, -1)
                        staged(UNITS, lower, t, 1)
                        staged(UNITS, rstd, t, -1)
                        staged(UNITS, prepare, t, 2)
                    prepare(*unit(0))
                    prepare(*unit(1))
                    lower(*unit(0))
                    pipeline(dve, UNITS, body)
                    moments(*unit(UNITS - 1))
                    rstd(*unit(UNITS - 1))


_NAMES = ['x', 'src', 'dst', 'edge_attr_96', 'L0_gnn_W1', 'L0_gnn_b1', 'L0_gnn_g1', 'L0_gnn_be1', 'L0_gnn_W2',
          'L0_gnn_b2', 'L0_gnn_g2', 'L0_gnn_be2', 'L0_gnn_Wo', 'L0_gnn_bo', 'L1_gnn_u', 'L1_gnn_W1', 'L1_gnn_b1',
          'L1_gnn_gamma', 'L1_gnn_beta', 'L1_gnn_W2', 'L1_gnn_b2']


def kernel(**inputs):
    import numpy as _np
    import concourse.bacc as _bacc
    from concourse import mybir as _mybir
    from concourse.bass_utils import run_bass_kernel_spmd as _run

    nc = _bacc.Bacc("TRN2", target_bir_lowering=False, num_devices=1)
    arrays, args = {}, []
    for name in _NAMES:
        a = _np.ascontiguousarray(inputs[name])
        arrays[f"in_{name}"] = a
        args.append(nc.dram_tensor(f"in_{name}", a.shape, _mybir.dt.from_np(a.dtype), kind="ExternalInput").ap())
    shape = arrays["in_x"].shape
    args.append(nc.dram_tensor("out_0", shape, _mybir.dt.float32, kind="ExternalOutput").ap())
    build_gnn(nc, *args)
    r = _run(nc, [arrays], core_ids=[0])
    return r.results[0]["out_0"]
```
